# Optimizing a Trainium2 kernel written in Bass

```python
import numpy as np
import jax
import jax.numpy as jnp

def _softmax(x, axis=-1):
    return jax.nn.softmax(x, axis=axis)
def _gelu(x):
    return jax.nn.gelu(x, approximate=True)
def _silu(x):
    return jax.nn.silu(x)
def _sigmoid(x):
    return jax.nn.sigmoid(x)
def _layernorm(x, axis=-1, eps=1e-5):
    m = jnp.mean(x, axis=axis, keepdims=True)
    v = jnp.var(x, axis=axis, keepdims=True)
    return (x - m) / jnp.sqrt(v + eps)
def _scatter_add(tgt, idx, src, axis=0):
    return tgt.at[idx].add(src)
def _segment_sum(src, seg, n):
    return jax.ops.segment_sum(src, seg, n)

kernel_name = 'mk_metaformer_d2_conv_nchw128_b2b33d'

def setup_inputs(seed: int = 0):
    np.random.seed(seed)
    _w = jnp.asarray
    def _rec_inputs():
        import jax
        import jax.numpy as jnp
        _gk = jax.random.key(seed)
        x = 7.22e-05 + 1 * jax.random.normal(jax.random.fold_in(_gk, 1), (4, 128, 128, 128), jnp.float32)
        return x
    x = _rec_inputs()
    def _L0_conv_setup():
        import jax, jax.numpy as jnp
        import numpy as np
        B, CIN, H, W = (4, 128, 128, 128)
        COUT, GROUPS, SPAN = (128, 8, 128)
        GC = COUT // GROUPS
        QC = GC // 2
        EPS = 1e-05

        def _bn(x, gamma, beta, ch_axis=1):
            axes = tuple((i for i in range(x.ndim) if i != ch_axis))
            m = x.mean(axes, keepdims=True)
            v = x.var(axes, keepdims=True)
            shape = [1] * x.ndim
            shape[ch_axis] = -1
            return (x - m) / jnp.sqrt(v + EPS) * gamma.reshape(shape) + beta.reshape(shape)
        key = jax.random.key(seed)
        ks = jax.random.split(key, 3)
        inp = {'input': jax.random.normal(ks[0], (B, CIN, H, W), dtype=jnp.float32), 'conv_w': jax.random.normal(ks[1], (2 * COUT, CIN), dtype=jnp.float32) / np.sqrt(CIN), 'bn_qkv_gamma': jnp.ones((2 * COUT,), jnp.float32), 'bn_qkv_beta': jnp.zeros((2 * COUT,), jnp.float32), 'bn_sim_gamma': jnp.ones((3 * GROUPS,), jnp.float32), 'bn_sim_beta': jnp.zeros((3 * GROUPS,), jnp.float32), 'bn_out_gamma': jnp.ones((2 * COUT,), jnp.float32), 'bn_out_beta': jnp.zeros((2 * COUT,), jnp.float32), 'rel_emb': jax.random.normal(ks[2], (2 * GC, 2 * SPAN - 1), dtype=jnp.float32)}
        return inp
    _L0_conv_all = _L0_conv_setup()
    _L0_conv_in = {k: v for k, v in _L0_conv_all.items() if k in ('conv_w', 'bn_qkv_gamma', 'bn_qkv_beta', 'bn_sim_gamma', 'bn_sim_beta', 'bn_out_gamma', 'bn_out_beta', 'rel_emb', )}
    del _L0_conv_all

    def _L0_ffn_setup():
        import jax, jax.numpy as jnp
        import numpy as np
        BN_EPS = 1e-05
        key = jax.random.key(seed)
        k1, k2, k3 = jax.random.split(key, 3)
        B, T, I, H = (64, 2048, 128, 128)
        x = jax.random.normal(k1, (B, T, I), dtype=jnp.float32)
        W = jax.random.normal(k2, (H, I), dtype=jnp.float32) * (1.0 / np.sqrt(I))
        V = jnp.linalg.qr(jax.random.normal(k3, (H, H), dtype=jnp.float32))[0]
        gamma = jnp.ones((H,), dtype=jnp.float32)
        beta = jnp.zeros((H,), dtype=jnp.float32)
        return {'x': x, 'W': W, 'V': V, 'gamma': gamma, 'beta': beta}
    _L0_ffn_all = _L0_ffn_setup()
    _L0_ffn_in = {k: v for k, v in _L0_ffn_all.items() if k in ('W', 'V', 'gamma', 'beta', )}
    del _L0_ffn_all

    def _L1_conv_setup():
        import jax, jax.numpy as jnp
        import numpy as np
        from jax import lax
        K = 3
        STRIDE = 1
        PAD = 1

        def _conv2d(x, w, b, stride, pad):
            y = lax.conv_general_dilated(x, w, window_strides=(stride, stride), padding=((pad, pad), (pad, pad)), dimension_numbers=('NCHW', 'OIHW', 'NCHW'))
            return y + b[None, :, None, None]

        def _deform_conv2d(x, offsets, w, b):
            B, C, H, W = x.shape
            Ho, Wo = (offsets.shape[2], offsets.shape[3])
            K2 = K * K
            off = offsets.reshape(B, K2, 2, Ho, Wo)
            ky, kx = jnp.meshgrid(jnp.arange(K), jnp.arange(K), indexing='ij')
            ky = ky.reshape(K2).astype(x.dtype)
            kx = kx.reshape(K2).astype(x.dtype)
            oy = (jnp.arange(Ho) * STRIDE - PAD).astype(x.dtype)
            ox = (jnp.arange(Wo) * STRIDE - PAD).astype(x.dtype)
            py = oy[None, None, :, None] + ky[None, :, None, None] + off[:, :, 0]
            px = ox[None, None, None, :] + kx[None, :, None, None] + off[:, :, 1]
            y0 = jnp.floor(py)
            x0 = jnp.floor(px)
            wy = py - y0
            wx = px - x0
            y0i = y0.astype(jnp.int32)
            x0i = x0.astype(jnp.int32)
            xf = x.reshape(B, C, H * W)
            gather = jax.vmap(lambda xb, ib: xb[:, ib])

            def corner(yi, xi, cw):
                valid = (yi >= 0) & (yi < H) & (xi >= 0) & (xi < W)
                idx = jnp.clip(yi, 0, H - 1) * W + jnp.clip(xi, 0, W - 1)
                v = gather(xf, idx)
                return v * (cw * valid.astype(x.dtype))[:, None]
            sampled = corner(y0i, x0i, (1 - wy) * (1 - wx)) + corner(y0i, x0i + 1, (1 - wy) * wx) + corner(y0i + 1, x0i, wy * (1 - wx)) + corner(y0i + 1, x0i + 1, wy * wx)
            wr = w.reshape(w.shape[0], C, K2)
            out = jnp.einsum('bckhw,ock->bohw', sampled, wr)
            return out + b[None, :, None, None]
        key = jax.random.key(seed)
        k1, k2, k3, k4, k5 = jax.random.split(key, 5)
        B, C, H, W, O = (8, 128, 96, 96, 128)
        x = jax.random.normal(k1, (B, C, H, W), dtype=jnp.float32)
        offset_w = jax.random.normal(k2, (2 * K * K, C, K, K), dtype=jnp.float32) * 0.01
        offset_b = jax.random.normal(k3, (2 * K * K,), dtype=jnp.float32) * 0.01
        conv_w = jax.random.normal(k4, (O, C, K, K), dtype=jnp.float32) * (1.0 / np.sqrt(C * K * K))
        conv_b = jax.random.normal(k5, (O,), dtype=jnp.float32) * 0.01
        return {'x': x, 'offset_w': offset_w, 'offset_b': offset_b, 'conv_w': conv_w, 'conv_b': conv_b}
    _L1_conv_all = _L1_conv_setup()
    _L1_conv_in = {k: v for k, v in _L1_conv_all.items() if k in ('offset_w', 'offset_b', 'conv_w', 'conv_b', )}
    del _L1_conv_all

    def _L1_ffn_setup():
        import jax, jax.numpy as jnp
        import numpy as np
        B, S, D, E, H, O, K = (512, 2048, 128, 64, 512, 128, 8)
        key = jax.random.key(seed)
        k0, k1, k2, k3 = jax.random.split(key, 4)
        x = jax.random.normal(k0, (B, S, D), dtype=jnp.float32)
        gate_w = jax.random.normal(k1, (E, D), dtype=jnp.float32) * (1.0 / np.sqrt(D))
        gate_b = jnp.zeros((E,), dtype=jnp.float32)
        weight1 = jax.random.uniform(k2, (E, D + 1, H), dtype=jnp.float32, minval=-1.0, maxval=1.0) * (1.0 / np.sqrt(D + 1))
        weight2 = jax.random.uniform(k3, (E, H + 1, O), dtype=jnp.float32, minval=-1.0, maxval=1.0) * (1.0 / np.sqrt(H + 1))
        return {'x': x, 'gate_w': gate_w, 'gate_b': gate_b, 'weight1': weight1, 'weight2': weight2}
    _L1_ffn_all = _L1_ffn_setup()
    _L1_ffn_in = {k: v for k, v in _L1_ffn_all.items() if k in ('gate_w', 'gate_b', 'weight1', 'weight2', )}
    del _L1_ffn_all

    return {
        "x": x,
        "L0_conv_conv_w": _L0_conv_in["conv_w"],
        "L0_conv_bn_qkv_gamma": _L0_conv_in["bn_qkv_gamma"],
        "L0_conv_bn_qkv_beta": _L0_conv_in["bn_qkv_beta"],
        "L0_conv_bn_sim_gamma": _L0_conv_in["bn_sim_gamma"],
        "L0_conv_bn_sim_beta": _L0_conv_in["bn_sim_beta"],
        "L0_conv_bn_out_gamma": _L0_conv_in["bn_out_gamma"],
        "L0_conv_bn_out_beta": _L0_conv_in["bn_out_beta"],
        "L0_conv_rel_emb": _L0_conv_in["rel_emb"],
        "L0_ffn_W": _L0_ffn_in["W"],
        "L0_ffn_V": _L0_ffn_in["V"],
        "L0_ffn_gamma": _L0_ffn_in["gamma"],
        "L0_ffn_beta": _L0_ffn_in["beta"],
        "L1_conv_offset_w": _L1_conv_in["offset_w"],
        "L1_conv_offset_b": _L1_conv_in["offset_b"],
        "L1_conv_conv_w": _L1_conv_in["conv_w"],
        "L1_conv_conv_b": _L1_conv_in["conv_b"],
        "L1_ffn_gate_w": _L1_ffn_in["gate_w"],
        "L1_ffn_gate_b": _L1_ffn_in["gate_b"],
        "L1_ffn_weight1": _L1_ffn_in["weight1"],
        "L1_ffn_weight2": _L1_ffn_in["weight2"],
    }

def reference(x, L0_conv_conv_w, L0_conv_bn_qkv_gamma, L0_conv_bn_qkv_beta, L0_conv_bn_sim_gamma, L0_conv_bn_sim_beta, L0_conv_bn_out_gamma, L0_conv_bn_out_beta, L0_conv_rel_emb, L0_ffn_W, L0_ffn_V, L0_ffn_gamma, L0_ffn_beta, L1_conv_offset_w, L1_conv_offset_b, L1_conv_conv_w, L1_conv_conv_b, L1_ffn_gate_w, L1_ffn_gate_b, L1_ffn_weight1, L1_ffn_weight2):
    import jax
    import jax.numpy as jnp
    def _L0_conv_ref(input, conv_w, bn_qkv_gamma, bn_qkv_beta, bn_sim_gamma, bn_sim_beta, bn_out_gamma, bn_out_beta, rel_emb):
        import jax, jax.numpy as jnp
        import numpy as np
        B, CIN, H, W = (4, 128, 128, 128)
        COUT, GROUPS, SPAN = (128, 8, 128)
        GC = COUT // GROUPS
        QC = GC // 2
        EPS = 1e-05

        def _bn(x, gamma, beta, ch_axis=1):
            axes = tuple((i for i in range(x.ndim) if i != ch_axis))
            m = x.mean(axes, keepdims=True)
            v = x.var(axes, keepdims=True)
            shape = [1] * x.ndim
            shape[ch_axis] = -1
            return (x - m) / jnp.sqrt(v + EPS) * gamma.reshape(shape) + beta.reshape(shape)
        x = jnp.transpose(input, (0, 2, 1, 3)).reshape(B * H, CIN, W)
        s = W
        qkv = jnp.einsum('oc,ncw->now', conv_w, x)
        qkv = _bn(qkv, bn_qkv_gamma, bn_qkv_beta)
        qkv = qkv.reshape(B * H, GROUPS, 2 * GC, s)
        q, k, v = (qkv[:, :, :QC], qkv[:, :, QC:2 * QC], qkv[:, :, 2 * QC:])
        idx = jnp.arange(s)[:, None] - jnp.arange(s)[None, :] + SPAN - 1
        emb = rel_emb[:, idx.reshape(-1)].reshape(2 * GC, s, s)
        q_emb, k_emb, v_emb = (emb[:QC], emb[QC:2 * QC], emb[2 * QC:])
        q_embedded = jnp.einsum('ngci,cij->ngij', q, q_emb)
        k_embedded = jnp.einsum('ngci,cij->ngij', k, k_emb)
        qk = jnp.einsum('ngci,ngcj->ngij', q_embedded, k_embedded)
        sim = jnp.concatenate([qk, q_embedded, k_embedded], axis=1)
        sim = _bn(sim, bn_sim_gamma, bn_sim_beta)
        sim = sim.reshape(B * H, 3, GROUPS, s, s).sum(axis=1)
        sim = jax.nn.softmax(sim, axis=3)
        attn = jnp.einsum('ngij,ngcj->ngci', sim, v)
        attn_emb = jnp.einsum('ngij,cij->ngci', sim, v_emb)
        out = jnp.concatenate([attn, attn_emb], axis=-1)
        out = out.reshape(B * H, 2 * COUT, s)
        out = _bn(out, bn_out_gamma, bn_out_beta)
        out = out.reshape(B, H, COUT, 2, s).sum(axis=-2)
        return jnp.transpose(out, (0, 2, 1, 3))

    def _L0_ffn_ref(x, W, V, gamma, beta):
        import jax, jax.numpy as jnp
        import numpy as np
        BN_EPS = 1e-05
        B, T, H = (x.shape[0], x.shape[1], W.shape[0])
        Wx = jnp.einsum('bti,hi->bth', x, W)
        flat = Wx.reshape(B * T, H)
        mean = jnp.mean(flat, axis=0)
        var = jnp.var(flat, axis=0)
        Wx = ((flat - mean) * jax.lax.rsqrt(var + BN_EPS) * gamma + beta).reshape(B, T, H)
        Vt = V.T

        def step(yt, wx_t):
            yt = jax.nn.sigmoid(wx_t + yt @ Vt)
            return (yt, yt)
        y0 = jnp.zeros((B, H), dtype=Wx.dtype)
        _, ys = jax.lax.scan(step, y0, jnp.swapaxes(Wx, 0, 1))
        return jnp.swapaxes(ys, 0, 1)

    def _L1_conv_ref(x, offset_w, offset_b, conv_w, conv_b):
        import jax, jax.numpy as jnp
        import numpy as np
        from jax import lax
        K = 3
        STRIDE = 1
        PAD = 1

        def _conv2d(x, w, b, stride, pad):
            y = lax.conv_general_dilated(x, w, window_strides=(stride, stride), padding=((pad, pad), (pad, pad)), dimension_numbers=('NCHW', 'OIHW', 'NCHW'))
            return y + b[None, :, None, None]

        def _deform_conv2d(x, offsets, w, b):
            B, C, H, W = x.shape
            Ho, Wo = (offsets.shape[2], offsets.shape[3])
            K2 = K * K
            off = offsets.reshape(B, K2, 2, Ho, Wo)
            ky, kx = jnp.meshgrid(jnp.arange(K), jnp.arange(K), indexing='ij')
            ky = ky.reshape(K2).astype(x.dtype)
            kx = kx.reshape(K2).astype(x.dtype)
            oy = (jnp.arange(Ho) * STRIDE - PAD).astype(x.dtype)
            ox = (jnp.arange(Wo) * STRIDE - PAD).astype(x.dtype)
            py = oy[None, None, :, None] + ky[None, :, None, None] + off[:, :, 0]
            px = ox[None, None, None, :] + kx[None, :, None, None] + off[:, :, 1]
            y0 = jnp.floor(py)
            x0 = jnp.floor(px)
            wy = py - y0
            wx = px - x0
            y0i = y0.astype(jnp.int32)
            x0i = x0.astype(jnp.int32)
            xf = x.reshape(B, C, H * W)
            gather = jax.vmap(lambda xb, ib: xb[:, ib])

            def corner(yi, xi, cw):
                valid = (yi >= 0) & (yi < H) & (xi >= 0) & (xi < W)
                idx = jnp.clip(yi, 0, H - 1) * W + jnp.clip(xi, 0, W - 1)
                v = gather(xf, idx)
                return v * (cw * valid.astype(x.dtype))[:, None]
            sampled = corner(y0i, x0i, (1 - wy) * (1 - wx)) + corner(y0i, x0i + 1, (1 - wy) * wx) + corner(y0i + 1, x0i, wy * (1 - wx)) + corner(y0i + 1, x0i + 1, wy * wx)
            wr = w.reshape(w.shape[0], C, K2)
            out = jnp.einsum('bckhw,ock->bohw', sampled, wr)
            return out + b[None, :, None, None]
        offsets = _conv2d(x, offset_w, offset_b, STRIDE, PAD)
        return _deform_conv2d(x, offsets, conv_w, conv_b)

    def _L1_ffn_ref(x, gate_w, gate_b, weight1, weight2):
        import jax, jax.numpy as jnp
        import numpy as np
        B, S, D, E, H, O, K = (512, 2048, 128, 64, 512, 128, 8)
        Bn, Sn, Dn = x.shape
        logits = jnp.einsum('bsd,ed->bse', x, gate_w) + gate_b
        probs = jax.nn.softmax(logits, axis=1)
        vals, idx = jax.lax.top_k(probs.transpose(0, 2, 1), K)
        topv = vals.transpose(0, 2, 1)
        topi = idx.transpose(0, 2, 1)
        flat_idx = topi.reshape(Bn, K * E)
        gathered = jnp.take_along_axis(x, flat_idx[:, :, None], axis=1)
        gathered = gathered.reshape(Bn, K, E, Dn)
        pooled = jnp.einsum('bked,bke->bed', gathered, topv)
        ones = jnp.ones((E, Bn, 1), dtype=x.dtype)
        h = jnp.concatenate([pooled.transpose(1, 0, 2), ones], axis=-1)
        h = jax.nn.gelu(jnp.einsum('ebd,edh->ebh', h, weight1), approximate=False)
        h = jnp.concatenate([h, ones], axis=-1)
        out = jnp.einsum('ebh,eho->ebo', h, weight2)
        out = out.transpose(1, 0, 2)
        weighted = jnp.einsum('beo,bke->bkeo', out, topv).reshape(Bn, K * E, O)
        outputs = jnp.zeros((Bn, Sn, O), dtype=x.dtype)
        outputs = outputs.at[jnp.arange(Bn)[:, None], flat_idx].add(weighted)
        return outputs

    def _gn(v, G=32, eps=1e-5):
        B_, C_, H_, W_ = v.shape
        g = v.reshape(B_, G, C_ // G, H_, W_)
        m = jnp.mean(g, axis=(2, 3, 4), keepdims=True)
        s = jnp.var(g, axis=(2, 3, 4), keepdims=True)
        return ((g - m) / jnp.sqrt(s + eps)).reshape(v.shape)

    def _ln_c(v, eps=1e-6):
        m = jnp.mean(v, axis=1, keepdims=True)
        s = jnp.var(v, axis=1, keepdims=True)
        return (v - m) / jnp.sqrt(s + eps)

    def _ln_t(v, eps=1e-5):
        m = jnp.mean(v, axis=-1, keepdims=True)
        s = jnp.var(v, axis=-1, keepdims=True)
        return (v - m) / jnp.sqrt(s + eps)

    def _to_tokens(v):
        B_, C_, H_, W_ = v.shape
        return v.reshape(B_, C_, H_ * W_).transpose(0, 2, 1)
    def _from_tokens(t, like):
        B_, C_, H_, W_ = like.shape
        return t.transpose(0, 2, 1).reshape(B_, C_, H_, W_)

    x = x + _L0_conv_ref(_ln_c(x), L0_conv_conv_w, L0_conv_bn_qkv_gamma, L0_conv_bn_qkv_beta, L0_conv_bn_sim_gamma, L0_conv_bn_sim_beta, L0_conv_bn_out_gamma, L0_conv_bn_out_beta, L0_conv_rel_emb)
    t = _to_tokens(x)
    t = t + _L0_ffn_ref(_ln_t(t), L0_ffn_W, L0_ffn_V, L0_ffn_gamma, L0_ffn_beta)
    x = _from_tokens(t, x)
    x = x + _L1_conv_ref(_ln_c(x), L1_conv_offset_w, L1_conv_offset_b, L1_conv_conv_w, L1_conv_conv_b)
    t = _to_tokens(x)
    t = t + _L1_ffn_ref(_ln_t(t), L1_ffn_gate_w, L1_ffn_gate_b, L1_ffn_weight1, L1_ffn_weight2)
    x = _from_tokens(t, x)
    return x


_drawn_inputs = setup_inputs


def setup_inputs(seed=0):
    import zlib

    import numpy as np

    out = dict(_drawn_inputs(seed))
    spreads = {'L0_conv_bn_qkv_gamma': (1.0, 0.2),
     'L0_conv_bn_qkv_beta': (0.0, 0.1),
     'L0_conv_bn_sim_gamma': (1.0, 0.2),
     'L0_conv_bn_sim_beta': (0.0, 0.8),
     'L0_conv_bn_out_gamma': (1.0, 0.2),
     'L0_conv_bn_out_beta': (0.0, 0.1),
     'L0_ffn_gamma': (1.0, 0.6),
     'L0_ffn_beta': (0.0, 0.587),
     'L1_ffn_gate_b': (0.0, 0.1)}
    factors = {'L1_conv_offset_b': 8.0,
     'L1_conv_conv_b': 8.0,
     'L1_ffn_gate_w': 8.0,
     'L1_ffn_weight1': 8.0,
     'L1_ffn_weight2': 8.0}
    for name, (base, spread) in spreads.items():
        noise = np.random.default_rng([zlib.crc32(name.encode()), seed]).standard_normal(out[name].shape)
        drawn = base * np.exp(spread * noise) if base else spread * noise
        out[name] = jnp.asarray(drawn.astype(out[name].dtype))
    for name, factor in factors.items():
        out[name] = (out[name] * factor).astype(out[name].dtype)
    return out
```

```python
from contextlib import ExitStack, contextmanager

import concourse.bass as bass
from concourse import mybir

F32 = mybir.dt.float32
I32 = mybir.dt.int32
U32 = mybir.dt.uint32
ALU = mybir.AluOpType
ACT = mybir.ActivationFunctionType
AX = mybir.AxisListType
DS = bass.ds

B, C, H, W = 4, 128, 128, 128
N = B * H
T = H * W
G = 8
QC, VC = 8, 16
REL = 2 * W - 1
EPS = 1e-5
LNC_EPS = 1e-6
BANK = 512

RB = 8
HB = RB * G
BLOCKS = N // RB
PACK = BANK // W
HG = HB // PACK
IG = BANK // HB


class Scope:

    def __init__(self, nc, sems):
        self.nc, self.own, self.names, self.ctx = nc, ExitStack(), [], ExitStack()

    def __enter__(self):
        return self

    def __exit__(self, kind, *a):
        self.ctx.close()
        if kind is None:
            with self.nc.Block() as block:
                @block.gpsimd
                def _(pool):
                    for n in self.names:
                        pool.sem_clear(n)
        self.own.close()

    def sb(self, name, shape, dt=F32):
        return self.ctx.enter_context(self.nc.sbuf_tensor(name, shape, dt))

    def ps(self, name, shape, dt=F32):
        return self.ctx.enter_context(self.nc.psum_tensor(name, shape, dt))

    def sem(self, name):
        self.names.append(self.own.enter_context(self.nc.semaphore(name)))
        return self.names[-1]


def setup_phase(nc, sems, ident, mean_mat, center_mat):
    with Scope(nc, sems) as s:
        made = s.sem("set_made")
        with nc.Block() as block:
            @block.gpsimd
            def _(pool):
                pool.memset(ident[:], 0.0).then_inc(made, 1)
                pool.memset(mean_mat[:], 1.0 / C).then_inc(made, 1)
                pool.wait_ge(made, 2)
                pool.affine_select(out=ident[:], in_=ident[:], compare_op=ALU.not_equal, fill=1.0, base=0,
                                   pattern=[[-1, 128]], channel_multiplier=1).then_inc(made, 1)
                pool.wait_ge(made, 3)
                pool.tensor_tensor(center_mat[:], ident[:], mean_mat[:], ALU.subtract).then_inc(made, 1)
                pool.wait_ge(made, 4)


def attention_phase(nc, sems, ident, mean_mat, io, stats_only, coef):
    tag = "sa" if stats_only else "at"
    NEV = 64 if stats_only else 64 + 16 + 8
    HALF = NEV // 2
    NA, ND, NQ = 4, 2, 2
    with Scope(nc, sems) as s:
        qk_in = s.sb(f"{tag}_qk_in", [40, G * RB * W])
        rel = s.sb(f"{tag}_rel", [40, REL])
        span_t = [s.sb(f"{tag}_span_t{x}", [128, HB, W]) for x in range(2)]
        span = [s.sb(f"{tag}_span{x}", [128, HB, W]) for x in range(2)]
        bank_a = s.ps(f"{tag}_bank_a", [128, NA, BANK])
        bank_d = s.ps(f"{tag}_bank_d", [128, ND, BANK])
        bank_q = s.ps(f"{tag}_bank_q", [128, NQ, BANK])
        rel_in = s.sem(f"{tag}_rel_in")
        qk_loaded = s.sem(f"{tag}_qk_loaded")
        qk_spent = s.sem(f"{tag}_qk_spent")
        filled_a, filled_d = s.sem(f"{tag}_filled_a"), s.sem(f"{tag}_filled_d")
        emptied_a, emptied_d = s.sem(f"{tag}_emptied_a"), s.sem(f"{tag}_emptied_d")
        sim_filled, sim_emptied = s.sem(f"{tag}_sim_filled"), s.sem(f"{tag}_sim_emptied")
        if stats_only:
            bn = s.sb("sa_bn", [128, 3 * G, 2, 6])
            agg = s.sb("sa_agg", [128, 3 * G, 2])
            hist = s.sb("sa_hist", [128, BLOCKS, 3 * G * 2])
            span_seen = s.sem("sa_span_seen")
            step = s.sem("sa_step")
        else:
            pt = span_t[0]
            sim = s.sb("at_sim", [128, 4, BANK])
            key_part = s.sb("at_key_part", [128, 2, BANK])
            nmax = s.sb("at_nmax", [128, 4, PACK])
            den = s.sb("at_den", [128, 4, PACK])
            inv = s.sb("at_inv", [128, 4, PACK])
            v_in = s.sb("at_v_in", [128, RB, C])
            rel_v = s.sb("at_rel_v", [128, W * VC])
            attn_i = s.sb("at_attn_i", [128, RB, C])
            attn_c = s.sb("at_attn_c", [128, RB, W])
            emb_c = s.sb("at_emb_c", [HB, VC, W])
            rel_v_in, v_loaded, v_spent = s.sem("at_rel_v_in"), s.sem("at_v_loaded"), s.sem("at_v_spent")
            part_made, sim_made, max_made = s.sem("at_part_made"), s.sem("at_sim_made"), s.sem("at_max_made")
            part_step, pool_passed = s.sem("at_part_step"), s.sem("at_pool_passed")
            exp_made, inv_made, prob_made = s.sem("at_exp_made"), s.sem("at_inv_made"), s.sem("at_prob_made")
            attn_stored, emb_stored = s.sem("at_attn_stored"), s.sem("at_emb_stored")

        def bank_of(j):
            n = j // 2
            return (bank_a[:, n % NA], filled_a, emptied_a, n) if j % 2 == 0 else (bank_d[:, n % ND], filled_d, emptied_d, n)

        PT0, EM0, AV0, TR0 = 64, 80, 84, 86

        def evacuate(eng, copy, j, emptied, filled, blk):
            bank, _, _, n = bank_of(j)
            eng.wait_ge(filled, blk * HALF + n + 1)
            if j < 32:
                x, k = j // 16, j % 16
                out = span_t[x][:, :, k * IG:(k + 1) * IG]
                src = bank.rearrange("p (i h) -> p h i", i=IG)
            elif j < 64:
                x, k = (j - 32) // 16, j % 16
                if stats_only and k < 2:
                    eng.wait_ge(span_seen, blk * 2 + x + 1)
                out = span[x][:, k * PACK:(k + 1) * PACK, :]
                src = bank.rearrange("p (h i) -> p h i", h=PACK)
            elif j < EM0:
                k = j - PT0
                out = pt[:, k * PACK:(k + 1) * PACK, :]
                src = bank.rearrange("p (h i) -> p h i", h=PACK)
            elif j < AV0:
                k = j - EM0
                if k < 2:
                    eng.wait_ge(emb_stored, blk * 16 + 16)
                out = emb_c[:, :, 32 * k:32 * k + 32]
                src = bank[0:HB].rearrange("p (i c) -> p c i", c=VC)
            elif j < TR0:
                k = j - AV0
                out = attn_i[:, 4 * k:4 * k + 4, :]
                src = bank.rearrange("p (n c) -> p n c", n=4)
            else:
                k = j - TR0
                eng.wait_ge(attn_stored, blk * 16 + 16)
                out = attn_c[:, 4 * k:4 * k + 4, :]
                src = bank.rearrange("p (n i) -> p n i", n=4)
            copy(out, src).then_inc(emptied, 1)

        block_ctx = ExitStack()
        block = block_ctx.enter_context(nc.Block())

        @block.sync
        def _(sp):
            sp.dma_start(rel[0:QC, :], io["rel_q"]).then_inc(rel_in, 16)
            sp.dma_start(rel[32:32 + QC, :], io["rel_k"]).then_inc(rel_in, 16)
            if not stats_only:
                sp.dma_start(rel_v[:], bass.AP(io["rel_v"].tensor, 0, [[VC, 128], [1, W * VC]])
                             ).then_inc(rel_v_in, 16)
            with sp.Fori(0, BLOCKS) as blk:
                sp.wait_ge(qk_spent, blk + 1)
                for x in range(2):
                    sp.dma_start(qk_in[32 * x:32 * x + QC, :].rearrange("c (g f) -> c g f", g=G),
                                 io["qk"][x][:, :, DS(blk * (RB * W), RB * W)]).then_inc(qk_loaded, 16)
                if not stats_only:
                    sp.wait_ge(v_spent, blk + 1)
                    sp.dma_start(v_in[:].rearrange("p n c -> p (n c)"),
                                 io["v"][:, DS(blk * (RB * C), RB * C)]).then_inc(v_loaded, 16)

        @block.tensor
        def _(pe):
            pe.sem_inc(qk_spent, 1)
            if not stats_only:
                pe.sem_inc(v_spent, 1)
            pe.wait_ge(rel_in, 32)
            with pe.Fori(0, BLOCKS) as blk:
                pe.wait_ge(qk_loaded, blk * 32 + 32)
                for x in range(2):
                    q = qk_in[32 * x:32 * x + QC, :].rearrange("c (h i) -> c h i", i=W)
                    for k in range(16):
                        bank, filled, emptied, n = bank_of(16 * x + k)
                        ring = NA if k % 2 == 0 else ND
                        pe.wait_ge(emptied, blk * HALF + n + 1)
                        for i in range(k * IG, (k + 1) * IG):
                            last = pe.matmul(bank[:, (i % IG) * HB:(i % IG + 1) * HB],
                                             rel[32 * x:32 * x + QC, W - 1 - i:2 * W - 1 - i],
                                             q[:, :, i], start=True, stop=True)
                        last.then_inc(filled, 1)
                for x in range(2):
                    pe.wait_ge(emptied_a, blk * HALF + 8 * (x + 1) + NA)
                    pe.wait_ge(emptied_d, blk * HALF + 8 * (x + 1) + ND)
                    if x == 1:
                        pe.sem_inc(qk_spent, 1)
                    for k in range(16):
                        bank, filled, emptied, n = bank_of(32 + 16 * x + k)
                        pe.wait_ge(emptied, blk * HALF + n + 1)
                        for h in range(PACK):
                            last = pe.transpose(bank[:, h * W:(h + 1) * W], span_t[x][:, k * PACK + h, :], ident[:])
                        last.then_inc(filled, 1)
                pe.wait_ge(emptied_a, blk * HALF + 32 + NA)
                pe.wait_ge(emptied_d, blk * HALF + 32 + ND)

                def turn_probs(k):
                    bank, filled, emptied, n = bank_of(PT0 + k)
                    pe.wait_ge(prob_made, blk * HG + k + 1)
                    pe.wait_ge(emptied, blk * HALF + n + 1)
                    for h in range(PACK):
                        last = pe.transpose(bank[:, h * W:(h + 1) * W], sim[:, k % 4, h * W:(h + 1) * W], ident[:])
                    last.then_inc(filled, 1)

                for k in range(HG):
                    pe.wait_ge(sim_emptied, blk * HG + k + 1)
                    for h in range(PACK):
                        head = k * PACK + h
                        last = pe.matmul(bank_q[:, k % NQ, h * W:(h + 1) * W], span[0][:, head, :], span[1][:, head, :],
                                         start=True, stop=True)
                    last.then_inc(sim_filled, 1)
                    if not stats_only and k >= 3:
                        turn_probs(k - 3)
                if not stats_only:
                    for k in range(HG - 3, HG):
                        turn_probs(k)
                    pe.wait_ge(emptied_a, blk * HALF + 40 + NA)
                    pe.wait_ge(emptied_d, blk * HALF + 40 + ND)
                    pe.wait_ge(rel_v_in, 16)
                    for k in range(4):
                        bank, filled, emptied, n = bank_of(EM0 + k)
                        pe.wait_ge(emptied, blk * HALF + n + 1)
                        for i in range(32):
                            p = 32 * k + i
                            last = pe.matmul(bank[0:HB, i * VC:(i + 1) * VC], pt[:, :, p], rel_v[:, (W - 1 - p) * VC:(W - p) * VC],
                                             start=True, stop=True)
                        last.then_inc(filled, 1)
                    pe.wait_ge(v_loaded, blk * 16 + 16)
                    for k in range(2):
                        bank, filled, emptied, n = bank_of(AV0 + k)
                        pe.wait_ge(emptied, blk * HALF + n + 1)
                        for r in range(4):
                            for g in range(G):
                                row = 4 * k + r
                                last = pe.matmul(bank[:, r * C + g * VC:r * C + (g + 1) * VC], pt[:, g * RB + row, :],
                                                 v_in[:, row, g * VC:(g + 1) * VC], start=True, stop=True)
                        last.then_inc(filled, 1)
                    pe.wait_ge(emptied_a, blk * HALF + 43 + NA)
                    pe.wait_ge(emptied_d, blk * HALF + 43 + ND)
                    pe.sem_inc(v_spent, 1)
                    for k in range(2):
                        bank, filled, emptied, n = bank_of(TR0 + k)
                        pe.wait_ge(emptied, blk * HALF + n + 1)
                        for r in range(4):
                            last = pe.transpose(bank[:, r * W:(r + 1) * W], attn_i[:, 4 * k + r, :], ident[:])
                        last.then_inc(filled, 1)

        @block.scalar
        def _(act):
            act.sem_inc(emptied_a, NA)
            if not stats_only:
                act.sem_inc(attn_stored, 16)
                act.sem_inc(emb_stored, 16)
            with act.Fori(0, BLOCKS) as blk:
                for j in range(0, 64, 2):
                    evacuate(act, act.copy, j, emptied_a, filled_a, blk)
                if not stats_only:
                    for k in range(HG + 3):
                        if k < HG:
                            act.wait_ge(max_made, blk * HG + k + 1)
                            for h in range(PACK):
                                last = act.activation(sim[:, k % 4, h * W:(h + 1) * W], sim[:, k % 4, h * W:(h + 1) * W],
                                                      ACT.Exp, bias=nmax[:, k % 4, h:h + 1],
                                                      accum_out=den[:, k % 4, h:h + 1])
                            last.then_inc(exp_made, 1)
                        if k >= 3 and (k - 3) % 2 == 0:
                            evacuate(act, act.copy, PT0 + k - 3, emptied_a, filled_a, blk)
                    for j in range(EM0, 88, 2):
                        evacuate(act, act.copy, j, emptied_a, filled_a, blk)
                    act.wait_ge(emptied_a, blk * HALF + HALF + NA)
                    act.wait_ge(emptied_d, blk * HALF + HALF + ND)
                    act.dma_start(io["attn"][:, DS(blk * (RB * W), RB * W)],
                                  attn_c[:].rearrange("p n i -> p (n i)")).then_inc(attn_stored, 16)
                    act.dma_start(io["emb"][DS(blk, 1)].rearrange("o h f -> (o h) f"),
                                  emb_c[:].rearrange("p c i -> p (c i)")).then_inc(emb_stored, 16)
            if not stats_only:
                act.wait_ge(attn_stored, 16 * BLOCKS + 16)
                act.wait_ge(emb_stored, 16 * BLOCKS + 16)

        @block.vector
        def _(dve):
            dve.sem_inc(emptied_d, ND)
            dve.sem_inc(sim_emptied, NQ)
            if stats_only:
                dve.sem_inc(span_seen, 2)
            with dve.Fori(0, BLOCKS) as blk:
                for j in range(1, 64, 2):
                    evacuate(dve, dve.tensor_copy, j, emptied_d, filled_d, blk)
                if stats_only:
                    dve.wait_ge(emptied_a, blk * HALF + 32 + NA)
                    dve.wait_ge(emptied_d, blk * HALF + 32 + ND)
                    for k in range(HG):
                        g, half = k // 2, k % 2
                        for x in range(2):
                            dve.bn_stats(bn[:, (x + 1) * G + g, half, :],
                                         span[x][:, k * PACK:(k + 1) * PACK, :].rearrange("p h j -> p (h j)")
                                         ).then_inc(step, 1)
                        dve.wait_ge(sim_filled, blk * HG + k + 1)
                        dve.bn_stats(bn[:, g, half, :], bank_q[:, k % NQ, :]).then_inc(sim_emptied, 1)
                    dve.wait_ge(step, blk * (2 * HG + 3 * G + 1) + 2 * HG)
                    dve.wait_ge(sim_emptied, blk * HG + HG + NQ)
                    dve.sem_inc(span_seen, 2)
                    for t in range(3 * G):
                        dve.bn_aggr(agg[:, t, :], bn[:, t].rearrange("p a b -> p (a b)")).then_inc(step, 1)
                    dve.wait_ge(step, blk * (2 * HG + 3 * G + 1) + 2 * HG + 3 * G)
                    dve.tensor_copy(hist[:, DS(blk, 1), :].rearrange("p o f -> p (o f)"),
                                    agg[:].rearrange("p t f -> p (t f)")).then_inc(step, 1)
                    dve.wait_ge(step, blk * (2 * HG + 3 * G + 1) + 2 * HG + 3 * G + 1)
                else:
                    for k in range(HG + 3):
                        if k < HG:
                            g = k // 2
                            dve.wait_ge(sim_filled, blk * HG + k + 1)
                            dve.wait_ge(part_made, blk * HG + k + 1)
                            dve.scalar_tensor_tensor(out=sim[:, k % 4, :], in0=bank_q[:, k % NQ, :],
                                                     scalar=coef[:, g:g + 1], in1=sim[:, k % 4, :],
                                                     op0=ALU.mult, op1=ALU.add).then_inc(sim_emptied, 1)
                            dve.wait_ge(sim_emptied, blk * HG + k + 1 + NQ)
                            dve.tensor_reduce(nmax[:, k % 4, :], sim[:, k % 4, :].rearrange("p (h j) -> p h j", h=PACK),
                                              AX.X, ALU.max, negate=True).then_inc(max_made, 1)
                        if 1 <= k < HG + 1:
                            dve.wait_ge(exp_made, blk * HG + k)
                            dve.reciprocal(inv[:, (k - 1) % 4, :], den[:, (k - 1) % 4, :]).then_inc(inv_made, 1)
                        if k >= 3 and (k - 3) % 2 == 1:
                            evacuate(dve, dve.tensor_copy, PT0 + k - 3, emptied_d, filled_d, blk)
                    for j in range(EM0 + 1, 88, 2):
                        evacuate(dve, dve.tensor_copy, j, emptied_d, filled_d, blk)

        @block.gpsimd
        def _(pool):
            if stats_only:
                return
            with pool.Fori(0, BLOCKS) as blk:
                pool.wait_ge(emptied_a, blk * HALF + 32 + NA)
                pool.wait_ge(emptied_d, blk * HALF + 32 + ND)
                for k in range(HG + 2):
                    if k < HG:
                        g = k // 2
                        if k >= 4:
                            _, filled, _, n = bank_of(PT0 + k - 4)
                            pool.wait_ge(filled, blk * HALF + n + 1)
                        pool.sem_inc(pool_passed, 1)
                        hs = slice(k * PACK, (k + 1) * PACK)
                        pool.tensor_scalar(sim[:, k % 4, :], span[0][:, hs, :].rearrange("p h j -> p (h j)"),
                                           coef[:, G + g:G + g + 1], coef[:, 3 * G + g:3 * G + g + 1],
                                           ALU.mult, ALU.add).then_inc(part_step, 1)
                        if k >= 2:
                            pool.wait_ge(part_made, blk * HG + k - 1)
                            pool.sem_inc(pool_passed, 1)
                        pool.tensor_scalar(key_part[:, k % 2, :], span[1][:, hs, :].rearrange("p h j -> p (h j)"),
                                           coef[:, 2 * G + g:2 * G + g + 1], None, ALU.mult).then_inc(part_step, 1)
                        pool.wait_ge(part_step, (blk * HG + k + 1) * 2)
                        pool.tensor_tensor(sim[:, k % 4, :], sim[:, k % 4, :], key_part[:, k % 2, :], ALU.add
                                           ).then_inc(part_made, 1)
                    if k >= 2:
                        m = k - 2
                        pool.wait_ge(inv_made, blk * HG + m + 1)
                        sv = sim[:, m % 4, :].rearrange("p (h j) -> p h j", h=PACK)
                        pool.tensor_tensor(sv, sv, inv[:, m % 4, :].unsqueeze(2).to_broadcast([128, PACK, W]),
                                           ALU.mult).then_inc(prob_made, 1)

        block_ctx.close()
        if stats_only:
            similarity_coefs(nc, s, hist, bank_q, mean_mat, io["sim_gamma"], io["sim_beta"], coef)


def similarity_coefs(nc, s, hist, acc, mean_mat, gamma, beta, coef):
    K = 3 * G
    gb = s.sb("sc_gb", [128, 2, K])
    m1 = s.sb("sc_m1", [128, K])
    dev = s.sb("sc_dev", [128, BLOCKS, K])
    gm = s.sb("sc_gm", [128, K])
    v1 = s.sb("sc_v1", [128, K])
    off = s.sb("sc_off", [128, K])
    gb_in, link, summed, rooted = s.sem("sc_gb_in"), s.sem("sc_link"), s.sem("sc_summed"), s.sem("sc_rooted")
    hv = hist[:].rearrange("p b (k t) -> p b k t", t=2)
    with nc.Block() as block:
        @block.sync
        def _(sp):
            sp.dma_start(gb[:, 0, :], gamma.partition_broadcast(128)).then_inc(gb_in, 16)
            sp.dma_start(gb[:, 1, :], beta.partition_broadcast(128)).then_inc(gb_in, 16)

        @block.tensor
        def _(pe):
            pe.wait_ge(link, 2)
            pe.matmul(acc[:, 0, 0:K], mean_mat[:], m1[:], start=True, stop=True).then_inc(summed, 1)
            pe.wait_ge(link, 8)
            pe.matmul(acc[:, 1, 0:K], mean_mat[:], v1[:], start=True, stop=True).then_inc(summed, 1)

        @block.scalar
        def _(act):
            act.wait_ge(link, 9)
            act.activation(v1[:], v1[:], ACT.Sqrt).then_inc(rooted, 1)

        @block.vector
        def _(dve):
            done = [0]

            def then(ins):
                done[0] += 1
                ins.then_inc(link, 1)
                dve.wait_ge(link, done[0])

            then(dve.tensor_reduce(m1[:], hv[:, :, :, 0].rearrange("p b k -> p k b"), AX.X, ALU.add))
            then(dve.tensor_scalar(m1[:], m1[:], 1.0 / BLOCKS, None, ALU.mult))
            dve.wait_ge(summed, 1)
            then(dve.tensor_copy(gm[:], acc[:, 0, 0:K]))
            then(dve.tensor_tensor(dev[:], hv[:, :, :, 0], gm[:].unsqueeze(1).to_broadcast([128, BLOCKS, K]), ALU.subtract))
            then(dve.tensor_tensor(dev[:], dev[:], dev[:], ALU.mult))
            then(dve.tensor_tensor(dev[:], dev[:], hv[:, :, :, 1], ALU.add))
            then(dve.tensor_reduce(v1[:], dev[:].rearrange("p b k -> p k b"), AX.X, ALU.add))
            then(dve.tensor_scalar(v1[:], v1[:], 1.0 / BLOCKS, None, ALU.mult))
            dve.wait_ge(summed, 2)
            then(dve.tensor_scalar(v1[:], acc[:, 1, 0:K], EPS, None, ALU.add))
            dve.wait_ge(rooted, 1)
            dve.wait_ge(gb_in, 32)
            then(dve.reciprocal(v1[:], v1[:]))
            then(dve.tensor_tensor(coef[:, 0:K], v1[:], gb[:, 0, :], ALU.mult))
            then(dve.tensor_tensor(off[:], coef[:, 0:K], gm[:], ALU.mult))
            then(dve.tensor_tensor(off[:], gb[:, 1, :], off[:], ALU.subtract))
            then(dve.tensor_reduce(coef[:, K:K + G], off[:].rearrange("p (k g) -> p g k", k=3), AX.X, ALU.add))


TILE = 4
COLS = TILE * W
TILES = N // TILE
IMG_TILES = H // TILE
PH, PW = H + 1, W + 2
F = 2


def tile_of(x, b, j):
    return x[DS(b, 1), :, DS(j * COLS, COLS)].rearrange("o c f -> (o c) f")


def norm_phase(nc, sems, consts, kind, io, eps):
    ident, mean_mat, center_mat = consts["ident"], consts["mean_mat"], consts["center_mat"]
    p = kind
    with Scope(nc, sems) as s:
        x_in = s.sb(f"{p}_x_in", [128, F, COLS])
        sq = s.sb(f"{p}_sq", [128, F, COLS])
        std = s.sb(f"{p}_std", [128, F, COLS])
        xn = s.sb(f"{p}_xn", [128, F, COLS])
        eps_col = s.sb(f"{p}_eps", [128, 1])
        cent = s.ps(f"{p}_cent", [128, F, BANK])
        var = s.ps(f"{p}_var", [128, F, BANK])
        out_ps = s.ps(f"{p}_out_ps", [128, 2 * F, BANK])
        eps_set = s.sem(f"{p}_eps_set")
        x_loaded = [s.sem(f"{p}_x_loaded{k}") for k in range(F)]
        cent_made, sq_made, var_made = s.sem(f"{p}_cent_made"), s.sem(f"{p}_sq_made"), s.sem(f"{p}_var_made")
        std_made, rstd_made, xn_made = s.sem(f"{p}_std_made"), s.sem(f"{p}_rstd_made"), s.sem(f"{p}_xn_made")
        prod_made = s.sem(f"{p}_prod_made")
        prod_taken = s.sem(f"{p}_prod_taken")
        prod_taken2 = s.sem(f"{p}_prod_taken2")
        w_in = s.sem(f"{p}_w_in")
        stored = [s.sem(f"{p}_stored{k}") for k in range(F)]
        stats = kind in ("qkv_stats", "ffn")
        if kind in ("qkv_stats", "qkv"):
            w_qk, w_v = s.sb(f"{p}_w_qk", [128, C]), s.sb(f"{p}_w_v", [128, C])
            weights = [(w_qk[:], io["w_qk"]), (w_v[:], io["w_v"])]
        elif kind == "ffn":
            w_f = s.sb("ffn_w", [128, C])
            weights = [(w_f[:], io["w_f"])]
        elif kind == "gate":
            w_g, b_g = s.sb("gate_w", [128, 64]), s.sb("gate_b", [64, 1])
            weights = [(w_g[:], io["w_g"]), (b_g[:], io["b_g"])]
        else:
            weights = []
        if stats:
            kinds = 2 if kind == "qkv_stats" else 1
            hist = s.sb(f"{p}_hist", [128, kinds, TILES, 6])
            mv = s.sb(f"{p}_mv", [128, kinds, 2])
            gb = s.sb(f"{p}_gb", [128, kinds, 2])
            weights += [(gb[:], io["gb"])]
        if kind == "qkv":
            coef_qk, coef_v = consts["coef_qk"], consts["coef_v"]
            diag = s.sb("qkv_diag", [128, 2, C])
            v_row = s.sb("qkv_v_row", [128, 2, C])
            w_v2 = s.sb("qkv_w_v2", [128, C])
            o_qk = s.sb("qkv_o_qk", [128, F, COLS])
            o_v = s.sb("qkv_o_v", [128, F, COLS])
            row_step, row_sum = s.sem("qkv_row_step"), s.sem("qkv_row_sum")
        if kind in ("image", "gate"):
            o_tok = s.sb(f"{p}_o_tok", [128, F, COLS])
            tok_made = s.sem(f"{p}_tok_made")
        if kind == "image":
            zeros = s.sb("image_zeros", [128, 6 * C])
            zeroed, edges = s.sem("image_zeroed"), s.sem("image_edges")
        if kind == "gate":
            o_log = s.sb("gate_o_log", [64, F, COLS])
            log_made = s.sem("gate_log_made")
        n_store = {"qkv_stats": 0, "qkv": 2, "ffn": 1, "image": 3, "gate": 2}[kind]
        block_ctx = ExitStack()
        block = block_ctx.enter_context(nc.Block())

        @contextmanager
        def pairs(eng):
            with eng.Fori(0, B) as b:
                with eng.Fori(0, IMG_TILES // F) as j:
                    yield b, j, b * (IMG_TILES // F) + j

        @block.sync
        def _(sp):
            for dst, src in weights:
                sp.dma_start(dst, src).then_inc(w_in, 16)
            with pairs(sp) as (b, j, i):
                for k in range(F):
                    t = i * F + k
                    sp.wait_ge(prod_taken, t + 1)
                    sp.dma_start(x_in[:, k, :], tile_of(io["src"], b, j * F + k)
                                 ).then_inc(x_loaded[k], 16)
            if n_store:
                for k in range(F):
                    sp.wait_ge(stored[k], 16 * n_store * (TILES // F + 1))

        @block.tensor
        def _(pe):
            pe.wait_ge(w_in, 16 * len(weights)) if weights else None
            if kind == "qkv":
                pe.wait_ge(row_step, 3)
                for r in range(2):
                    last = pe.matmul(out_ps[:, r, 0:C], mean_mat[:], diag[:, r, :], start=True, stop=True)
                last.then_inc(row_sum, 1)
                pe.wait_ge(row_step, 5)
            with pairs(pe) as (b, j, i):
                for k in range(F):
                    t = i * F + k
                    pe.wait_ge(x_loaded[k], 16 * (i + 1))
                    pe.matmul(cent[:, k, :], center_mat[:], x_in[:, k, :], start=True, stop=True).then_inc(cent_made, 1)
                for k in range(F):
                    t = i * F + k
                    pe.wait_ge(sq_made, t + 1)
                    pe.matmul(var[:, k, :], mean_mat[:], sq[:, k, :], start=True, stop=True).then_inc(var_made, 1)
                for k in range(F):
                    t = i * F + k
                    pe.wait_ge(xn_made, t + 1)
                    pe.wait_ge(prod_taken, t + 1)
                    pe.wait_ge(prod_taken2, t + 1)
                    a, b = out_ps[:, 2 * k, :], out_ps[:, 2 * k + 1, :]
                    if kind in ("qkv_stats", "qkv"):
                        last = pe.matmul(a, w_qk[:], xn[:, k, :], start=True, stop=True)
                    if kind == "qkv_stats":
                        last = pe.matmul(b, w_v[:], xn[:, k, :], start=True, stop=True)
                    if kind == "qkv":
                        for r in range(TILE):
                            last = pe.matmul(b[:, r * C:(r + 1) * C], xn[:, k, r * W:(r + 1) * W], w_v2[:], start=True, stop=True)
                    if kind == "ffn":
                        last = pe.matmul(a, w_f[:], xn[:, k, :], start=True, stop=True)
                    if kind == "gate":
                        last = pe.matmul(a[0:64], w_g[:], xn[:, k, :], start=True, stop=True)
                    if kind in ("image", "gate"):
                        for r in range(TILE):
                            last = pe.transpose(b[:, r * C:(r + 1) * C], xn[:, k, r * W:(r + 1) * W], ident[:])
                    last.then_inc(prod_made, 1)

        @block.scalar
        def _(act):
            act.sem_inc(prod_taken2, F)
            for k in range(F if n_store else 0):
                act.sem_inc(stored[k], 16 * n_store)
            act.wait_ge(eps_set, 1)
            with pairs(act) as (b, j, i):
                for k in range(F):
                    t = i * F + k
                    act.wait_ge(cent_made, t + 1)
                    act.activation(sq[:, k, :], cent[:, k, :], ACT.Square).then_inc(sq_made, 1)
                for k in range(F):
                    t = i * F + k
                    act.wait_ge(var_made, t + 1)
                    act.activation(std[:, k, :], var[:, k, :], ACT.Sqrt, bias=eps_col[:]).then_inc(std_made, 1)
                for k in range(F):
                    t = i * F + k
                    act.wait_ge(prod_made, t + 1)
                    if n_store:
                        act.wait_ge(stored[k], 16 * n_store * (i + 1))
                    if kind == "qkv":
                        act.activation(o_qk[:, k, :], out_ps[:, 2 * k, :], ACT.Identity, scale=coef_qk[:, 0:1],
                                       bias=coef_qk[:, 1:2]).then_inc(prod_taken2, 1)
                    elif kind in ("image", "gate"):
                        act.copy(o_tok[:, k, :], out_ps[:, 2 * k + 1, :]).then_inc(prod_taken2, 1)
                    else:
                        act.sem_inc(prod_taken2, 1)
                    if n_store:
                        act.wait_ge(prod_taken, t + F + 1)
                        act.wait_ge(prod_taken2, t + F + 1)
                    if kind == "ffn":
                        act.dma_start(tile_of(io["xn"], b, j * F + k), xn[:, k, :]).then_inc(stored[k], 16)
                    if kind == "qkv":
                        act.dma_start(io["qk_by_channel"][:, DS(t * COLS, COLS)], o_qk[:, k, :]).then_inc(stored[k], 16)
                        act.dma_start(io["v"][:, DS(t * COLS, COLS)], o_v[:, k, :]).then_inc(stored[k], 16)
                    if kind == "gate":
                        act.dma_start(tile_of(io["logits"], b, j * F + k), o_log[:, k, :]).then_inc(stored[k], 16)
                        act.dma_start(io["tokens"][DS(b, 1), DS((j * F + k) * TILE, TILE)].rearrange("o r w c -> w (o r) c"),
                                      o_tok[:, k, :].rearrange("p (r c) -> p r c", r=TILE)).then_inc(stored[k], 16)
                    if kind == "image":
                        act.dma_start(io["rows"][DS(b, 1), :, DS((j * F + k) * TILE + 1, TILE), :].rearrange("o c r w -> (o c) (r w)"),
                                      xn[:, k, :]).then_inc(stored[k], 16)
                        for half in range(2):
                            act.dma_start(io["patches"][DS(b, 1), DS((j * F + k) * TILE + 1 - half, TILE), 1:W + 1, half, :
                                                        ].rearrange("o r w c -> w (o r) c"),
                                          o_tok[:, k, :].rearrange("p (r c) -> p r c", r=TILE)).then_inc(stored[k], 16)

        @block.vector
        def _(dve):
            dve.memset(eps_col[:], eps).then_inc(eps_set, 1)
            dve.sem_inc(prod_taken, F)
            if kind == "qkv":
                dve.wait_ge(w_in, 32)
                for r in range(2):
                    dve.tensor_scalar(diag[:, r, :], ident[:], coef_v[:, r:r + 1], float(C), ALU.mult, ALU.mult).then_inc(row_step, 1)
                dve.sem_inc(row_step, 1)
                dve.wait_ge(row_sum, 1)
                dve.tensor_copy(v_row[:], out_ps[:, 0:2, 0:C]).then_inc(row_step, 1)
                dve.wait_ge(row_step, 4)
                dve.tensor_tensor(w_v2[:], w_v[:], v_row[:, 0, :], ALU.mult).then_inc(row_step, 1)
            with pairs(dve) as (b, j, i):
                for k in range(F):
                    t = i * F + k
                    dve.wait_ge(std_made, t + 1)
                    if kind in ("ffn", "image"):
                        dve.wait_ge(stored[k], 16 * n_store * (i + 1))
                    dve.reciprocal(std[:, k, :], std[:, k, :]).then_inc(rstd_made, 1)
                    dve.wait_ge(rstd_made, t + 1)
                    dve.tensor_tensor(xn[:, k, :], cent[:, k, :], std[:, k, :], ALU.mult).then_inc(xn_made, 1)
                for k in range(F):
                    t = i * F + k
                    dve.wait_ge(prod_made, t + 1)
                    if kind in ("qkv_stats", "ffn"):
                        for m in range(kinds):
                            last = dve.bn_stats(hist[:, m, DS(t, 1), :].rearrange("p o f -> p (o f)"),
                                                out_ps[:, 2 * k + m, :])
                        last.then_inc(prod_taken, 1)
                    elif kind == "qkv":
                        dve.wait_ge(stored[k], 16 * n_store * (i + 1))
                        dve.tensor_tensor(o_v[:, k, :].rearrange("p (r c) -> p r c", r=TILE),
                                          out_ps[:, 2 * k + 1, :].rearrange("p (r c) -> p r c", r=TILE),
                                          v_row[:, 1, :].unsqueeze(1).to_broadcast([128, TILE, C]), ALU.add
                                          ).then_inc(prod_taken, 1)
                    elif kind == "gate":
                        dve.wait_ge(stored[k], 16 * n_store * (i + 1))
                        dve.tensor_scalar(o_log[:, k, :], out_ps[0:64, 2 * k, :], b_g[:, 0:1], None, ALU.add
                                          ).then_inc(prod_taken, 1)
                    else:
                        dve.sem_inc(prod_taken, 1)

        @block.gpsimd
        def _(pool):
            if kind == "image":
                pool.memset(zeros[:], 0.0).then_inc(zeroed, 1)
                pool.wait_ge(zeroed, 1)
                img, rows = io["patches"], io["rows"]
                n = 0
                for b in range(B):
                    for y, half in ((0, 0), (PH - 1, 1)):
                        pool.dma_start(img[b, y, 1:W + 1, half, :].rearrange("(p q) c -> p q c", q=2),
                                       zeros[0:W // 2, 0:2 * C].rearrange("p (q c) -> p q c", q=2)).then_inc(edges, 16)
                        n += 1
                    for x in (0, PW - 1):
                        pool.dma_start(img[b, :, x].rearrange("(p q) h c -> p q (h c)", q=3),
                                       zeros[0:PH // 3, :].rearrange("p (q f) -> p q f", q=3)).then_inc(edges, 16)
                        n += 1
                    for y in (0, H + 1):
                        pool.dma_start(rows[b, :, y, :], zeros[:, 0:W]).then_inc(edges, 16)
                        n += 1
                pool.wait_ge(edges, 16 * n)
        block_ctx.close()
        if stats:
            channel_coefs(nc, s, p, hist, mv, gb, io["coef"])


def channel_coefs(nc, s, p, hist, mv, gb, coef):
    link, rooted = s.sem(f"{p}_cc_link"), s.sem(f"{p}_cc_rooted")
    kinds = hist.shape[1]
    with nc.Block() as block:
        @block.scalar
        def _(act):
            act.wait_ge(link, kinds + 1)
            act.activation(mv[:, :, 1], mv[:, :, 1], ACT.Sqrt).then_inc(rooted, 1)

        @block.vector
        def _(dve):
            done = [0]

            def then(ins):
                done[0] += 1
                ins.then_inc(link, 1)
                dve.wait_ge(link, done[0])

            for m in range(kinds):
                then(dve.bn_aggr(mv[:, m, :], hist[:, m].rearrange("p t f -> p (t f)")))
            then(dve.tensor_scalar(mv[:, :, 1], mv[:, :, 1], EPS, None, ALU.add))
            dve.wait_ge(rooted, 1)
            then(dve.reciprocal(mv[:, :, 1], mv[:, :, 1]))
            for m in range(kinds):
                c = coef[m]
                then(dve.tensor_tensor(c[:, 0:1], mv[:, m, 1:2], gb[:, m, 0:1], ALU.mult))
                then(dve.tensor_tensor(c[:, 1:2], mv[:, m, 0:1], c[:, 0:1], ALU.mult))
                then(dve.tensor_tensor(c[:, 1:2], gb[:, m, 1:2], c[:, 1:2], ALU.subtract))


def mix_phase(nc, sems, io, coef_a, coef_e, stats):
    p = "ms" if stats else "mx"
    MC = RB * W
    with Scope(nc, sems) as s:
        att = s.sb(f"{p}_att", [128, F, MC])
        emb = s.sb(f"{p}_emb", [128, F, MC])
        loaded = [s.sem(f"{p}_loaded{k}") for k in range(F)]
        spent = s.sem(f"{p}_spent")
        per = 16 * (1 + G + (not stats))
        if stats:
            hist = s.sb("ms_hist", [128, 2, 2 * BLOCKS, 6])
            mv, gb = s.sb("ms_mv", [128, 2, 2]), s.sb("ms_gb", [128, 2, 2])
            gb_in = s.sem("ms_gb_in")
        else:
            x = s.sb("mx_x", [128, F, MC])
            shift = s.sb("mx_shift", [128, 1])
            shift_made, att_made, sum_made = s.sem("mx_shift_made"), s.sem("mx_att_made"), s.sem("mx_sum_made")
            out_made = s.sem("mx_out_made")
            stored = [s.sem(f"mx_stored{k}") for k in range(F)]
        block_ctx = ExitStack()
        block = block_ctx.enter_context(nc.Block())

        @block.sync
        def _(sp):
            if stats:
                sp.dma_start(gb[:], io["gb_out"]).then_inc(gb_in, 16)
            with sp.Fori(0, BLOCKS // F) as i:
                for k in range(F):
                    t = i * F + k
                    sp.wait_ge(spent, t + 1)
                    if not stats:
                        sp.wait_ge(stored[k], 16 * (i + 1))
                        sp.dma_start(x[:, k, :], io["x"][DS(t // (H // RB), 1), :, DS((t % (H // RB)) * MC, MC)
                                                         ].rearrange("o c f -> (o c) f")).then_inc(loaded[k], 16)
                    sp.dma_start(att[:, k, :], io["attn"][:, DS(t * MC, MC)]).then_inc(loaded[k], 16)
                    for g in range(G):
                        sp.dma_start(emb[g * VC:(g + 1) * VC, k, :].rearrange("c (n i) -> c n i", i=W),
                                     io["emb"][DS(t, 1), g * RB:(g + 1) * RB].rearrange("o n (c i) -> (o c) n i", i=W)
                                     ).then_inc(loaded[k], 16)
            if not stats:
                for k in range(F):
                    sp.wait_ge(stored[k], 16 * (BLOCKS // F + 1))

        @block.scalar
        def _(act):
            if stats:
                return
            for k in range(F):
                act.sem_inc(stored[k], 16)
            act.wait_ge(shift_made, 1)
            with act.Fori(0, BLOCKS // F) as i:
                for k in range(F):
                    t = i * F + k
                    act.wait_ge(loaded[k], per * (i + 1))
                    act.activation(att[:, k, :], att[:, k, :], ACT.Identity, scale=coef_a[:, 0:1], bias=shift[:]
                                   ).then_inc(att_made, 1)
                for k in range(F):
                    t = i * F + k
                    act.wait_ge(out_made, t + 1)
                    act.dma_start(io["x1"][DS(t // (H // RB), 1), :, DS((t % (H // RB)) * MC, MC)
                                           ].rearrange("o c f -> (o c) f"), att[:, k, :]).then_inc(stored[k], 16)

        @block.vector
        def _(dve):
            dve.sem_inc(spent, F)
            if not stats:
                dve.tensor_tensor(shift[:], coef_a[:, 1:2], coef_e[:, 1:2], ALU.add).then_inc(shift_made, 1)
            with dve.Fori(0, BLOCKS // F) as i:
                for k in range(F):
                    t = i * F + k
                    dve.wait_ge(loaded[k], per * (i + 1))
                    if stats:
                        for m, src in enumerate((att, emb)):
                            for half in range(2):
                                last = dve.bn_stats(hist[:, m, DS(2 * t + half, 1), :].rearrange("p o f -> p (o f)"),
                                                    src[:, k, half * BANK:(half + 1) * BANK])
                        last.then_inc(spent, 1)
                        continue
                    dve.scalar_tensor_tensor(out=x[:, k, :], in0=emb[:, k, :], scalar=coef_e[:, 0:1], in1=x[:, k, :],
                                             op0=ALU.mult, op1=ALU.add).then_inc(sum_made, 1)
                    dve.wait_ge(sum_made, t + 1)
                    dve.wait_ge(att_made, t + 1)
                    dve.tensor_tensor(att[:, k, :], att[:, k, :], x[:, k, :], ALU.add).then_inc(out_made, 1)
                    dve.sem_inc(spent, 1)
            if stats:
                dve.wait_ge(spent, BLOCKS + F)
                dve.wait_ge(gb_in, 16)
        block_ctx.close()
        if stats:
            channel_coefs(nc, s, p, hist, mv, gb, [coef_a, coef_e])


CHUNKS = 32
LEN = T // CHUNKS
SPAN = 64
SPANS = LEN // SPAN
RC = B * CHUNKS
RING = 4


def recurrence_phase(nc, sems, consts, io, coef_f):
    assert RC == 128
    ident = consts["ident"]
    with Scope(nc, sems) as s:
        w_nat = s.sb("rn_w_nat", [128, C])
        w_eff = s.sb("rn_w_eff", [128, C])
        v_t = s.sb("rn_v_t", [128, C])
        diag = s.sb("rn_diag", [128, C])
        xs = s.sb("rn_xs", [128, 2, RC, SPAN])
        os_ = s.sb("rn_os", [128, 2, RC, SPAN])
        y = s.sb("rn_y", [128, RING, RC])
        start = s.sb("rn_start", [128, RC])
        nxt = s.sb("rn_nxt", [128, RC])
        differ = s.sb("rn_differ", [128, RC])
        worst = s.sb("rn_worst", [128, 1])
        again = s.sb("rn_again", [128, 1], I32)
        pre = s.ps("rn_pre", [128, RING, BANK])
        misc = s.ps("rn_misc", [128, BANK])
        w_in, diag_made, eff_made, eff_taken = s.sem("rn_w_in"), s.sem("rn_diag_made"), s.sem("rn_eff_made"), s.sem("rn_eff_taken")
        warm_loaded = s.sem("rn_warm_loaded")
        loaded = [s.sem(f"rn_loaded{k}") for k in range(2)]
        slot_free = s.sem("rn_slot_free")
        pre_made, y_made, added = s.sem("rn_pre_made"), s.sem("rn_y_made"), s.sem("rn_added")
        stored = [s.sem(f"rn_stored{k}") for k in range(2)]
        started = s.sem("rn_started")
        link, counted, settled = s.sem("rn_link"), s.sem("rn_counted"), s.sem("rn_settled")
        judged = s.sem("rn_judged")
        passed = {e: s.sem(f"rn_passed_{e}") for e in ("pe", "act", "dve", "sp", "pool")}
        xn_c = io["xn"].rearrange("b c (k t) -> b c k t", t=LEN)
        x1_c = io["x1"].rearrange("b c (k t) -> b c k t", t=LEN)
        x2_c = io["x2"].rearrange("b c (k t) -> b c k t", t=LEN)
        warm_steps = SPAN

        def rounds(eng, name):
            @contextmanager
            def one():
                with eng.Fori(0, CHUNKS) as r:
                    eng.wait_ge(settled, r + 1)
                    eng.sem_inc(passed[name], 1)
                    go = eng.value_load(again[0:1, 0:1], min_val=0, max_val=1)
                    with eng.If(go > 0):
                        yield r
                    if name == "dve":
                        eng.sem_inc(settled, 1)
            return one()

        block = s.ctx.enter_context(nc.Block())

        @block.sync
        def _(sp):
            sp.dma_start(w_nat[:], io["w_f_nat"]).then_inc(w_in, 16)
            sp.dma_start(v_t[:], io["v_t"]).then_inc(w_in, 16)
            for b in range(B):
                sp.dma_start(xs[:, 1, b * CHUNKS:(b + 1) * CHUNKS, :], xn_c[b, :, :, LEN - SPAN:LEN]).then_inc(warm_loaded, 16)
            with rounds(sp, "sp") as r:
                with sp.Fori(0, SPANS // 2) as j:
                    for k in range(2):
                        n = r * SPANS + j * 2 + k
                        sp.wait_ge(slot_free, n + 1)
                        for b in range(B):
                            sp.dma_start(xs[:, k, b * CHUNKS:(b + 1) * CHUNKS, :],
                                         xn_c[b, :, :, DS((j * 2 + k) * SPAN, SPAN)]).then_inc(loaded[k], 16)
                            sp.dma_start(os_[:, k, b * CHUNKS:(b + 1) * CHUNKS, :],
                                         x1_c[b, :, :, DS((j * 2 + k) * SPAN, SPAN)]).then_inc(loaded[k], 16)

        @block.tensor
        def _(pe):
            pe.wait_ge(w_in, 32)
            pe.wait_ge(diag_made, 1)
            pe.matmul(misc[:, 0:C], w_nat[:], diag[:], start=True, stop=True).then_inc(eff_made, 1)
            pe.wait_ge(eff_taken, 1)
            pe.wait_ge(warm_loaded, 16 * B)
            pe.wait_ge(started, 1)
            with pe.Fori(0, SPAN // RING) as q:
                for u in range(RING):
                    pe.matmul(pre[:, u, 0:RC], w_eff[:], xs[:, 1, :, DS(q * RING + u, 1)].rearrange("p c o -> p (c o)"),
                              start=True, stop=False)
                    pe.wait_ge(y_made, q * RING + u + 1)
                    pe.matmul(pre[:, u, 0:RC], v_t[:], y[:, (u - 1) % RING, :], start=False, stop=True).then_inc(pre_made, 1)
            pe.wait_ge(y_made, warm_steps + 1)
            pe.sem_inc(slot_free, 2)
            pe.wait_ge(link, 3)
            pe.matmul(misc[:, 0:1], consts["mean_mat"][:], worst[:], start=True, stop=True).then_inc(counted, 1)
            with rounds(pe, "pe") as r:
                pe.wait_ge(started, r + 2)
                pe.sem_inc(passed["pe"], 1)
                with pe.Fori(0, SPANS // 2) as j:
                    for k in range(2):
                        pe.wait_ge(loaded[k], 16 * 2 * B * (r * (SPANS // 2) + j + 1))
                        pe.sem_inc(passed["pe"], 1)
                        with pe.Fori(0, SPAN // RING) as q:
                            for u in range(RING):
                                m = r * LEN + (j * 2 + k) * SPAN + q * RING + u
                                pe.matmul(pre[:, u, 0:RC], w_eff[:],
                                          xs[:, k, :, DS(q * RING + u, 1)].rearrange("p c o -> p (c o)"),
                                          start=True, stop=False)
                                pe.wait_ge(y_made, m + warm_steps + 1)
                                pe.matmul(pre[:, u, 0:RC], v_t[:], y[:, (u - 1) % RING, :], start=False, stop=True
                                          ).then_inc(pre_made, 1)
                pe.wait_ge(link, r * 3 + 6)
                pe.matmul(misc[:, 0:1], consts["mean_mat"][:], worst[:], start=True, stop=True).then_inc(counted, 1)

        @block.scalar
        def _(act):
            act.sem_inc(y_made, 1)
            with act.Fori(0, SPAN // RING) as q:
                for u in range(RING):
                    act.wait_ge(pre_made, q * RING + u + 1)
                    act.activation(y[:, u, :], pre[:, u, 0:RC], ACT.Sigmoid, bias=coef_f[:, 1:2]).then_inc(y_made, 1)
            with rounds(act, "act") as r:
                act.wait_ge(started, r + 2)
                act.sem_inc(passed["act"], 1)
                with act.Fori(0, LEN // RING) as q:
                    for u in range(RING):
                        m = r * LEN + q * RING + u
                        act.wait_ge(added, m + 1)
                        act.wait_ge(pre_made, m + warm_steps + 1)
                        act.activation(y[:, u, :], pre[:, u, 0:RC], ACT.Sigmoid, bias=coef_f[:, 1:2]).then_inc(y_made, 1)

        @block.vector
        def _(dve):
            dve.sem_inc(added, RING)
            dve.tensor_scalar(diag[:], ident[:], coef_f[:, 0:1], None, ALU.mult).then_inc(diag_made, 1)
            dve.memset(start[:], 0.0).then_inc(eff_taken, 1)
            dve.memset(nxt[:], 0.0).then_inc(eff_taken, 1)
            dve.wait_ge(eff_made, 1)
            dve.tensor_copy(w_eff[:], misc[:, 0:C]).then_inc(eff_taken, 1)
            dve.wait_ge(eff_taken, 3)
            dve.tensor_copy(y[:, RING - 1, :], start[:]).then_inc(started, 1)

            def judge(m, steps):
                dve.wait_ge(y_made, steps + 1)
                for b in range(B):
                    last = dve.tensor_copy(nxt[:, b * CHUNKS + 1:(b + 1) * CHUNKS], y[:, RING - 1, b * CHUNKS:(b + 1) * CHUNKS - 1])
                last.then_inc(link, 1)
                dve.wait_ge(link, m * 3 + 1)
                dve.tensor_tensor(differ[:], nxt[:], start[:], ALU.not_equal).then_inc(link, 1)
                dve.wait_ge(link, m * 3 + 2)
                dve.tensor_reduce(worst[:], differ[:], AX.X, ALU.add).then_inc(link, 1)
                dve.wait_ge(counted, m + 1)
                if type(m) is int:
                    dve.memset(again[:], 1).then_inc(judged, 1)
                else:
                    dve.tensor_scalar(again[:], misc[:, 0:1], 0.0, None, ALU.is_gt).then_inc(judged, 1)
                dve.tensor_copy(start[:], nxt[:]).then_inc(judged, 1)
                dve.wait_ge(judged, m * 2 + 2)
                dve.tensor_copy(y[:, RING - 1, :], nxt[:]).then_inc(started, 1)

            judge(0, warm_steps)
            dve.sem_inc(settled, 1)
            with rounds(dve, "dve") as r:
                dve.wait_ge(started, r + 2)
                dve.sem_inc(passed["dve"], 1)
                with dve.Fori(0, SPANS // 2) as j:
                    for k in range(2):
                        dve.wait_ge(loaded[k], 16 * 2 * B * (r * (SPANS // 2) + j + 1))
                        dve.sem_inc(passed["dve"], 1)
                        with dve.Fori(0, SPAN // RING) as q:
                            for u in range(RING):
                                m = r * LEN + (j * 2 + k) * SPAN + q * RING + u
                                dve.wait_ge(y_made, m + warm_steps + 2)
                                o = os_[:, k, :, DS(q * RING + u, 1)].rearrange("p c o -> p (c o)")
                                dve.tensor_tensor(o, y[:, u, :], o, ALU.add).then_inc(added, 1)
                dve.wait_ge(added, RING + r * LEN + LEN)
                judge(r + 1, r * LEN + LEN + warm_steps)

        @block.gpsimd
        def _(pool):
            with rounds(pool, "pool") as r:
                with pool.Fori(0, SPANS // 2) as j:
                    for k in range(2):
                        n = r * SPANS + j * 2 + k
                        pool.wait_ge(added, RING + (n + 1) * SPAN)
                        for b in range(B):
                            pool.dma_start(x2_c[b, :, :, DS((j * 2 + k) * SPAN, SPAN)],
                                           os_[:, k, b * CHUNKS:(b + 1) * CHUNKS, :]).then_inc(stored[k], 16)
                        pool.wait_ge(stored[k], 16 * B * (r * (SPANS // 2) + j + 1))
                        pool.sem_inc(slot_free, 1)


TAPS = 9
NP = TILE * TAPS
GR = 12
SR = 8
PATCH = 4 * C
ROW_STEP = PW * 2 * C
COL_STEP = 2 * C


def deform_phase(nc, sems, consts, io):
    ident = consts["ident"]
    with Scope(nc, sems) as s:
        off_w = s.sb("df_off_w", [128, TAPS, 2 * TAPS])
        off_b = s.sb("df_off_b", [2 * TAPS, 1])
        tap_w = s.sb("df_tap_w", [128, TAPS, C])
        tap_b = s.sb("df_tap_b", [128, 1])
        xr = s.sb("df_xr", [128, 2, TILE + 2, W + 2])
        off = s.sb("df_off", [2 * TAPS, COLS])
        base_y = s.sb("df_base_y", [128, IMG_TILES, NP])
        base_x = s.sb("df_base_x", [128, NP])
        base_i = s.sb("df_base_i", [128, B])
        pos = s.sb("df_pos", [128, 2, NP])
        low = s.sb("df_low", [128, 2, NP])
        low_i = s.sb("df_low_i", [128, 2, NP], I32)
        over = s.sb("df_over", [128, 2, NP])
        frac = s.sb("df_frac", [128, 2, 2, NP])
        at = s.sb("df_at", [128, NP])
        idx = s.sb("df_idx", [128, 2, NP], U32)
        wgt = s.sb("df_wgt", [128, 2, NP, 2, 2])
        patch = s.sb("df_patch", [128, GR, PATCH])
        samp = s.sb("df_samp", [128, SR, C])
        samp_t = s.sb("df_samp_t", [128, 2, COLS])
        x2 = s.sb("df_x2", [128, 2, COLS])
        off_ps = s.ps("df_off_ps", [128, BANK])
        pos_ps = s.ps("df_pos_ps", [128, BANK])
        turn_ps = s.ps("df_turn_ps", [128, 3, BANK])
        out_ps = s.ps("df_out_ps", [128, 2, BANK])
        w_in, border, tables = s.sem("df_w_in"), s.sem("df_border"), s.sem("df_tables")
        xr_loaded = [s.sem(f"df_xr_loaded{k}") for k in range(2)]
        x2_loaded = [s.sem(f"df_x2_loaded{k}") for k in range(2)]
        off_made, off_taken, pos_made = s.sem("df_off_made"), s.sem("df_off_taken"), s.sem("df_pos_made")
        link, idx_made = s.sem("df_link"), s.sem("df_idx_made")
        gathered = [s.sem(f"df_gathered{k}") for k in range(GR)]
        pool_passed, pe_passed = s.sem("df_pool_passed"), s.sem("df_pe_passed")
        mixed0, mixed = s.sem("df_mixed0"), s.sem("df_mixed")
        turned, turn_taken = s.sem("df_turned"), s.sem("df_turn_taken")
        tap_done, out_made, out_taken = s.sem("df_tap_done"), s.sem("df_out_made"), s.sem("df_out_taken")
        stored = [s.sem(f"df_stored{k}") for k in range(2)]
        LINKS = 14
        PRIME = 3 * GR

        def sweep(eng, front, taps):
            front(0, 0)
            with eng.Fori(0, TILES // 2 - 1) as i:
                for k in range(2):
                    front(2 * i + k + 1, (k + 1) % 2)
                    taps(2 * i + k, k)
            front(TILES - 1, 1)
            taps(TILES - 2, 0)
            taps(TILES - 1, 1)

        block = s.ctx.enter_context(nc.Block())

        @block.sync
        def _(sp):
            sp.dma_start(off_w[:], io["off_w"]).then_inc(w_in, 16)
            sp.dma_start(off_b[:], io["off_b"]).then_inc(w_in, 16)
            sp.dma_start(tap_w[:], io["tap_w"]).then_inc(w_in, 16)
            sp.dma_start(tap_b[:], io["tap_b"]).then_inc(w_in, 16)
            sp.wait_ge(border, 1)

            def front(t, k):
                b, j = t // IMG_TILES, t % IMG_TILES
                sp.wait_ge(off_made, t + 1)
                sp.dma_start(xr[:, k, :, 1:W + 1],
                             io["rows"][DS(b, 1), :, DS(j * TILE, TILE + 2), :].rearrange("o c r w -> (o c) r w")
                             ).then_inc(xr_loaded[k], 16)
                sp.wait_ge(stored[k], 16 * (t // 2 + 1))
                sp.dma_start(x2[:, k, :], tile_of(io["x2"], b, j)).then_inc(x2_loaded[k], 16)

            def store(t, k):
                b, j = t // IMG_TILES, t % IMG_TILES
                sp.wait_ge(out_taken, t + 3)
                sp.dma_start(tile_of(io["x3"], b, j), x2[:, k, :]).then_inc(stored[k], 16)

            for k in range(2):
                sp.sem_inc(stored[k], 16)
            sweep(sp, front, store)
            for k in range(2):
                sp.wait_ge(stored[k], 16 * (TILES // 2 + 1))

        @block.tensor
        def _(pe):
            pe.sem_inc(off_made, 2)
            pe.wait_ge(w_in, 64)

            def front(t, k):
                pe.wait_ge(xr_loaded[k], 16 * (t // 2 + 1))
                pe.wait_ge(off_taken, t + 1)
                for m in range(TAPS):
                    ky, kx = m // 3, m % 3
                    last = pe.matmul(off_ps[0:2 * TAPS, :], off_w[:, m, :], xr[:, k, ky:ky + TILE, kx:kx + W],
                                     start=(m == 0), stop=(m == TAPS - 1))
                last.then_inc(off_made, 1)
                pe.wait_ge(off_taken, t + 2)
                pe.wait_ge(link, t * LINKS + 2)
                pe.sem_inc(pe_passed, 1)
                for r in range(TILE):
                    last = pe.transpose(pos_ps[:, r * 2 * TAPS:(r + 1) * 2 * TAPS], off[:, r * W:(r + 1) * W],
                                        ident[0:2 * TAPS, 0:2 * TAPS])
                last.then_inc(pos_made, 1)

            def taps(t, k):
                pe.wait_ge(out_taken, t + 1)

                def product(m):
                    pe.wait_ge(turn_taken, t * TAPS + m + 3 + 1)
                    last = pe.matmul(out_ps[:, k, :], tap_w[:, m, :], samp_t[:, (TAPS * k + m) % 2, :],
                                     start=(m == 0), stop=(m == TAPS - 1))
                    last.then_inc(tap_done, 1)

                for m in range(TAPS):
                    pe.wait_ge(turn_taken, t * TAPS + m + 1)
                    for r in range(TILE):
                        pe.wait_ge(mixed, PRIME + 3 * TILE * (TAPS * t + m) + 2 * TILE + r + 1)
                        last = pe.transpose(turn_ps[:, m % 3, r * W:(r + 1) * W], samp[:, ((TAPS * k + m) * TILE + r) % SR, :],
                                            ident[:])
                    last.then_inc(turned, 1)
                    if m >= 1:
                        product(m - 1)
                product(TAPS - 1)

            sweep(pe, front, taps)

        @block.scalar
        def _(act):
            act.sem_inc(off_taken, 1)
            act.sem_inc(turn_taken, 3)
            act.wait_ge(w_in, 64)

            def front(t, k):
                act.wait_ge(off_made, t + 3)
                act.wait_ge(pos_made, t + 1)
                act.activation(off[:], off_ps[0:2 * TAPS, :], ACT.Identity, bias=off_b[:]).then_inc(off_taken, 1)

            def taps(t, k):
                def first(m):
                    for r in range(TILE):
                        q = (TAPS * k + m) * TILE + r
                        n = m * TILE + r
                        g = n % GR
                        act.wait_ge(gathered[g], 16 * (t * (NP // GR) + n // GR + 1))
                        if r == 0:
                            act.wait_ge(turned, t * TAPS + m + 1)
                        act.activation(samp[:, q % SR, :], patch[:, g, 0:C], ACT.Copy, scale=wgt[:, k, r * TAPS + m, 0, 0:1]
                                       ).then_inc(mixed0, 1)

                def take(m):
                    act.wait_ge(turned, t * TAPS + m + 3)
                    act.wait_ge(tap_done, t * TAPS + m + 1)
                    act.copy(samp_t[:, (TAPS * k + m) % 2, :], turn_ps[:, m % 3, :]).then_inc(turn_taken, 1)

                for m in range(TAPS):
                    first(m)
                    if m >= 1:
                        take(m - 1)
                take(TAPS - 1)

            sweep(act, front, taps)

        @block.vector
        def _(dve):
            dve.memset(xr[:], 0.0).then_inc(border, 1)
            dve.sem_inc(pos_made, 1)
            dve.sem_inc(link, 2)
            dve.sem_inc(out_taken, 2)
            dve.sem_inc(turned, 2)
            dve.sem_inc(tap_done, 2)
            dve.sem_inc(mixed, PRIME)
            dve.wait_ge(tables, 2 + B)
            dve.wait_ge(w_in, 64)

            def front(t, k):
                b, j = t // IMG_TILES, t % IMG_TILES
                n = [t * LINKS + 2]

                def then(ins):
                    n[0] += 1
                    ins.then_inc(link, 1)
                    dve.wait_ge(link, n[0])

                o = pos_ps[:, 0:2 * NP].rearrange("p (m d) -> p d m", d=2)
                dve.wait_ge(pos_made, t + 2)
                dve.tensor_tensor(pos[:, 0, :], o[:, 0, :], base_y[:, DS(j, 1), :].rearrange("p o m -> p (o m)"),
                                  ALU.add).then_inc(link, 1)
                n[0] += 1
                then(dve.tensor_tensor(pos[:, 1, :], o[:, 1, :], base_x[:], ALU.add))
                then(dve.tensor_scalar(pos[:], pos[:], -1.0, float(H), ALU.max, ALU.min))
                then(dve.tensor_copy(low_i[:], pos[:]))
                then(dve.tensor_copy(low[:], low_i[:]))
                then(dve.tensor_tensor(over[:], low[:], pos[:], ALU.is_gt))
                then(dve.tensor_tensor(low[:], low[:], over[:], ALU.subtract))
                then(dve.tensor_scalar(low[:], low[:], float(H - 1), None, ALU.min))
                then(dve.tensor_tensor(frac[:, 1], pos[:], low[:], ALU.subtract))
                then(dve.tensor_scalar(frac[:, 0], frac[:, 1], -1.0, 1.0, ALU.mult, ALU.add))
                for cx in range(2):
                    for cy in range(2):
                        last = dve.tensor_tensor(wgt[:, k, :, cx, cy], frac[:, cx, 1, :], frac[:, cy, 0, :], ALU.mult)
                last.then_inc(link, 1)
                n[0] += 1
                then(dve.tensor_scalar(at[:], low[:, 1, :], float(COL_STEP), base_i[:, DS(b, 1)], ALU.mult, ALU.add))
                then(dve.scalar_tensor_tensor(out=at[:], in0=low[:, 0, :], scalar=float(ROW_STEP), in1=at[:],
                                              op0=ALU.mult, op1=ALU.add))
                then(dve.tensor_copy(idx[:, k, :], at[:]))
                dve.sem_inc(idx_made, 1)

            def taps(t, k):
                for m in range(TAPS):
                    for c in range(1, 4):
                        for r in range(TILE):
                            q = (TAPS * k + m) * TILE + r
                            n = m * TILE + r
                            base = PRIME + 3 * TILE * (TAPS * t + m)
                            if c == 1:
                                dve.wait_ge(mixed0, (TAPS * t + m) * TILE + r + 1)
                            else:
                                dve.wait_ge(mixed, base + (c - 2) * TILE + r + 1)
                            dve.scalar_tensor_tensor(out=samp[:, q % SR, :], in0=patch[:, n % GR, c * C:(c + 1) * C],
                                                     scalar=wgt[:, k, r * TAPS + m, c // 2, c % 2:c % 2 + 1], in1=samp[:, q % SR, :],
                                                     op0=ALU.mult, op1=ALU.add).then_inc(mixed, 1)
                dve.wait_ge(tap_done, t * TAPS + TAPS + 2)
                dve.wait_ge(x2_loaded[k], 16 * (t // 2 + 1))
                dve.scalar_tensor_tensor(out=x2[:, k, :], in0=out_ps[:, k, :], scalar=tap_b[:, 0:1], in1=x2[:, k, :],
                                         op0=ALU.add, op1=ALU.add).then_inc(out_taken, 1)

            sweep(dve, front, taps)

        @block.gpsimd
        def _(pool):
            pool.iota(base_y[:].rearrange("p j m -> p (j m)"), [[TILE, IMG_TILES], [1, TILE], [1, 3], [0, 3]], base=-1,
                      channel_multiplier=0, allow_small_or_imprecise_dtypes=True).then_inc(tables, 1)
            pool.iota(base_x[:], [[0, TILE], [0, 3], [1, 3]], base=-1, channel_multiplier=1,
                      allow_small_or_imprecise_dtypes=True).then_inc(tables, 1)
            for b in range(B):
                pool.memset(base_i[:, b:b + 1], float(b * PH * ROW_STEP + ROW_STEP + COL_STEP)).then_inc(tables, 1)

            def front(t, k):
                pass

            def taps(t, k):
                pool.wait_ge(idx_made, t + 1)
                for n in range(NP):
                    m, r = n // TILE, n % TILE
                    pool.wait_ge(mixed, 3 * TILE * (TAPS * t + m) + 2 * TILE + r + 1)
                    pool.sem_inc(pool_passed, 1)
                    pool.indirect_dma_start(out=patch[:, n % GR, :], out_offset=None, in_=io["patch_rows"],
                                            in_offset=bass.IndirectOffsetOnAxis(ap=idx[:, k, r * TAPS + m:r * TAPS + m + 1], axis=1)
                                            ).then_inc(gathered[n % GR], 16)

            sweep(pool, front, taps)


EX = 64
TOP = 8
PAIRS = B // 2
HID = 512
HC = HID // 128


def pick_phase(nc, sems, consts, io, pooled_t):
    ident = consts["ident"]
    with Scope(nc, sems) as s:
        logit = s.sb("pk_logit", [128, T])
        rest = s.sb("pk_rest", [128, T])
        top = s.sb("pk_top", [128, TOP])
        place = s.sb("pk_place", [128, TOP], U32)
        place_f = s.sb("pk_place_f", [128, TOP])
        place_i = s.sb("pk_place_i", [128, PAIRS, TOP], U32)
        row0 = s.sb("pk_row0", [128, PAIRS])
        nmax, total, inv = s.sb("pk_nmax", [128, 1]), s.sb("pk_total", [128, 1]), s.sb("pk_inv", [128, 1])
        prob = s.sb("pk_prob", [128, PAIRS, TOP])
        token = s.sb("pk_token", [128, TOP, C])
        pooled = s.sb("pk_pooled", [128, C])
        turn = s.ps("pk_turn", [128, BANK])
        loaded, rows_set, link = s.sem("pk_loaded"), s.sem("pk_rows_set"), s.sem("pk_link")
        exp_ready, exp_made, stored = s.sem("pk_exp_ready"), s.sem("pk_exp_made"), s.sem("pk_stored")
        idx_made, gathered, pooled_made, turned = (s.sem(f"pk_{n}") for n in ("idx_made", "gathered", "pooled_made", "turned"))
        picked_made, turn_taken = s.sem("pk_picked_made"), s.sem("pk_turn_taken")
        block = s.ctx.enter_context(nc.Block())

        @block.sync
        def _(sp):
            for p in range(PAIRS):
                if p:
                    sp.wait_ge(stored, 16 * p)
                sp.dma_start(logit[:], io["logits_p"][p]).then_inc(loaded, 16)
                sp.wait_ge(picked_made, p + 1)
                sp.dma_start(io["picked"][p], logit[:]).then_inc(stored, 16)
            sp.wait_ge(stored, 16 * PAIRS)

        @block.gpsimd
        def _(pool):
            for p in range(PAIRS):
                for h in range(2):
                    pool.memset(row0[64 * h:64 * h + 64, p:p + 1], float((2 * p + h) * T)).then_inc(rows_set, 1)
            for p in range(PAIRS):
                pool.wait_ge(idx_made, p + 1)
                if p:
                    pool.wait_ge(pooled_made, p)
                for k in range(TOP):
                    pool.indirect_dma_start(out=token[:, k, :], out_offset=None, in_=io["token_rows"],
                                            in_offset=bass.IndirectOffsetOnAxis(ap=place_i[:, p, k:k + 1], axis=0)
                                            ).then_inc(gathered, 16)

        @block.scalar
        def _(act):
            for p in range(PAIRS):
                act.wait_ge(exp_ready, p + 1)
                act.activation(logit[:], logit[:], ACT.Exp, bias=nmax[:], accum_out=total[:]).then_inc(exp_made, 1)
                act.activation(prob[:, p, :], top[:], ACT.Exp, bias=nmax[:]).then_inc(exp_made, 1)

        @block.tensor
        def _(pe):
            for p in range(PAIRS):
                pe.wait_ge(pooled_made, p + 1)
                if p:
                    pe.wait_ge(turn_taken, p)
                pe.transpose(turn[:, 0:C], pooled[:], ident[:]).then_inc(turned, 1)

        @block.vector
        def _(dve):
            n = [0]

            def then(ins):
                n[0] += 1
                ins.then_inc(link, 1)
                dve.wait_ge(link, n[0])

            dve.wait_ge(rows_set, 2 * PAIRS)
            for p in range(PAIRS):
                dve.wait_ge(loaded, 16 * (p + 1))
                then(dve.max(out=top[:], in_=logit[:]))
                then(dve.max_index(out=place[:], in_max=top[:], in_values=logit[:]))
                then(dve.match_replace(out=rest[:], in_to_replace=top[:], in_values=logit[:], imm_value=-3.0e38))
                then(dve.tensor_tensor(rest[:], rest[:], logit[:], ALU.not_equal))
                then(dve.tensor_scalar(nmax[:], top[:, 0:1], -1.0, None, ALU.mult))
                then(dve.tensor_copy(place_f[:], place[:]))
                then(dve.tensor_scalar(place_f[:], place_f[:], row0[:, p:p + 1], None, ALU.add))
                then(dve.tensor_copy(place_i[:, p, :], place_f[:]))
                dve.sem_inc(exp_ready, 1)
                dve.sem_inc(idx_made, 1)
                dve.wait_ge(exp_made, 2 * p + 2)
                then(dve.reciprocal(inv[:], total[:]))
                then(dve.tensor_scalar(prob[:, p, :], prob[:, p, :], inv[:, 0:1], None, ALU.mult))
                then(dve.scalar_tensor_tensor(out=logit[:], in0=logit[:], scalar=inv[:, 0:1], in1=rest[:],
                                              op0=ALU.mult, op1=ALU.mult))
                dve.sem_inc(picked_made, 1)
                dve.wait_ge(gathered, 16 * TOP * (p + 1))
                if p:
                    dve.wait_ge(turned, p)
                then(dve.tensor_scalar(pooled[:], token[:, 0, :], prob[:, p, 0:1], None, ALU.mult))
                for k in range(1, TOP):
                    then(dve.scalar_tensor_tensor(out=pooled[:], in0=token[:, k, :], scalar=prob[:, p, k:k + 1],
                                                  in1=pooled[:], op0=ALU.mult, op1=ALU.add))
                dve.sem_inc(pooled_made, 1)
                dve.wait_ge(turned, p + 1)
                dve.tensor_copy(pooled_t[:, p, :], turn[:, 0:C]).then_inc(turn_taken, 1)


def expert_phase(nc, sems, consts, io, pooled_t):
    ident = consts["ident"]
    NW = 4
    with Scope(nc, sems) as s:
        w1, w2 = s.sb("ex_w1", [128, NW, HID]), s.sb("ex_w2", [128, NW, HC, C])
        b1, b2 = s.sb("ex_b1", [128, EX * HC]), s.sb("ex_b2", [128, EX])
        hid = s.sb("ex_hid", [128, 2, HC, B])
        act_h = s.sb("ex_act_h", [128, 2, HC, B])
        out_c = s.sb("ex_out_c", [128, B, EX])
        out_t = s.sb("ex_out_t", [128, PAIRS, C])
        pick = s.sb("ex_pick", [128, F, COLS])
        x3 = s.sb("ex_x3", [128, F, 2, COLS])
        hid_ps, o_ps = s.ps("ex_hid_ps", [128, 2, BANK]), s.ps("ex_o_ps", [128, 2, BANK])
        sum_ps = s.ps("ex_sum_ps", [128, 2 * F, BANK])
        b_in = s.sem("ex_b_in")
        w_loaded = [s.sem(f"ex_w_loaded{k}") for k in range(NW)]
        hid_made, hid_taken, gelu_made = s.sem("ex_hid_made"), s.sem("ex_hid_taken"), s.sem("ex_gelu_made")
        o_made, o_taken = s.sem("ex_o_made"), s.sem("ex_o_taken")
        turned, turn_taken = s.sem("ex_turned"), s.sem("ex_turn_taken")
        t_loaded = [s.sem(f"ex_t_loaded{k}") for k in range(F)]
        sum_made, sum_taken = s.sem("ex_sum_made"), s.sem("ex_sum_taken")
        stored = [s.sem(f"ex_stored{k}") for k in range(F)]
        pooled = pooled_t[:].rearrange("d p (h e) -> d (p h) e", e=EX)
        block = s.ctx.enter_context(nc.Block())

        @block.sync
        def _(sp):
            sp.dma_start(b1[:], io["b1"]).then_inc(b_in, 16)
            sp.dma_start(b2[:], io["b2"]).then_inc(b_in, 16)
            with sp.Fori(0, EX // NW) as i:
                for k in range(NW):
                    e = i * NW + k
                    sp.wait_ge(o_taken, e + 1)
                    sp.dma_start(w1[:, k, :], io["w1"][DS(e, 1), 0:C, :].rearrange("o d h -> (o d) h")).then_inc(w_loaded[k], 16)
                    sp.dma_start(w2[:, k, :, :], io["w2"][DS(e, 1), 0:HID, :].rearrange("o (p c) f -> (o p) c f", c=HC)
                                 ).then_inc(w_loaded[k], 16)
            for p in range(PAIRS):
                with sp.Fori(0, IMG_TILES // F) as j:
                    for k in range(F):
                        t = p * IMG_TILES + j * F + k
                        n = p * (IMG_TILES // F) + j
                        sp.wait_ge(sum_taken, t + 1)
                        sp.wait_ge(stored[k], 32 * (n + 1))
                        sp.dma_start(pick[:, k, :], io["picked"][p, :, DS((j * F + k) * COLS, COLS)]).then_inc(t_loaded[k], 16)
                        for h in range(2):
                            sp.dma_start(x3[:, k, h, :], io["x3"][2 * p + h, :, DS((j * F + k) * COLS, COLS)]
                                         ).then_inc(t_loaded[k], 16)
            for k in range(F):
                sp.wait_ge(stored[k], 32 * (PAIRS * IMG_TILES // F + 1))

        @block.tensor
        def _(pe):
            with pe.Fori(0, EX // NW) as i:
                for k in range(NW):
                    e = i * NW + k
                    pe.wait_ge(w_loaded[k], 32 * (i + 1))
                    pe.wait_ge(hid_taken, e + 1)
                    for c in range(HC):
                        last = pe.matmul(hid_ps[:, k % 2, c * B:(c + 1) * B], w1[:, k, c:HID:HC],
                                         pooled[:, :, DS(e, 1)].rearrange("d b o -> d (b o)"), start=True, stop=True)
                    last.then_inc(hid_made, 1)
                    pe.wait_ge(gelu_made, e + 1)
                    pe.wait_ge(o_taken, e + NW - 1)
                    for c in range(HC):
                        last = pe.matmul(o_ps[:, k % 2, 0:B], w2[:, k, c, :], act_h[:, k % 2, c, :],
                                         start=(c == 0), stop=(c == HC - 1))
                    last.then_inc(o_made, 1)
            pe.wait_ge(o_taken, EX + NW)
            for p in range(PAIRS):
                pe.transpose(o_ps[:, p, 0:C], out_c[:, 2 * p:2 * p + 2, :].rearrange("o b e -> o (b e)"), ident[:]).then_inc(turned, 1)
            pe.wait_ge(turn_taken, PAIRS)
            for p in range(PAIRS):
                with pe.Fori(0, IMG_TILES // F) as j:
                    for k in range(F):
                        t = p * IMG_TILES + j * F + k
                        pe.wait_ge(t_loaded[k], 48 * (p * (IMG_TILES // F) + j + 1))
                        pe.wait_ge(sum_taken, t + 1)
                        for h in range(2):
                            last = pe.matmul(sum_ps[:, 2 * k + h, :], out_t[64 * h:64 * h + 64, p, :],
                                             pick[64 * h:64 * h + 64, k, :], start=True, stop=True)
                        last.then_inc(sum_made, 1)

        @block.scalar
        def _(act):
            for k in range(F):
                act.sem_inc(stored[k], 32)
            with act.Fori(0, EX // 2) as i:
                for k in range(2):
                    e = i * 2 + k
                    act.wait_ge(hid_taken, e + 3)
                    act.activation(act_h[:, k, :, :], hid[:, k, :, :], ACT.Gelu).then_inc(gelu_made, 1)
            for p in range(PAIRS):
                with act.Fori(0, IMG_TILES // F) as j:
                    for k in range(F):
                        t = p * IMG_TILES + j * F + k
                        act.wait_ge(sum_taken, t + F + 1)
                        for h in range(2):
                            act.dma_start(io["out"][2 * p + h, :, DS((j * F + k) * COLS, COLS)], x3[:, k, h, :]
                                          ).then_inc(stored[k], 16)

        @block.vector
        def _(dve):
            dve.sem_inc(o_taken, NW)
            dve.sem_inc(hid_taken, 2)
            dve.sem_inc(sum_taken, F)
            dve.wait_ge(b_in, 32)
            with dve.Fori(0, EX // 2) as i:
                for k in range(2):
                    e = i * 2 + k
                    dve.wait_ge(hid_made, e + 1)
                    dve.tensor_tensor(hid[:, k, :, :], hid_ps[:, k, 0:HC * B].rearrange("p (c b) -> p c b", b=B),
                                      b1[:, DS(e * HC, HC)].unsqueeze(2).to_broadcast([128, HC, B]), ALU.add
                                      ).then_inc(hid_taken, 1)
                    dve.wait_ge(o_made, e + 1)
                    dve.tensor_scalar(out_c[:, :, DS(e, 1)].rearrange("o b x -> o (b x)"), o_ps[:, k, 0:B],
                                      b2[:, DS(e, 1)], None, ALU.add).then_inc(o_taken, 1)
            for p in range(PAIRS):
                dve.wait_ge(turned, p + 1)
                dve.tensor_copy(out_t[:, p, :], o_ps[:, p, 0:C]).then_inc(turn_taken, 1)
            for p in range(PAIRS):
                with dve.Fori(0, IMG_TILES // F) as j:
                    for k in range(F):
                        t = p * IMG_TILES + j * F + k
                        dve.wait_ge(sum_made, t + 1)
                        dve.tensor_tensor(x3[:, k], x3[:, k], sum_ps[:, 2 * k:2 * k + 2, :], ALU.add).then_inc(sum_taken, 1)


def network(nc, sems, io):
    with ExitStack() as ctx:
        def sb(name, shape):
            return ctx.enter_context(nc.sbuf_tensor(name, shape, F32))

        def dram(name, shape):
            return nc.dram_tensor(name, shape, F32, kind="Internal").ap()

        consts = {"ident": sb("ident", [128, 128]), "mean_mat": sb("mean_mat", [128, 128]),
                  "center_mat": sb("center_mat", [128, 128]), "coef_qk": sb("coef_qk", [128, 2]),
                  "coef_v": sb("coef_v", [128, 2])}
        coef_sim, coef_att, coef_emb, coef_f = (sb("coef_sim", [128, 4 * G]), sb("coef_att", [128, 2]),
                                                sb("coef_emb", [128, 2]), sb("coef_f", [128, 2]))
        pooled_t = sb("pooled_t", [128, PAIRS, 2 * EX])
        qk = dram("d_qk", (2 * QC * G, N * W))
        v = dram("d_v", (W, N * C))
        attn, emb = dram("d_attn", (C, N * W)), dram("d_emb", (BLOCKS, HB, VC * W))
        x1, xn1, x2, x3 = (dram(f"d_{n}", (B, C, T)) for n in ("x1", "xn1", "x2", "x3"))
        rows = dram("d_rows", (B, C, H + 2, W))
        patches = dram("d_patches", (B, PH, PW, 2, C))
        logits, tokens = dram("d_logits", (B, EX, T)), dram("d_tokens", (B, H, W, C))
        picked = dram("d_picked", (PAIRS, 2 * EX, T))
        x = io["x"].rearrange("b c h w -> b c (h w)")

        setup_phase(nc, sems, consts["ident"], consts["mean_mat"], consts["center_mat"])
        norm_phase(nc, sems, consts, "qkv_stats", {"src": x, "w_qk": io["w_qk"], "w_v": io["w_v"], "gb": io["gb_qkv"],
                                                   "coef": [consts["coef_qk"], consts["coef_v"]]}, LNC_EPS)
        norm_phase(nc, sems, consts, "qkv", {"src": x, "w_qk": io["w_qk"], "w_v": io["w_v"], "qk_by_channel": qk, "v": v}, LNC_EPS)
        att_io = {"qk": qk.rearrange("(s c g) f -> s c g f", s=2, c=QC), "v": v, "rel_q": io["rel_rev"][0:QC],
                  "rel_k": io["rel_rev"][QC:2 * QC], "rel_v": io["rel_v"], "sim_gamma": io["sim_gamma"],
                  "sim_beta": io["sim_beta"], "attn": attn, "emb": emb}
        attention_phase(nc, sems, consts["ident"], consts["mean_mat"], att_io, True, coef_sim)
        attention_phase(nc, sems, consts["ident"], consts["mean_mat"], att_io, False, coef_sim)
        mix_io = {"attn": attn, "emb": emb, "x": x, "x1": x1, "gb_out": io["gb_out"]}
        mix_phase(nc, sems, mix_io, coef_att, coef_emb, True)
        mix_phase(nc, sems, mix_io, coef_att, coef_emb, False)
        norm_phase(nc, sems, consts, "ffn", {"src": x1, "xn": xn1, "w_f": io["w_f"], "gb": io["gb_f"], "coef": [coef_f]}, EPS)
        recurrence_phase(nc, sems, consts, {"xn": xn1, "x1": x1, "x2": x2, "w_f_nat": io["w_f_nat"], "v_t": io["v_t"]}, coef_f)
        norm_phase(nc, sems, consts, "image", {"src": x2, "rows": rows, "patches": patches}, LNC_EPS)
        deform_phase(nc, sems, consts, {"rows": rows, "x2": x2, "x3": x3, "off_w": io["off_w"], "off_b": io["off_b"],
                                        "tap_w": io["tap_w"], "tap_b": io["tap_b"],
                                        "patch_rows": patches.rearrange("b y x h c -> (b y x h c)").rearrange("(n f) -> n f", f=PATCH)})
        norm_phase(nc, sems, consts, "gate", {"src": x3, "w_g": io["w_g"], "b_g": io["b_g"], "logits": logits, "tokens": tokens}, EPS)
        pick_phase(nc, sems, consts, {"logits_p": logits.rearrange("(p h) e t -> p (h e) t", h=2), "picked": picked,
                                      "token_rows": tokens.rearrange("b h w c -> (b h w) c")}, pooled_t)
        expert_phase(nc, sems, consts, {"w1": io["w1"], "w2": io["w2"], "b1": io["b1"], "b2": io["b2"], "picked": picked,
                                        "x3": x3, "out": io["out"].rearrange("b c h w -> b c (h w)")}, pooled_t)


def kernel(**inputs):
    import numpy as np
    import concourse.bacc as bacc
    from concourse.bass_utils import run_bass_kernel_spmd

    a = {n: np.asarray(v) for n, v in inputs.items()}

    def qk_rows(m):
        m = m.reshape((G, 4, QC) + m.shape[1:])[:, :2]
        return np.moveaxis(m, 0, 2).reshape((2 * QC * G,) + m.shape[3:])

    def v_rows(m):
        return m.reshape((G, 2, VC) + m.shape[1:])[:, 1].reshape((C,) + m.shape[1:])

    qg, qb = a["L0_conv_bn_qkv_gamma"], a["L0_conv_bn_qkv_beta"]
    og, ob = (a[f"L0_conv_bn_out_{n}"].reshape(C, 2) for n in ("gamma", "beta"))
    wq = a["L0_conv_conv_w"]
    rel = a["L0_conv_rel_emb"]
    w1, w2 = a["L1_ffn_weight1"], a["L1_ffn_weight2"]
    arrays = {
        "x": a["x"],
        "w_qk": qk_rows(wq).T, "w_v": v_rows(wq).T,
        "gb_qkv": np.stack([np.stack([qk_rows(m), v_rows(m)], -1) for m in (qg, qb)], -1),
        "rel_rev": rel[:, ::-1], "rel_v": rel[2 * QC:, ::-1].T,
        "sim_gamma": a["L0_conv_bn_sim_gamma"], "sim_beta": a["L0_conv_bn_sim_beta"],
        "gb_out": np.stack([og, ob], -1),
        "w_f": a["L0_ffn_W"].T, "w_f_nat": a["L0_ffn_W"], "v_t": a["L0_ffn_V"].T,
        "gb_f": np.stack([a["L0_ffn_gamma"], a["L0_ffn_beta"]], -1)[:, None],
        "off_w": a["L1_conv_offset_w"].reshape(2 * TAPS, C, TAPS).transpose(1, 2, 0), "off_b": a["L1_conv_offset_b"][:, None],
        "tap_w": a["L1_conv_conv_w"].reshape(C, C, TAPS).transpose(1, 2, 0), "tap_b": a["L1_conv_conv_b"][:, None],
        "w_g": a["L1_ffn_gate_w"].T, "b_g": a["L1_ffn_gate_b"][:, None],
        "w1": w1, "w2": w2,
        "b1": w1[:, C, :].reshape(EX, 128, HC).transpose(1, 0, 2).reshape(128, EX * HC), "b2": w2[:, HID, :].T,
    }
    arrays = {n: np.ascontiguousarray(v) for n, v in arrays.items()}
    nc = bacc.Bacc("TRN2", target_bir_lowering=False, num_devices=1)
    io = {n: nc.dram_tensor(f"in_{n}", v.shape, mybir.dt.from_np(v.dtype), kind="ExternalInput").ap() for n, v in arrays.items()}
    io["out"] = nc.dram_tensor("out_x", (B, C, H, W), F32, kind="ExternalOutput").ap()
    with ExitStack() as sems:
        network(nc, sems, io)
    r = run_bass_kernel_spmd(nc, [{f"in_{n}": v for n, v in arrays.items()}], core_ids=[0])
    return r.results[0]["out_x"]
```

```python
from contextlib import ExitStack, contextmanager

import concourse.bass as bass
from concourse import mybir

F32 = mybir.dt.float32
I32 = mybir.dt.int32
U32 = mybir.dt.uint32
BF16 = mybir.dt.bfloat16
ALU = mybir.AluOpType
ACT = mybir.ActivationFunctionType
AX = mybir.AxisListType
DS = bass.ds

B, C, H, W = 4, 128, 128, 128
N = B * H
T = H * W
G = 8
QC, VC = 8, 16
REL = 2 * W - 1
EPS = 1e-5
LNC_EPS = 1e-6
BANK = 512

RB = 8
HB = RB * G
BLOCKS = N // RB
PACK = BANK // W
HG = HB // PACK

PARTS = 3
PART_PAIRS = [(a, b) for a in range(PARTS) for b in range(PARTS) if a + b < 2 * PARTS - 2]
QK_ROWS = 2 * len(PART_PAIRS) * QC


class Scope:

    def __init__(self, nc, sems):
        self.nc, self.own, self.names, self.ctx = nc, ExitStack(), [], ExitStack()

    def __enter__(self):
        return self

    def __exit__(self, kind, *a):
        self.ctx.close()
        if kind is None:
            with self.nc.Block() as block:
                @block.gpsimd
                def _(pool):
                    for n in self.names:
                        pool.sem_clear(n)
        self.own.close()

    def sb(self, name, shape, dt=F32):
        return self.ctx.enter_context(self.nc.sbuf_tensor(name, shape, dt))

    def ps(self, name, shape, dt=F32):
        return self.ctx.enter_context(self.nc.psum_tensor(name, shape, dt))

    def sem(self, name):
        self.names.append(self.own.enter_context(self.nc.semaphore(name)))
        return self.names[-1]


def setup_phase(nc, sems, ident, mean_mat, center_mat):
    with Scope(nc, sems) as s:
        made = s.sem("set_made")
        with nc.Block() as block:
            @block.gpsimd
            def _(pool):
                pool.memset(ident[:], 0.0).then_inc(made, 1)
                pool.memset(mean_mat[:], 1.0 / C).then_inc(made, 1)
                pool.wait_ge(made, 2)
                pool.affine_select(out=ident[:], in_=ident[:], compare_op=ALU.not_equal, fill=1.0, base=0,
                                   pattern=[[-1, 128]], channel_multiplier=1).then_inc(made, 1)
                pool.wait_ge(made, 3)
                pool.tensor_tensor(center_mat[:], ident[:], mean_mat[:], ALU.subtract).then_inc(made, 1)
                pool.wait_ge(made, 4)


def embedding_parts_phase(nc, sems, rel_rev, rel_parts):
    with Scope(nc, sems) as s:
        whole, rest = s.sb("ep_whole", [2 * QC, REL]), s.sb("ep_rest", [2 * QC, REL])
        part = s.sb("ep_part", [2 * QC, PARTS, REL], BF16)
        loaded, made, stored = s.sem("ep_loaded"), s.sem("ep_made"), s.sem("ep_stored")
        block = s.ctx.enter_context(nc.Block())

        @block.sync
        def _(sp):
            sp.dma_start(whole[:], rel_rev).then_inc(loaded, 16)
            sp.wait_ge(made, 2 * PARTS - 1)
            for x in range(2):
                sp.dma_start(rel_parts[x].rearrange("a c f -> c a f"), part[x * QC:(x + 1) * QC, :, :]).then_inc(stored, 16)
            sp.wait_ge(stored, 32)

        @block.vector
        def _(dve):
            dve.wait_ge(loaded, 16)
            left = whole
            for a in range(PARTS):
                dve.tensor_copy(part[:, a, :], left[:]).then_inc(made, 1)
                dve.wait_ge(made, 2 * a + 1)
                if a < PARTS - 1:
                    dve.tensor_tensor(rest[:], left[:], part[:, a, :], ALU.subtract).then_inc(made, 1)
                    dve.wait_ge(made, 2 * a + 2)
                    left = rest


def similarity_order():
    return [((2 * q + e) * 2 + half, 2 * q + e, half, q, e) for e in range(2) for half in range(2) for q in range(4)]


def attention_phase(nc, sems, ident, mean_mat, io, stats_only, coef):
    tag = "sa" if stats_only else "at"
    if stats_only:
        ring = {st: {"a": (0, 4), "d": (4, 2)} for st in "AB"}
    else:
        ring = {"A": {"a": (0, 4), "d": (4, 4)}, "B": {"a": (0, 4), "d": (4, 4)}, "P": {"a": (0, 1), "d": (1, 1)}}
    Q0, NQ, V0 = (6, 2, None) if stats_only else (2, 4, 6)
    LAG, AVLAG, SLOTS = 3, 6, 6
    place, count = {}, {"a": 0, "d": 0}
    for job in [("A", k) for k in range(32)] + [("B", k) for k in range(32)] + [("P", k) for k in range(0 if stats_only else HG)]:
        e = "a" if job[0] == "A" and (stats_only or job[1] % 16 == 15) else "ad"[job[1] % 2]
        place[job] = (e, count[e])
        count[e] += 1
    CA, CD = count["a"], count["d"]
    done = {e: {st: sum(1 for j, (o, n) in place.items() if o == e and j[0] <= st) for st in "ABP"} for e in "ad"}
    first = {e: {"A": 0, "B": done[e]["A"], "P": done[e]["B"]} for e in "ad"}
    with Scope(nc, sems) as s:
        qk_in = s.sb(f"{tag}_qk_in", [QK_ROWS, 2, HB, W], BF16)
        rel = s.sb(f"{tag}_rel", [QK_ROWS, REL], BF16)
        span_t = s.sb(f"{tag}_span_t", [128, 2 * HB, W])
        span = s.sb(f"{tag}_span", [128, 2 * HB, W])
        banks = s.ps(f"{tag}_banks", [128, 8, BANK])
        rel_in, cleared = s.sem(f"{tag}_rel_in"), s.sem(f"{tag}_cleared")
        qk_loaded, loads_passed = s.sem(f"{tag}_qk_loaded"), s.sem(f"{tag}_loads_passed")
        qk_spent = s.sem(f"{tag}_qk_spent")
        filled = {"a": s.sem(f"{tag}_filled_a"), "d": s.sem(f"{tag}_filled_d")}
        emptied = {"a": s.sem(f"{tag}_emptied_a"), "d": s.sem(f"{tag}_emptied_d")}
        sim_filled, sim_emptied = s.sem(f"{tag}_sim_filled"), s.sem(f"{tag}_sim_emptied")
        if stats_only:
            bn = s.sb("sa_bn", [128, 3 * G, 2, 6])
            agg = s.sb("sa_agg", [128, 3 * G, 2])
            hist = s.sb("sa_hist", [128, BLOCKS, 3 * G * 2])
            span_seen = s.sem("sa_span_seen")
            step = s.sem("sa_step")
        else:
            pt = span_t[:, 0:HB, :]
            sim = s.sb("at_sim", [128, SLOTS, BANK])
            diag = s.sb("at_diag", [128, 2, G, W])
            top, nmax, den, inv = (s.sb(f"at_{n}", [128, SLOTS, PACK]) for n in ("top", "nmax", "den", "inv"))
            v_in = s.sb("at_v_in", [128, RB, C])
            rel_v = s.sb("at_rel_v", [128, W * VC + VC])
            parity = s.sb("at_parity", [128, 2])
            attn_c = s.sb("at_attn_c", [128, RB, W])
            emb_c = s.sb("at_emb_c", [128, HB, W // 4])
            rel_v_in, v_loaded, v_spent = s.sem("at_rel_v_in"), s.sem("at_v_loaded"), s.sem("at_v_spent")
            diag_made, top_made, max_made = (s.sem(f"at_{n}") for n in ("diag_made", "top_made", "max_made"))
            exp_made, inv_made, prob_made = s.sem("at_exp_made"), s.sem("at_inv_made"), s.sem("at_prob_made")
            av_filled = [s.sem(f"at_av_filled{q}") for q in range(4)]
            av_even, av_odd = s.sem("at_av_even"), s.sem("at_av_odd")
            em_filled = {e: s.sem(f"at_em_filled_{e}") for e in "ad"}
            em_emptied = {e: s.sem(f"at_em_emptied_{e}") for e in "ad"}
            attn_stored, emb_stored = s.sem("at_attn_stored"), s.sem("at_emb_stored")
            padded, parity_in = s.sem("at_padded"), s.sem("at_parity_in")
        order = similarity_order()

        def value_columns(p):
            at = (31 - p) // 2 * 128 + (31 - p) % 2 * VC
            return slice(at, at + 128)

        def bank_of(job):
            e, n = place[job]
            start, size = ring[job[0]][e]
            return banks[:, start + (n - first[e][job[0]]) % size, :], e, n

        def span_head(k):
            return (HB if k % 2 == 0 else 0) + k // 2 * PACK

        def total(e):
            return CA if e == "a" else CD

        def evacuate(eng, copy, job, blk):
            bank, e, n = bank_of(job)
            st, k = job
            eng.wait_ge(filled[e], blk * total(e) + n + 1)
            if st == "A":
                out, src = span_t[:, :, 4 * k:4 * k + 4], bank.rearrange("p (i h) -> p h i", i=4)
            elif st == "B":
                if stats_only and k < 2:
                    eng.wait_ge(span_seen, blk + 1)
                h0 = span_head(k)
                out, src = span[:, h0:h0 + PACK, :], bank.rearrange("p (h j) -> p h j", h=PACK)
                if h0 < HB and not stats_only:
                    g = h0 // RB
                    eng.scalar_tensor_tensor(out=out, in0=src, scalar=coef[:, g:g + 1],
                                             in1=diag[:, 1, g:g + 1, :].to_broadcast([128, PACK, W]),
                                             op0=ALU.mult, op1=ALU.add).then_inc(emptied[e], 1)
                    return
            else:
                at = order[k][0]
                out, src = pt[:, at * PACK:(at + 1) * PACK, :], bank.rearrange("p (h i) -> p h i", h=PACK)
            copy(out, src).then_inc(emptied[e], 1)

        def copied(eng, st, blk):
            for e in "ad":
                if done[e][st]:
                    eng.wait_ge(emptied[e], blk * total(e) + done[e][st])

        block_ctx = ExitStack()
        block = block_ctx.enter_context(nc.Block())

        @block.sync
        def _(sp):
            for x in range(2):
                for m, (_, b) in enumerate(PART_PAIRS):
                    sp.dma_start(rel[x * QK_ROWS // 2 + m * QC:x * QK_ROWS // 2 + (m + 1) * QC, :], io["rel_parts"][x, b]
                                 ).then_inc(rel_in, 16)
            if not stats_only:
                for q in range(4):
                    sp.dma_start(rel_v[:, 0:W * VC].rearrange("j (r q f) -> j r q f", r=16, q=4)[:, :, q, :],
                                 bass.AP(io["rel_v"].tensor, 32 * q * VC, [[VC, 128], [2 * VC, 16], [1, 2 * VC]])
                                 ).then_inc(rel_v_in, 16)
                sp.dma_start(parity[:], io["parity"]).then_inc(parity_in, 16)
            sp.wait_ge(cleared, 1)

            def load(blk):
                sp.wait_ge(qk_spent, blk + 1)
                sp.sem_inc(loads_passed, 1)
                for x in range(2):
                    for m, (a, _) in enumerate(PART_PAIRS):
                        r = x * QK_ROWS // 2 + m * QC
                        sp.dma_start(qk_in[r:r + QC, x, :, :].rearrange("c (g n) i -> c g (n i)", g=G),
                                     io["qk_parts"][a, x][:, :, DS(blk * (RB * W), RB * W)]).then_inc(qk_loaded, 16)
                if not stats_only:
                    sp.wait_ge(v_spent, blk + 1)
                    sp.sem_inc(loads_passed, 1)
                    sp.dma_start(v_in[:].rearrange("p n c -> p (n c)"),
                                 io["v"][:, DS(blk * (RB * C), RB * C)]).then_inc(v_loaded, 16)

            def store(blk):
                if stats_only:
                    return
                sp.wait_ge(av_odd, blk * 2 + 4)
                sp.sem_inc(loads_passed, 1)
                sp.dma_start(io["attn"][:, DS(blk * (RB * W), RB * W)],
                             attn_c[:].rearrange("p n i -> p (n i)")).then_inc(attn_stored, 16)
                sp.wait_ge(em_emptied["a"], blk * 4 + 8)
                sp.wait_ge(em_emptied["d"], blk * 4 + 8)
                sp.sem_inc(loads_passed, 1)
                for q in range(4):
                    i0 = 32 * (3 - q)
                    sp.dma_start(io["emb"][DS(blk, 1)].rearrange("o c h i -> (o c) h i")[:, :, i0:i0 + 32],
                                 emb_c[32 * q:32 * q + VC, :, :]).then_inc(emb_stored, 16)

            if not stats_only:
                sp.sem_inc(attn_stored, 16)
                sp.sem_inc(emb_stored, 64)
            load(0)
            with sp.Fori(1, BLOCKS) as blk:
                load(blk)
                store(blk - 1)
            store(BLOCKS - 1)
            if not stats_only:
                sp.wait_ge(attn_stored, 16 * BLOCKS + 16)
                sp.wait_ge(emb_stored, 64 * BLOCKS + 64)

        @block.tensor
        def _(pe):
            pe.sem_inc(qk_spent, 1)
            if not stats_only:
                pe.sem_inc(v_spent, 1)
                pe.wait_ge(rel_v_in, 64)
                pe.wait_ge(padded, 1)
                pe.wait_ge(diag_made, 2 * G)
            pe.wait_ge(rel_in, 32 * len(PART_PAIRS))

            def fill(job, blk, parts):
                bank, e, n = bank_of(job)
                size = ring[job[0]][e][1]
                if n - first[e][job[0]] >= size:
                    pe.wait_ge(emptied[e], blk * total(e) + n + 1 - size)
                for last in parts(bank):
                    pass
                last.then_inc(filled[e], 1)

            with pe.Fori(0, BLOCKS) as blk:
                pe.wait_ge(qk_loaded, (blk + 1) * (32 * len(PART_PAIRS)))
                moving = qk_in[:].rearrange("c x h i -> c (x h) i")
                left = {} if stats_only else {0: ("a", 3), 1: ("a", 4), 4: ("d", 3), 5: ("d", 4)}
                for k in range(32):
                    if k in left:
                        e, n = left[k]
                        pe.wait_ge(em_emptied[e], blk * 4 + n)
                    fill(("A", k), blk, lambda bank: (
                        pe.matmul(bank[:, u * 2 * HB:(u + 1) * 2 * HB], rel[:, W - 1 - i:2 * W - 1 - i], moving[:, :, i],
                                  start=True, stop=True) for u, i in enumerate(range(4 * k, 4 * k + 4))))
                copied(pe, "A", blk)
                pe.sem_inc(qk_spent, 1)
                for k in range(32):
                    fill(("B", k), blk, lambda bank: (
                        pe.transpose(bank[:, h * W:(h + 1) * W], span_t[:, span_head(k) + h, :], ident[:]) for h in range(PACK)))
                copied(pe, "B", blk)

                def turn_probs(k):
                    pe.wait_ge(prob_made, blk * HG + k + 1)
                    fill(("P", k), blk, lambda bank: (
                        pe.transpose(bank[:, h * W:(h + 1) * W], sim[:, k % SLOTS, h * W:(h + 1) * W], ident[:])
                        for h in range(PACK)))

                def values(k):
                    at, g, half, q, e = order[k]
                    _, side, n = bank_of(("P", k))
                    m = k // 4
                    if k == 0:
                        pe.wait_ge(v_loaded, blk * 16 + 16)
                    if q == 0:
                        if e:
                            pe.wait_ge(av_even, blk * 2 + half + 3)
                        else:
                            pe.wait_ge(av_odd, blk * 2 + half + 1)
                    pe.wait_ge(emptied[side], blk * total(side) + n + 1)
                    for r in range(PACK):
                        row = half * PACK + r
                        last = pe.matmul(banks[32 * q:32 * q + 32, V0 + m % 2, r * W:(r + 1) * W],
                                         v_in[:, row, 32 * q:32 * q + 32], pt[:, at * PACK + r, :], start=True, stop=True)
                    last.then_inc(av_filled[q], 1)

                for k in range(HG):
                    if stats_only:
                        pe.wait_ge(sim_emptied, blk * HG + k + 1)
                    elif k >= NQ:
                        pe.wait_ge(exp_made, blk * HG + k - NQ + 1)
                    at, g = order[k][:2]
                    for h in range(PACK):
                        head = at * PACK + h
                        sum_of = banks[:, Q0 + k % NQ, h * W:(h + 1) * W]
                        last = pe.matmul(sum_of, span[:, head, :], span[:, HB + head, :], start=True, stop=stats_only)
                        if not stats_only:
                            last = pe.matmul(sum_of, span_t[:, head, :], diag[:, 0, g, :], start=False, stop=True)
                    last.then_inc(sim_filled, 1)
                    if not stats_only and k >= LAG:
                        turn_probs(k - LAG)
                    if not stats_only and k >= AVLAG:
                        values(k - AVLAG)
                if not stats_only:
                    for k in range(HG, HG + AVLAG):
                        if k < HG + LAG:
                            turn_probs(k - LAG)
                        values(k - AVLAG)
                    copied(pe, "P", blk)
                    pe.wait_ge(av_even, blk * 2 + 4)
                    pe.wait_ge(av_odd, blk * 2 + 4)
                    pe.sem_inc(v_spent, 1)
                    pt_i = pt.rearrange("j h (m p) -> j p m h", m=4)
                    for u in range(8):
                        e = "ad"[u % 2]
                        if u >= 4:
                            pe.wait_ge(em_emptied[e], blk * 4 + (u // 2) - 1 + 4)
                        for w in range(4):
                            p = u * 4 + w
                            b = 2 * (u % 4) + w // 2
                            last = pe.matmul(banks[:, b, (w % 2) * 4 * HB:(w % 2 + 1) * 4 * HB].rearrange("p (m h) -> p m h", m=4),
                                             rel_v[:, value_columns(p)],
                                             pt_i[:, p], start=True, stop=True)
                        last.then_inc(em_filled[e], 1)

        def take_embedded(eng, copy, e, blk):
            for u in range(8):
                if "ad"[u % 2] != e:
                    continue
                eng.wait_ge(em_filled[e], blk * 4 + u // 2 + 1)
                if u < 2:
                    eng.wait_ge(emb_stored, blk * 64 + 64)
                src = banks[:, 2 * (u % 4):2 * (u % 4) + 2, :].rearrange("p b (w m h) -> p m (b w) h", w=2, m=4)
                for q in range(4):
                    last = copy(emb_c[32 * q:32 * q + 32, :, 4 * u:4 * u + 4].rearrange("p h w -> p w h"),
                                src[32 * q:32 * q + 32, 3 - q])
                last.then_inc(em_emptied[e], 1)

        @block.scalar
        def _(act):
            if not stats_only:
                act.sem_inc(em_emptied["a"], 4)
                act.sem_inc(av_even, 2)
                act.wait_ge(parity_in, 16)
            with act.Fori(0, BLOCKS) as blk:
                for job, (e, _) in place.items():
                    if e == "a" and job[0] != "P":
                        evacuate(act, act.copy, job, blk)
                if not stats_only:
                    for k in range(HG + LAG + 1):
                        m = k - LAG - 1
                        if m >= 0 and place[("P", m)][0] == "a":
                            evacuate(act, act.copy, ("P", m), blk)
                        if k < HG:
                            act.wait_ge(max_made, blk * HG + k + 1)
                            if k >= SLOTS:
                                _, e, n = bank_of(("P", k - SLOTS))
                                act.wait_ge(filled[e], blk * total(e) + n + 1)
                            for h in range(PACK):
                                last = act.activation(sim[:, k % SLOTS, h * W:(h + 1) * W], banks[:, Q0 + k % NQ, h * W:(h + 1) * W],
                                                      ACT.Exp, bias=nmax[:, k % SLOTS, h:h + 1],
                                                      accum_out=den[:, k % SLOTS, h:h + 1])
                            last.then_inc(exp_made, 1)
                        if m in (6, 10):
                            half = (m - 6) // 4
                            if half == 0:
                                act.wait_ge(attn_stored, blk * 16 + 16)
                            for q in range(4):
                                act.wait_ge(av_filled[q], blk * 4 + half + 1)
                            act.activation(attn_c[:, half * PACK:(half + 1) * PACK, :].rearrange("p n i -> p (n i)"),
                                           banks[:, V0 + half, :], ACT.Copy, scale=parity[:, 0:1]).then_inc(av_even, 1)
                    take_embedded(act, act.copy, "a", blk)

        @block.vector
        def _(dve):
            if stats_only:
                dve.sem_inc(sim_emptied, NQ)
                dve.sem_inc(span_seen, 1)
            else:
                for x in range(2):
                    for g in range(G):
                        c = (x + 1) * G + g
                        dve.tensor_scalar(diag[:, x, g, :], ident[:], coef[:, c:c + 1], None, ALU.mult).then_inc(diag_made, 1)
                dve.wait_ge(diag_made, 2 * G)
                dve.sem_inc(em_emptied["d"], 4)
                dve.sem_inc(av_odd, 2)
                dve.wait_ge(parity_in, 16)
            with dve.Fori(0, BLOCKS) as blk:
                for job, (e, _) in place.items():
                    if e == "d" and job[0] != "P":
                        evacuate(dve, dve.tensor_copy, job, blk)
                if stats_only:
                    def span_stats(x, at):
                        dve.bn_stats(bn[:, (x + 1) * G + at // 2, at % 2, :],
                                     span[:, x * HB + at * PACK:x * HB + (at + 1) * PACK, :].rearrange("p h j -> p (h j)")
                                     ).then_inc(step, 1)

                    copied(dve, "B", blk)
                    for k in range(HG):
                        at, g, half = order[k][:3]
                        span_stats(0, k)
                        dve.wait_ge(sim_filled, blk * HG + k + 1)
                        dve.bn_stats(bn[:, g, half, :], banks[:, Q0 + k % NQ, :]).then_inc(sim_emptied, 1)
                    for at in range(HG):
                        span_stats(1, at)
                    dve.wait_ge(step, blk * (2 * HG + 3 * G + 1) + 2 * HG)
                    dve.wait_ge(sim_emptied, blk * HG + HG + NQ)
                    dve.sem_inc(span_seen, 1)
                    for t in range(3 * G):
                        dve.bn_aggr(agg[:, t, :], bn[:, t].rearrange("p a b -> p (a b)")).then_inc(step, 1)
                    dve.wait_ge(step, blk * (2 * HG + 3 * G + 1) + 2 * HG + 3 * G)
                    dve.tensor_copy(hist[:, DS(blk, 1), :].rearrange("p o f -> p (o f)"),
                                    agg[:].rearrange("p t f -> p (t f)")).then_inc(step, 1)
                    dve.wait_ge(step, blk * (2 * HG + 3 * G + 1) + 2 * HG + 3 * G + 1)
                else:
                    for k in range(HG + LAG + 1):
                        m = k - LAG - 1
                        if m >= 0 and place[("P", m)][0] == "d":
                            evacuate(dve, dve.tensor_copy, ("P", m), blk)
                        if k < HG:
                            g = order[k][1]
                            c = coef[:, 3 * G + g:3 * G + g + 1]
                            dve.wait_ge(sim_filled, blk * HG + k + 1)
                            dve.tensor_reduce(top[:, k % SLOTS, :], banks[:, Q0 + k % NQ, :].rearrange("p (h j) -> p h j", h=PACK),
                                              AX.X, ALU.max, negate=True).then_inc(top_made, 1)
                            dve.wait_ge(top_made, blk * HG + k + 1)
                            dve.tensor_scalar(nmax[:, k % SLOTS, :], top[:, k % SLOTS, :], c, c, ALU.subtract, ALU.add
                                              ).then_inc(max_made, 1)
                        if 1 <= k < HG + 1:
                            dve.wait_ge(exp_made, blk * HG + k)
                            dve.reciprocal(inv[:, (k - 1) % SLOTS, :], den[:, (k - 1) % SLOTS, :]).then_inc(inv_made, 1)
                    for half in range(2):
                        for q in range(4):
                            dve.wait_ge(av_filled[q], blk * 4 + 2 + half + 1)
                        dve.wait_ge(av_even, blk * 2 + 4)
                        dst = attn_c[:, half * PACK:(half + 1) * PACK, :].rearrange("p n i -> p (n i)")
                        dve.scalar_tensor_tensor(out=dst, in0=banks[:, V0 + half, :], scalar=parity[:, 1:2], in1=dst,
                                                 op0=ALU.mult, op1=ALU.add).then_inc(av_odd, 1)
                    take_embedded(dve, dve.tensor_copy, "d", blk)

        @block.gpsimd
        def _(pool):
            pool.memset(qk_in[:], 0.0).then_inc(cleared, 1)
            if stats_only:
                return
            pool.memset(rel_v[:, W * VC:], 0.0).then_inc(padded, 1)
            with pool.Fori(0, BLOCKS) as blk:
                for k in range(HG):
                    pool.wait_ge(inv_made, blk * HG + k + 1)
                    sv = sim[:, k % SLOTS, :].rearrange("p (h j) -> p h j", h=PACK)
                    pool.tensor_tensor(sv, sv, inv[:, k % SLOTS, :].unsqueeze(2).to_broadcast([128, PACK, W]),
                                       ALU.mult).then_inc(prob_made, 1)

        block_ctx.close()
        if stats_only:
            similarity_coefs(nc, s, hist, banks, mean_mat, io["sim_gamma"], io["sim_beta"], coef)


def similarity_coefs(nc, s, hist, acc, mean_mat, gamma, beta, coef):
    K = 3 * G
    gb = s.sb("sc_gb", [128, 2, K])
    m1 = s.sb("sc_m1", [128, K])
    dev = s.sb("sc_dev", [128, BLOCKS, K])
    gm = s.sb("sc_gm", [128, K])
    v1 = s.sb("sc_v1", [128, K])
    off = s.sb("sc_off", [128, K])
    gb_in, link, summed, rooted = s.sem("sc_gb_in"), s.sem("sc_link"), s.sem("sc_summed"), s.sem("sc_rooted")
    hv = hist[:].rearrange("p b (k t) -> p b k t", t=2)
    with nc.Block() as block:
        @block.sync
        def _(sp):
            sp.dma_start(gb[:, 0, :], gamma.partition_broadcast(128)).then_inc(gb_in, 16)
            sp.dma_start(gb[:, 1, :], beta.partition_broadcast(128)).then_inc(gb_in, 16)

        @block.tensor
        def _(pe):
            pe.wait_ge(link, 2)
            pe.matmul(acc[:, 0, 0:K], mean_mat[:], m1[:], start=True, stop=True).then_inc(summed, 1)
            pe.wait_ge(link, 8)
            pe.matmul(acc[:, 1, 0:K], mean_mat[:], v1[:], start=True, stop=True).then_inc(summed, 1)

        @block.scalar
        def _(act):
            act.wait_ge(link, 9)
            act.activation(v1[:], v1[:], ACT.Sqrt).then_inc(rooted, 1)

        @block.vector
        def _(dve):
            done = [0]

            def then(ins):
                done[0] += 1
                ins.then_inc(link, 1)
                dve.wait_ge(link, done[0])

            then(dve.tensor_reduce(m1[:], hv[:, :, :, 0].rearrange("p b k -> p k b"), AX.X, ALU.add))
            then(dve.tensor_scalar(m1[:], m1[:], 1.0 / BLOCKS, None, ALU.mult))
            dve.wait_ge(summed, 1)
            then(dve.tensor_copy(gm[:], acc[:, 0, 0:K]))
            then(dve.tensor_tensor(dev[:], hv[:, :, :, 0], gm[:].unsqueeze(1).to_broadcast([128, BLOCKS, K]), ALU.subtract))
            then(dve.tensor_tensor(dev[:], dev[:], dev[:], ALU.mult))
            then(dve.tensor_tensor(dev[:], dev[:], hv[:, :, :, 1], ALU.add))
            then(dve.tensor_reduce(v1[:], dev[:].rearrange("p b k -> p k b"), AX.X, ALU.add))
            then(dve.tensor_scalar(v1[:], v1[:], 1.0 / BLOCKS, None, ALU.mult))
            dve.wait_ge(summed, 2)
            then(dve.tensor_scalar(v1[:], acc[:, 1, 0:K], EPS, None, ALU.add))
            dve.wait_ge(rooted, 1)
            dve.wait_ge(gb_in, 32)
            then(dve.reciprocal(v1[:], v1[:]))
            then(dve.tensor_tensor(coef[:, 0:K], v1[:], gb[:, 0, :], ALU.mult))
            then(dve.tensor_tensor(off[:], coef[:, 0:K], gm[:], ALU.mult))
            then(dve.tensor_tensor(off[:], gb[:, 1, :], off[:], ALU.subtract))
            then(dve.tensor_reduce(coef[:, K:K + G], off[:].rearrange("p (k g) -> p g k", k=3), AX.X, ALU.add))


TILE = 4
COLS = TILE * W
TILES = N // TILE
IMG_TILES = H // TILE
PH, PW = H + 1, W + 2


def tile_of(x, b, j):
    return x[DS(b, 1), :, DS(j * COLS, COLS)].rearrange("o c f -> (o c) f")


SLOTS = 4
TOK_LAG, STORE_LAG = 3, 6
LEAD = 2


class Tile:

    def __init__(self, turn, k, lag):
        self.turn, self.slot = turn + (k - lag) // SLOTS, (k - lag) % SLOTS
        self.n = self.turn * SLOTS + self.slot
        self.bank = self.slot % 2
        self.exists = not isinstance(self.n, int) or 0 <= self.n < TILES


def turns(eng, step):
    for turn in range(LEAD):
        for k in range(SLOTS):
            step(turn, k)
    with eng.Fori(LEAD, TILES // SLOTS) as turn:
        for k in range(SLOTS):
            step(turn, k)
    for k in range(STORE_LAG):
        step(TILES // SLOTS, k)


def wait_for(eng, sem, count):
    if not isinstance(count, int) or count > 0:
        eng.wait_ge(sem, count)


def norm_phase(nc, sems, consts, kind, io, eps):
    ident, mean_mat, center_mat = consts["ident"], consts["mean_mat"], consts["center_mat"]
    p = kind
    with Scope(nc, sems) as s:
        x_in = s.sb(f"{p}_x_in", [128, SLOTS, COLS])
        moments = s.sb(f"{p}_moments", [128, SLOTS, TILE, 6])
        mean_var = s.sb(f"{p}_mean_var", [128, SLOTS, TILE, 2])
        std = s.sb(f"{p}_std", [128, SLOTS, TILE])
        rstd = s.sb(f"{p}_rstd", [128, SLOTS, TILE])
        tok = s.sb(f"{p}_tok", [128, SLOTS, COLS])
        xn = s.sb(f"{p}_xn", [128, SLOTS, COLS])
        eps_col = s.sb(f"{p}_eps", [128, 1])
        cent = s.ps(f"{p}_cent", [128, 2, BANK])
        back = s.ps(f"{p}_back", [128, 2, BANK])
        out_ps = s.ps(f"{p}_out_ps", [128, 4, BANK])
        eps_set, w_in = s.sem(f"{p}_eps_set"), s.sem(f"{p}_w_in")
        x_loaded = [s.sem(f"{p}_x_loaded{k}") for k in range(SLOTS)]
        cent_made, moments_made, var_made = s.sem(f"{p}_cent_made"), s.sem(f"{p}_moments_made"), s.sem(f"{p}_var_made")
        std_made, rstd_made, tok_made = s.sem(f"{p}_std_made"), s.sem(f"{p}_rstd_made"), s.sem(f"{p}_tok_made")
        back_made, xn_made, prod_made = s.sem(f"{p}_back_made"), s.sem(f"{p}_xn_made"), s.sem(f"{p}_prod_made")
        taken_a, taken_d = s.sem(f"{p}_taken_a"), s.sem(f"{p}_taken_d")
        stored = [s.sem(f"{p}_stored{k}") for k in range(SLOTS)]
        moments_passed = s.sem(f"{p}_moments_passed")
        stats = kind in ("qkv_stats", "ffn")
        products = kind != "image"
        if kind in ("qkv_stats", "qkv"):
            w_qk, w_v = s.sb(f"{p}_w_qk", [128, C]), s.sb(f"{p}_w_v", [128, C])
            weights = [(w_qk[:], io["w_qk"]), (w_v[:], io["w_v"])]
        elif kind == "ffn":
            w_f = s.sb("ffn_w", [128, C])
            weights = [(w_f[:], io["w_f"])]
        elif kind == "gate":
            w_g, b_g = s.sb("gate_w", [128, 64]), s.sb("gate_b", [64, 1])
            weights = [(w_g[:], io["w_g"]), (b_g[:], io["b_g"])]
        else:
            weights = []
        if stats:
            kinds = 2 if kind == "qkv_stats" else 1
            hist = s.sb(f"{p}_hist", [128, kinds, TILES, 6])
            mv = s.sb(f"{p}_mv", [128, kinds, 2])
            gb = s.sb(f"{p}_gb", [128, kinds, 2])
            weights += [(gb[:], io["gb"])]
        if kind == "qkv":
            coef_qk, coef_v = consts["coef_qk"], consts["coef_v"]
            diag = s.sb("qkv_diag", [128, 2, C])
            v_row = s.sb("qkv_v_row", [128, 2, C])
            w_v2 = s.sb("qkv_w_v2", [128, C])
            o_qk = s.sb("qkv_o_qk", [128, SLOTS, COLS])
            rest = s.sb("qkv_rest", [128, SLOTS, COLS])
            part = s.sb("qkv_part", [128, SLOTS, PARTS, COLS], BF16)
            o_v = s.sb("qkv_o_v", [128, SLOTS, COLS])
            row_step, row_sum = s.sem("qkv_row_step"), s.sem("qkv_row_sum")
            rest_made, part2_made, part3_made = s.sem("qkv_rest_made"), s.sem("qkv_part2_made"), s.sem("qkv_part3_made")
        if kind == "image":
            zeros = s.sb("image_zeros", [128, 6 * C])
            zeroed, edges = s.sem("image_zeroed"), s.sem("image_edges")
        if kind == "gate":
            o_log = s.sb("gate_o_log", [64, SLOTS, COLS])
        n_store = {"qkv_stats": 0, "qkv": 4, "ffn": 1, "image": 1, "gate": 1}[kind]
        tok_stores = {"image": 2, "gate": 1}.get(kind, 0)
        tok_stored = [s.sem(f"{p}_tok_stored{k}") for k in range(SLOTS if tok_stores else 0)]
        block_ctx = ExitStack()
        block = block_ctx.enter_context(nc.Block())

        def slot_stored(eng, t):
            if n_store:
                wait_for(eng, stored[t.slot], t.turn * (16 * n_store))

        @block.sync
        def _(sp):
            for dst, src in weights:
                sp.dma_start(dst, src).then_inc(w_in, 16)

            def step(turn, k):
                t = Tile(turn, k, 0)
                if t.exists:
                    wait_for(sp, cent_made, t.n - SLOTS + 1)
                    sp.dma_start(x_in[:, t.slot, :], tile_of(io["src"], t.n // IMG_TILES, t.n % IMG_TILES)
                                 ).then_inc(x_loaded[t.slot], 16)
                t = Tile(turn, k, TOK_LAG)
                if t.exists and tok_stores:
                    b, j, src = t.n // IMG_TILES, t.n % IMG_TILES, tok[:, t.slot, :].rearrange("p (r c) -> p r c", r=TILE)
                    sp.wait_ge(tok_made, t.n + 1)
                    if kind == "gate":
                        sp.dma_start(io["tokens"][DS(b, 1), DS(j * TILE, TILE)].rearrange("o r w c -> w (o r) c"), src
                                     ).then_inc(tok_stored[t.slot], 16)
                    else:
                        for half in range(2):
                            sp.dma_start(io["patches"][DS(b, 1), DS(j * TILE + 1 - half, TILE), 1:W + 1, half, :
                                                       ].rearrange("o r w c -> w (o r) c"), src).then_inc(tok_stored[t.slot], 16)
                t = Tile(turn, k, STORE_LAG)
                if not t.exists or not n_store:
                    return
                b, j, done = t.n // IMG_TILES, t.n % IMG_TILES, stored[t.slot]
                if kind == "qkv":
                    sp.wait_ge(part3_made, t.n + 1)
                    sp.wait_ge(taken_d, t.n + 1)
                    for a in range(PARTS):
                        sp.dma_start(io["qk_parts"][a][:, DS(t.n * COLS, COLS)], part[:, t.slot, a, :]).then_inc(done, 16)
                    sp.dma_start(io["v"][:, DS(t.n * COLS, COLS)], o_v[:, t.slot, :]).then_inc(done, 16)
                if kind in ("ffn", "image"):
                    sp.wait_ge(xn_made, t.n + 1)
                if kind == "ffn":
                    sp.dma_start(tile_of(io["xn"], b, j), xn[:, t.slot, :]).then_inc(done, 16)
                if kind == "gate":
                    sp.wait_ge(taken_d, t.n + 1)
                    sp.dma_start(tile_of(io["logits"], b, j), o_log[:, t.slot, :]).then_inc(done, 16)
                if kind == "image":
                    sp.dma_start(io["rows"][DS(b, 1), :, DS(j * TILE + 1, TILE), :].rearrange("o c r w -> (o c) (r w)"),
                                 xn[:, t.slot, :]).then_inc(done, 16)

            turns(sp, step)
            if n_store:
                for k in range(SLOTS):
                    sp.wait_ge(stored[k], 16 * n_store * (TILES // SLOTS))
                    if tok_stores:
                        sp.wait_ge(tok_stored[k], 16 * tok_stores * (TILES // SLOTS))

        @block.tensor
        def _(pe):
            pe.wait_ge(w_in, 16 * len(weights)) if weights else None
            if kind == "qkv":
                pe.wait_ge(row_step, 3)
                for r in range(2):
                    last = pe.matmul(out_ps[:, r, 0:C], mean_mat[:], diag[:, r, :], start=True, stop=True)
                last.then_inc(row_sum, 1)
                pe.wait_ge(row_step, 5)

            def step(turn, k):
                t = Tile(turn, k, 0)
                if t.exists:
                    pe.wait_ge(x_loaded[t.slot], t.turn * 16 + 16)
                    wait_for(pe, tok_made, t.n - 1)
                    for r in range(TILE):
                        last = pe.matmul(cent[:, t.bank, r * C:(r + 1) * C], x_in[:, t.slot, r * W:(r + 1) * W], center_mat[:],
                                         start=True, stop=True)
                    last.then_inc(cent_made, 1)
                t = Tile(turn, k, 2)
                if t.exists:
                    pe.wait_ge(tok_made, t.n + 1)
                    wait_for(pe, xn_made, t.n - 1)
                    for r in range(TILE):
                        last = pe.transpose(back[:, t.bank, r * W:(r + 1) * W], tok[:, t.slot, r * C:(r + 1) * C], ident[:])
                    last.then_inc(back_made, 1)
                t = Tile(turn, k, 3)
                if not t.exists or not products:
                    return
                pe.wait_ge(xn_made, t.n + 1)
                wait_for(pe, taken_d, t.n - 1)
                if kind == "qkv":
                    wait_for(pe, taken_a, t.n - 1)
                a, b, x = out_ps[:, 2 * t.bank, :], out_ps[:, 2 * t.bank + 1, :], xn[:, t.slot, :]
                if kind in ("qkv_stats", "qkv"):
                    last = pe.matmul(a, w_qk[:], x, start=True, stop=True)
                if kind == "qkv_stats":
                    last = pe.matmul(b, w_v[:], x, start=True, stop=True)
                if kind == "qkv":
                    for r in range(TILE):
                        last = pe.matmul(b[:, r * C:(r + 1) * C], x[:, r * W:(r + 1) * W], w_v2[:], start=True, stop=True)
                if kind == "ffn":
                    last = pe.matmul(a, w_f[:], x, start=True, stop=True)
                if kind == "gate":
                    last = pe.matmul(a[0:64], w_g[:], x, start=True, stop=True)
                last.then_inc(prod_made, 1)

            turns(pe, step)

        def copy_back(eng, copy, t):
            eng.wait_ge(back_made, t.n + 1)
            if kind in ("ffn", "image"):
                slot_stored(eng, t)
            else:
                wait_for(eng, prod_made, t.n - SLOTS + 1)
            copy(xn[:, t.slot, :], back[:, t.bank, :]).then_inc(xn_made, 1)

        @block.scalar
        def _(act):
            act.wait_ge(eps_set, 1)

            def step(turn, k):
                t = Tile(turn, k, 1)
                if t.exists:
                    act.wait_ge(rstd_made, t.n + 1)
                    wait_for(act, back_made, t.n - SLOTS + 1)
                    if tok_stores:
                        wait_for(act, tok_stored[t.slot], t.turn * (16 * tok_stores))
                    for r in range(TILE):
                        last = act.activation(tok[:, t.slot, r * C:(r + 1) * C], cent[:, t.bank, r * C:(r + 1) * C], ACT.Copy,
                                              scale=rstd[:, t.slot, r:r + 1])
                    last.then_inc(tok_made, 1)
                t = Tile(turn, k, 2)
                if t.exists and kind != "qkv":
                    copy_back(act, act.copy, t)
                t = Tile(turn, k, 0)
                if t.exists:
                    act.wait_ge(var_made, t.n + 1)
                    act.activation(std[:, t.slot, :], mean_var[:, t.slot, :, 1], ACT.Sqrt, bias=eps_col[:]).then_inc(std_made, 1)
                if kind != "qkv":
                    return
                t = Tile(turn, k, 4)
                if t.exists:
                    act.wait_ge(rest_made, t.n + 1)
                    act.copy(part[:, t.slot, 1, :], rest[:, t.slot, :]).then_inc(part2_made, 1)
                t = Tile(turn, k, 3)
                if t.exists:
                    act.wait_ge(prod_made, t.n + 1)
                    slot_stored(act, t)
                    for dst in (part[:, t.slot, 0, :], o_qk[:, t.slot, :]):
                        last = act.activation(dst, out_ps[:, 2 * t.bank, :], ACT.Identity, scale=coef_qk[:, 0:1],
                                              bias=coef_qk[:, 1:2])
                    last.then_inc(taken_a, 1)

            turns(act, step)

        @block.vector
        def _(dve):
            dve.memset(eps_col[:], eps).then_inc(eps_set, 1)
            if kind == "qkv":
                dve.wait_ge(w_in, 32)
                for r in range(2):
                    dve.tensor_scalar(diag[:, r, :], ident[:], coef_v[:, r:r + 1], float(C), ALU.mult, ALU.mult).then_inc(row_step, 1)
                dve.sem_inc(row_step, 1)
                dve.wait_ge(row_sum, 1)
                dve.tensor_copy(v_row[:], out_ps[:, 0:2, 0:C]).then_inc(row_step, 1)
                dve.wait_ge(row_step, 4)
                dve.tensor_tensor(w_v2[:], w_v[:], v_row[:, 0, :], ALU.mult).then_inc(row_step, 1)

            def take(t):
                dve.wait_ge(prod_made, t.n + 1)
                if stats:
                    for m in range(kinds):
                        last = dve.bn_stats(hist[:, m, DS(t.n, 1), :].rearrange("p o f -> p (o f)"),
                                            out_ps[:, 2 * t.bank + m, :])
                    last.then_inc(taken_d, 1)
                    return
                slot_stored(dve, t)
                if kind == "qkv":
                    dve.tensor_tensor(o_v[:, t.slot, :].rearrange("p (r c) -> p r c", r=TILE),
                                      out_ps[:, 2 * t.bank + 1, :].rearrange("p (r c) -> p r c", r=TILE),
                                      v_row[:, 1, :].unsqueeze(1).to_broadcast([128, TILE, C]), ALU.add).then_inc(taken_d, 1)
                else:
                    dve.tensor_scalar(o_log[:, t.slot, :], out_ps[0:64, 2 * t.bank, :], b_g[:, 0:1], None, ALU.add
                                      ).then_inc(taken_d, 1)

            def step(turn, k):
                t = Tile(turn, k, 0)
                if t.exists:
                    dve.wait_ge(cent_made, t.n + 1)
                    for r in range(TILE):
                        last = dve.bn_stats(moments[:, t.slot, r, :], cent[:, t.bank, r * C:(r + 1) * C])
                        last.then_inc(moments_made, 1)
                    dve.wait_ge(moments_made, t.n * TILE + TILE)
                    dve.sem_inc(moments_passed, 1)
                    for r in range(TILE):
                        last = dve.bn_aggr(mean_var[:, t.slot, r, :], moments[:, t.slot, r, :])
                    last.then_inc(var_made, 1)
                t2 = Tile(turn, k, 2)
                if t2.exists and kind == "qkv":
                    copy_back(dve, dve.tensor_copy, t2)
                t3 = Tile(turn, k, 3)
                if t3.exists and products:
                    take(t3)
                if t.exists:
                    dve.wait_ge(std_made, t.n + 1)
                    dve.reciprocal(rstd[:, t.slot, :], std[:, t.slot, :]).then_inc(rstd_made, 1)

            turns(dve, step)

        @block.gpsimd
        def _(pool):
            if kind == "qkv":
                def step(turn, k):
                    t = Tile(turn, k, 3)
                    if t.exists:
                        pool.wait_ge(taken_a, t.n + 1)
                        pool.tensor_tensor(rest[:, t.slot, :], o_qk[:, t.slot, :], part[:, t.slot, 0, :], ALU.subtract
                                           ).then_inc(rest_made, 1)
                    t = Tile(turn, k, 4)
                    if t.exists:
                        pool.wait_ge(part2_made, t.n + 1)
                        pool.tensor_tensor(part[:, t.slot, 2, :], rest[:, t.slot, :], part[:, t.slot, 1, :], ALU.subtract
                                           ).then_inc(part3_made, 1)

                turns(pool, step)

            if kind == "image":
                pool.memset(zeros[:], 0.0).then_inc(zeroed, 1)
                pool.wait_ge(zeroed, 1)
                img, rows = io["patches"], io["rows"]
                n = 0
                for b in range(B):
                    for y, half in ((0, 0), (PH - 1, 1)):
                        pool.dma_start(img[b, y, 1:W + 1, half, :].rearrange("(p q) c -> p q c", q=2),
                                       zeros[0:W // 2, 0:2 * C].rearrange("p (q c) -> p q c", q=2)).then_inc(edges, 16)
                        n += 1
                    for x in (0, PW - 1):
                        pool.dma_start(img[b, :, x].rearrange("(p q) h c -> p q (h c)", q=3),
                                       zeros[0:PH // 3, :].rearrange("p (q f) -> p q f", q=3)).then_inc(edges, 16)
                        n += 1
                    for y in (0, H + 1):
                        pool.dma_start(rows[b, :, y, :], zeros[:, 0:W]).then_inc(edges, 16)
                        n += 1
                pool.wait_ge(edges, 16 * n)
        block_ctx.close()
        if stats:
            channel_coefs(nc, s, p, hist, mv, gb, io["coef"])


def channel_coefs(nc, s, p, hist, mv, gb, coef):
    link, rooted = s.sem(f"{p}_cc_link"), s.sem(f"{p}_cc_rooted")
    kinds = hist.shape[1]
    with nc.Block() as block:
        @block.scalar
        def _(act):
            act.wait_ge(link, kinds + 1)
            act.activation(mv[:, :, 1], mv[:, :, 1], ACT.Sqrt).then_inc(rooted, 1)

        @block.vector
        def _(dve):
            done = [0]

            def then(ins):
                done[0] += 1
                ins.then_inc(link, 1)
                dve.wait_ge(link, done[0])

            for m in range(kinds):
                then(dve.bn_aggr(mv[:, m, :], hist[:, m].rearrange("p t f -> p (t f)")))
            then(dve.tensor_scalar(mv[:, :, 1], mv[:, :, 1], EPS, None, ALU.add))
            dve.wait_ge(rooted, 1)
            then(dve.reciprocal(mv[:, :, 1], mv[:, :, 1]))
            for m in range(kinds):
                c = coef[m]
                then(dve.tensor_tensor(c[:, 0:1], mv[:, m, 1:2], gb[:, m, 0:1], ALU.mult))
                then(dve.tensor_tensor(c[:, 1:2], mv[:, m, 0:1], c[:, 0:1], ALU.mult))
                then(dve.tensor_tensor(c[:, 1:2], gb[:, m, 1:2], c[:, 1:2], ALU.subtract))


MIX_SLOTS = 4


def mix_phase(nc, sems, io, coef_a, coef_e, stats):
    p = "ms" if stats else "mx"
    MC = RB * W
    with Scope(nc, sems) as s:
        att = s.sb(f"{p}_att", [128, MIX_SLOTS, MC])
        emb = s.sb(f"{p}_emb", [128, MIX_SLOTS, MC])
        loaded = [s.sem(f"{p}_loaded{k}") for k in range(MIX_SLOTS)]
        spent = s.sem(f"{p}_spent")
        per = 16 * (2 + (not stats))
        if stats:
            hist = s.sb("ms_hist", [128, 2, 2 * BLOCKS, 6])
            mv, gb = s.sb("ms_mv", [128, 2, 2]), s.sb("ms_gb", [128, 2, 2])
            gb_in = s.sem("ms_gb_in")
        else:
            x = s.sb("mx_x", [128, MIX_SLOTS, MC])
            shift = s.sb("mx_shift", [128, 1])
            shift_made, att_made, sum_made = s.sem("mx_shift_made"), s.sem("mx_att_made"), s.sem("mx_sum_made")
            out_made = s.sem("mx_out_made")
            stored = [s.sem(f"mx_stored{k}") for k in range(MIX_SLOTS)]
        block_ctx = ExitStack()
        block = block_ctx.enter_context(nc.Block())

        @block.sync
        def _(sp):
            if stats:
                sp.dma_start(gb[:], io["gb_out"]).then_inc(gb_in, 16)
            with sp.Fori(0, BLOCKS // MIX_SLOTS) as i:
                for k in range(MIX_SLOTS):
                    t = i * MIX_SLOTS + k
                    sp.wait_ge(spent, t + 1)
                    if not stats:
                        sp.wait_ge(stored[k], 16 * (i + 1))
                        sp.dma_start(x[:, k, :], io["x"][DS(t // (H // RB), 1), :, DS((t % (H // RB)) * MC, MC)
                                                         ].rearrange("o c f -> (o c) f")).then_inc(loaded[k], 16)
                    sp.dma_start(att[:, k, :], io["attn"][:, DS(t * MC, MC)]).then_inc(loaded[k], 16)
                    sp.dma_start(emb[:, k, :], io["emb"][DS(t, 1)].rearrange("o c (g n) i -> (o g) c (n i)", g=G)).then_inc(loaded[k], 16)
            if not stats:
                for k in range(MIX_SLOTS):
                    sp.wait_ge(stored[k], 16 * (BLOCKS // MIX_SLOTS + 1))

        @block.scalar
        def _(act):
            if stats:
                return
            for k in range(MIX_SLOTS):
                act.sem_inc(stored[k], 16)
            act.wait_ge(shift_made, 1)
            with act.Fori(0, BLOCKS // MIX_SLOTS) as i:
                for k in range(MIX_SLOTS):
                    t = i * MIX_SLOTS + k
                    act.wait_ge(loaded[k], per * (i + 1))
                    act.activation(att[:, k, :], att[:, k, :], ACT.Identity, scale=coef_a[:, 0:1], bias=shift[:]
                                   ).then_inc(att_made, 1)
                for k in range(MIX_SLOTS):
                    t = i * MIX_SLOTS + k
                    act.wait_ge(out_made, t + 1)
                    act.dma_start(io["x1"][DS(t // (H // RB), 1), :, DS((t % (H // RB)) * MC, MC)
                                           ].rearrange("o c f -> (o c) f"), att[:, k, :]).then_inc(stored[k], 16)

        @block.vector
        def _(dve):
            dve.sem_inc(spent, MIX_SLOTS)
            if not stats:
                dve.tensor_tensor(shift[:], coef_a[:, 1:2], coef_e[:, 1:2], ALU.add).then_inc(shift_made, 1)
            with dve.Fori(0, BLOCKS // MIX_SLOTS) as i:
                for k in range(MIX_SLOTS):
                    t = i * MIX_SLOTS + k
                    dve.wait_ge(loaded[k], per * (i + 1))
                    if stats:
                        for m, src in enumerate((att, emb)):
                            for half in range(2):
                                last = dve.bn_stats(hist[:, m, DS(2 * t + half, 1), :].rearrange("p o f -> p (o f)"),
                                                    src[:, k, half * BANK:(half + 1) * BANK])
                        last.then_inc(spent, 1)
                        continue
                    dve.scalar_tensor_tensor(out=x[:, k, :], in0=emb[:, k, :], scalar=coef_e[:, 0:1], in1=x[:, k, :],
                                             op0=ALU.mult, op1=ALU.add).then_inc(sum_made, 1)
                    dve.wait_ge(sum_made, t + 1)
                    dve.wait_ge(att_made, t + 1)
                    dve.tensor_tensor(att[:, k, :], att[:, k, :], x[:, k, :], ALU.add).then_inc(out_made, 1)
                    dve.sem_inc(spent, 1)
            if stats:
                dve.wait_ge(spent, BLOCKS + MIX_SLOTS)
                dve.wait_ge(gb_in, 16)
        block_ctx.close()
        if stats:
            channel_coefs(nc, s, p, hist, mv, gb, [coef_a, coef_e])


CHUNKS = 32
LEN = T // CHUNKS
SPAN = 64
SPANS = LEN // SPAN
RC = B * CHUNKS
SETTLED = 2.0 ** -20
RING = 4


def recurrence_phase(nc, sems, consts, io, coef_f):
    assert RC == 128
    ident = consts["ident"]
    with Scope(nc, sems) as s:
        w_nat = s.sb("rn_w_nat", [128, C])
        w_eff = s.sb("rn_w_eff", [128, C])
        v_t = s.sb("rn_v_t", [128, C])
        diag = s.sb("rn_diag", [128, C])
        xs = s.sb("rn_xs", [128, 2, RC, SPAN])
        os_ = s.sb("rn_os", [128, 2, RC, SPAN])
        y = s.sb("rn_y", [128, RING, RC])
        start = s.sb("rn_start", [128, RC])
        nxt = s.sb("rn_nxt", [128, RC])
        differ = s.sb("rn_differ", [128, RC])
        worst = s.sb("rn_worst", [128, 1])
        again = s.sb("rn_again", [128, 1], I32)
        pre = s.ps("rn_pre", [128, RING, BANK])
        misc = s.ps("rn_misc", [128, BANK])
        w_in, diag_made, eff_made, eff_taken = s.sem("rn_w_in"), s.sem("rn_diag_made"), s.sem("rn_eff_made"), s.sem("rn_eff_taken")
        warm_loaded = s.sem("rn_warm_loaded")
        loaded = [s.sem(f"rn_loaded{k}") for k in range(2)]
        slot_free = s.sem("rn_slot_free")
        pre_made, y_made, added = s.sem("rn_pre_made"), s.sem("rn_y_made"), s.sem("rn_added")
        stored = [s.sem(f"rn_stored{k}") for k in range(2)]
        started = s.sem("rn_started")
        link, counted, settled = s.sem("rn_link"), s.sem("rn_counted"), s.sem("rn_settled")
        judged = s.sem("rn_judged")
        passed = {e: s.sem(f"rn_passed_{e}") for e in ("pe", "act", "dve", "sp", "pool")}
        xn_c = io["xn"].rearrange("b c (k t) -> b c k t", t=LEN)
        x1_c = io["x1"].rearrange("b c (k t) -> b c k t", t=LEN)
        x2_c = io["x2"].rearrange("b c (k t) -> b c k t", t=LEN)
        warm_steps = SPAN

        def rounds(eng, name):
            @contextmanager
            def one():
                with eng.Fori(0, CHUNKS) as r:
                    eng.wait_ge(settled, r + 1)
                    eng.sem_inc(passed[name], 1)
                    go = eng.value_load(again[0:1, 0:1], min_val=0, max_val=1)
                    with eng.If(go > 0):
                        yield r
                    if name == "dve":
                        eng.sem_inc(settled, 1)
            return one()

        block = s.ctx.enter_context(nc.Block())

        @block.sync
        def _(sp):
            sp.dma_start(w_nat[:], io["w_f_nat"]).then_inc(w_in, 16)
            sp.dma_start(v_t[:], io["v_t"]).then_inc(w_in, 16)
            for b in range(B):
                sp.dma_start(xs[:, 1, b * CHUNKS:(b + 1) * CHUNKS, :], xn_c[b, :, :, LEN - SPAN:LEN]).then_inc(warm_loaded, 16)
            with rounds(sp, "sp") as r:
                with sp.Fori(0, SPANS // 2) as j:
                    for k in range(2):
                        n = r * SPANS + j * 2 + k
                        sp.wait_ge(slot_free, n + 1)
                        for b in range(B):
                            sp.dma_start(xs[:, k, b * CHUNKS:(b + 1) * CHUNKS, :],
                                         xn_c[b, :, :, DS((j * 2 + k) * SPAN, SPAN)]).then_inc(loaded[k], 16)
                            sp.dma_start(os_[:, k, b * CHUNKS:(b + 1) * CHUNKS, :],
                                         x1_c[b, :, :, DS((j * 2 + k) * SPAN, SPAN)]).then_inc(loaded[k], 16)

        @block.tensor
        def _(pe):
            pe.wait_ge(w_in, 32)
            pe.wait_ge(diag_made, 1)
            pe.matmul(misc[:, 0:C], w_nat[:], diag[:], start=True, stop=True).then_inc(eff_made, 1)
            pe.wait_ge(eff_taken, 1)
            pe.wait_ge(warm_loaded, 16 * B)
            pe.wait_ge(started, 1)
            with pe.Fori(0, SPAN // RING) as q:
                for u in range(RING):
                    pe.matmul(pre[:, u, 0:RC], w_eff[:], xs[:, 1, :, DS(q * RING + u, 1)].rearrange("p c o -> p (c o)"),
                              start=True, stop=False)
                    pe.wait_ge(y_made, q * RING + u + 1)
                    pe.matmul(pre[:, u, 0:RC], v_t[:], y[:, (u - 1) % RING, :], start=False, stop=True).then_inc(pre_made, 1)
            pe.wait_ge(y_made, warm_steps + 1)
            pe.sem_inc(slot_free, 2)
            pe.wait_ge(link, 5)
            pe.matmul(misc[:, 0:1], consts["mean_mat"][:], worst[:], start=True, stop=True).then_inc(counted, 1)
            with rounds(pe, "pe") as r:
                pe.wait_ge(started, r + 2)
                pe.sem_inc(passed["pe"], 1)
                with pe.Fori(0, SPANS // 2) as j:
                    for k in range(2):
                        pe.wait_ge(loaded[k], 16 * 2 * B * (r * (SPANS // 2) + j + 1))
                        pe.sem_inc(passed["pe"], 1)
                        with pe.Fori(0, SPAN // RING) as q:
                            for u in range(RING):
                                m = r * LEN + (j * 2 + k) * SPAN + q * RING + u
                                pe.matmul(pre[:, u, 0:RC], w_eff[:],
                                          xs[:, k, :, DS(q * RING + u, 1)].rearrange("p c o -> p (c o)"),
                                          start=True, stop=False)
                                pe.wait_ge(y_made, m + warm_steps + 1)
                                pe.matmul(pre[:, u, 0:RC], v_t[:], y[:, (u - 1) % RING, :], start=False, stop=True
                                          ).then_inc(pre_made, 1)
                pe.wait_ge(link, r * 5 + 10)
                pe.matmul(misc[:, 0:1], consts["mean_mat"][:], worst[:], start=True, stop=True).then_inc(counted, 1)

        @block.scalar
        def _(act):
            act.sem_inc(y_made, 1)
            with act.Fori(0, SPAN // RING) as q:
                for u in range(RING):
                    act.wait_ge(pre_made, q * RING + u + 1)
                    act.activation(y[:, u, :], pre[:, u, 0:RC], ACT.Sigmoid, bias=coef_f[:, 1:2]).then_inc(y_made, 1)
            with rounds(act, "act") as r:
                act.wait_ge(started, r + 2)
                act.sem_inc(passed["act"], 1)
                with act.Fori(0, LEN // RING) as q:
                    for u in range(RING):
                        m = r * LEN + q * RING + u
                        act.wait_ge(added, m + 1)
                        act.wait_ge(pre_made, m + warm_steps + 1)
                        act.activation(y[:, u, :], pre[:, u, 0:RC], ACT.Sigmoid, bias=coef_f[:, 1:2]).then_inc(y_made, 1)

        @block.vector
        def _(dve):
            dve.sem_inc(added, RING)
            dve.tensor_scalar(diag[:], ident[:], coef_f[:, 0:1], None, ALU.mult).then_inc(diag_made, 1)
            dve.memset(start[:], 0.0).then_inc(eff_taken, 1)
            dve.memset(nxt[:], 0.0).then_inc(eff_taken, 1)
            dve.wait_ge(eff_made, 1)
            dve.tensor_copy(w_eff[:], misc[:, 0:C]).then_inc(eff_taken, 1)
            dve.wait_ge(eff_taken, 3)
            dve.tensor_copy(y[:, RING - 1, :], start[:]).then_inc(started, 1)

            def judge(m, steps):
                dve.wait_ge(y_made, steps + 1)
                for b in range(B):
                    last = dve.tensor_copy(nxt[:, b * CHUNKS + 1:(b + 1) * CHUNKS], y[:, RING - 1, b * CHUNKS:(b + 1) * CHUNKS - 1])
                last.then_inc(link, 1)
                dve.wait_ge(link, m * 5 + 1)
                dve.tensor_tensor(differ[:], nxt[:], start[:], ALU.subtract).then_inc(link, 1)
                dve.wait_ge(link, m * 5 + 2)
                dve.tensor_tensor(differ[:], differ[:], differ[:], ALU.mult).then_inc(link, 1)
                dve.wait_ge(link, m * 5 + 3)
                dve.tensor_scalar(differ[:], differ[:], SETTLED ** 2, None, ALU.is_gt).then_inc(link, 1)
                dve.wait_ge(link, m * 5 + 4)
                dve.tensor_reduce(worst[:], differ[:], AX.X, ALU.add).then_inc(link, 1)
                dve.wait_ge(counted, m + 1)
                if type(m) is int:
                    dve.memset(again[:], 1).then_inc(judged, 1)
                else:
                    dve.tensor_scalar(again[:], misc[:, 0:1], 0.0, None, ALU.is_gt).then_inc(judged, 1)
                dve.tensor_copy(start[:], nxt[:]).then_inc(judged, 1)
                dve.wait_ge(judged, m * 2 + 2)
                dve.tensor_copy(y[:, RING - 1, :], nxt[:]).then_inc(started, 1)

            judge(0, warm_steps)
            dve.sem_inc(settled, 1)
            with rounds(dve, "dve") as r:
                dve.wait_ge(started, r + 2)
                dve.sem_inc(passed["dve"], 1)
                with dve.Fori(0, SPANS // 2) as j:
                    for k in range(2):
                        dve.wait_ge(loaded[k], 16 * 2 * B * (r * (SPANS // 2) + j + 1))
                        dve.sem_inc(passed["dve"], 1)
                        with dve.Fori(0, SPAN // RING) as q:
                            for u in range(RING):
                                m = r * LEN + (j * 2 + k) * SPAN + q * RING + u
                                dve.wait_ge(y_made, m + warm_steps + 2)
                                o = os_[:, k, :, DS(q * RING + u, 1)].rearrange("p c o -> p (c o)")
                                dve.tensor_tensor(o, y[:, u, :], o, ALU.add).then_inc(added, 1)
                dve.wait_ge(added, RING + r * LEN + LEN)
                judge(r + 1, r * LEN + LEN + warm_steps)

        @block.gpsimd
        def _(pool):
            with rounds(pool, "pool") as r:
                with pool.Fori(0, SPANS // 2) as j:
                    for k in range(2):
                        n = r * SPANS + j * 2 + k
                        pool.wait_ge(added, RING + (n + 1) * SPAN)
                        for b in range(B):
                            pool.dma_start(x2_c[b, :, :, DS((j * 2 + k) * SPAN, SPAN)],
                                           os_[:, k, b * CHUNKS:(b + 1) * CHUNKS, :]).then_inc(stored[k], 16)
                        pool.wait_ge(stored[k], 16 * B * (r * (SPANS // 2) + j + 1))
                        pool.sem_inc(slot_free, 1)


TAPS = 9
NP = TILE * TAPS
GR = 12
SR = 8
PATCH = 4 * C
ROW_STEP = PW * 2 * C
COL_STEP = 2 * C


def deform_phase(nc, sems, consts, io):
    ident = consts["ident"]
    with Scope(nc, sems) as s:
        off_w = s.sb("df_off_w", [128, TAPS, 2 * TAPS])
        off_b = s.sb("df_off_b", [2 * TAPS, 1])
        tap_w = s.sb("df_tap_w", [128, TAPS, C])
        tap_b = s.sb("df_tap_b", [128, 1])
        xr = s.sb("df_xr", [128, 2, TILE + 2, W + 2])
        off = s.sb("df_off", [2 * TAPS, COLS])
        base_y = s.sb("df_base_y", [128, IMG_TILES, NP])
        base_x = s.sb("df_base_x", [128, NP])
        base_i = s.sb("df_base_i", [128, B])
        pos = s.sb("df_pos", [128, 2, NP])
        low = s.sb("df_low", [128, 2, NP])
        low_i = s.sb("df_low_i", [128, 2, NP], I32)
        over = s.sb("df_over", [128, 2, NP])
        frac = s.sb("df_frac", [128, 2, 2, NP])
        at = s.sb("df_at", [128, NP])
        idx = s.sb("df_idx", [128, 2, NP], U32)
        wgt = s.sb("df_wgt", [128, 2, NP, 2, 2])
        patch = s.sb("df_patch", [128, GR, PATCH])
        samp = s.sb("df_samp", [128, SR, C])
        samp_t = s.sb("df_samp_t", [128, 2, COLS])
        x2 = s.sb("df_x2", [128, 2, COLS])
        off_ps = s.ps("df_off_ps", [128, BANK])
        pos_ps = s.ps("df_pos_ps", [128, BANK])
        turn_ps = s.ps("df_turn_ps", [128, 3, BANK])
        out_ps = s.ps("df_out_ps", [128, 2, BANK])
        w_in, border, tables = s.sem("df_w_in"), s.sem("df_border"), s.sem("df_tables")
        xr_loaded = [s.sem(f"df_xr_loaded{k}") for k in range(2)]
        x2_loaded = [s.sem(f"df_x2_loaded{k}") for k in range(2)]
        off_made, off_taken, pos_made = s.sem("df_off_made"), s.sem("df_off_taken"), s.sem("df_pos_made")
        link, idx_made = s.sem("df_link"), s.sem("df_idx_made")
        gathered = [s.sem(f"df_gathered{k}") for k in range(GR)]
        pool_passed, pe_passed = s.sem("df_pool_passed"), s.sem("df_pe_passed")
        mixed0, mixed = s.sem("df_mixed0"), s.sem("df_mixed")
        turned, turn_taken = s.sem("df_turned"), s.sem("df_turn_taken")
        tap_done, out_made, out_taken = s.sem("df_tap_done"), s.sem("df_out_made"), s.sem("df_out_taken")
        stored = [s.sem(f"df_stored{k}") for k in range(2)]
        LINKS = 14
        PRIME = 3 * GR

        OFF_TAPS, OFF_COPY, OFF_TURN, INDEX = 3, 3, 4, 5

        def sweep(eng, front, taps):
            front(0, 0)
            with eng.Fori(0, TILES // 2 - 1) as i:
                for k in range(2):
                    taps(2 * i + k, k, (2 * i + k + 1, (k + 1) % 2))
            taps(TILES - 2, 0, (TILES - 1, 1))
            taps(TILES - 1, 1, None)

        block = s.ctx.enter_context(nc.Block())

        @block.sync
        def _(sp):
            sp.dma_start(off_w[:], io["off_w"]).then_inc(w_in, 16)
            sp.dma_start(off_b[:], io["off_b"]).then_inc(w_in, 16)
            sp.dma_start(tap_w[:], io["tap_w"]).then_inc(w_in, 16)
            sp.dma_start(tap_b[:], io["tap_b"]).then_inc(w_in, 16)
            sp.wait_ge(border, 1)

            def front(t, k):
                b, j = t // IMG_TILES, t % IMG_TILES
                sp.wait_ge(off_made, t + 1)
                sp.dma_start(xr[:, k, :, 1:W + 1],
                             io["rows"][DS(b, 1), :, DS(j * TILE, TILE + 2), :].rearrange("o c r w -> (o c) r w")
                             ).then_inc(xr_loaded[k], 16)
                sp.wait_ge(stored[k], 16 * (t // 2 + 1))
                sp.dma_start(x2[:, k, :], tile_of(io["x2"], b, j)).then_inc(x2_loaded[k], 16)

            def store(t, k, following):
                if following:
                    front(*following)
                b, j = t // IMG_TILES, t % IMG_TILES
                sp.wait_ge(out_taken, t + 3)
                sp.dma_start(tile_of(io["x3"], b, j), x2[:, k, :]).then_inc(stored[k], 16)

            for k in range(2):
                sp.sem_inc(stored[k], 16)
            sweep(sp, front, store)
            for k in range(2):
                sp.wait_ge(stored[k], 16 * (TILES // 2 + 1))

        @block.tensor
        def _(pe):
            pe.sem_inc(off_made, 2)
            pe.wait_ge(w_in, 64)

            def offsets(t, k, ky):
                if ky == 0:
                    pe.wait_ge(xr_loaded[k], 16 * (t // 2 + 1))
                    pe.wait_ge(off_taken, t + 1)
                for kx in range(3):
                    m = ky * 3 + kx
                    last = pe.matmul(off_ps[0:2 * TAPS, :], off_w[:, m, :], xr[:, k, ky:ky + TILE, kx:kx + W],
                                     start=(m == 0), stop=(m == TAPS - 1))
                if ky == 2:
                    last.then_inc(off_made, 1)

            def turn_offsets(t, k):
                pe.wait_ge(off_taken, t + 2)
                pe.wait_ge(link, t * LINKS + 2)
                pe.sem_inc(pe_passed, 1)
                for r in range(TILE):
                    last = pe.transpose(pos_ps[:, r * 2 * TAPS:(r + 1) * 2 * TAPS], off[:, r * W:(r + 1) * W],
                                        ident[0:2 * TAPS, 0:2 * TAPS])
                last.then_inc(pos_made, 1)

            def front(t, k):
                for ky in range(3):
                    offsets(t, k, ky)
                turn_offsets(t, k)

            def taps(t, k, following):
                pe.wait_ge(out_taken, t + 1)

                def product(m):
                    pe.wait_ge(turn_taken, t * TAPS + m + 3 + 1)
                    last = pe.matmul(out_ps[:, k, :], tap_w[:, m, :], samp_t[:, (TAPS * k + m) % 2, :],
                                     start=(m == 0), stop=(m == TAPS - 1))
                    last.then_inc(tap_done, 1)

                for m in range(TAPS):
                    pe.wait_ge(turn_taken, t * TAPS + m + 1)
                    for r in range(TILE):
                        pe.wait_ge(mixed, PRIME + 3 * TILE * (TAPS * t + m) + 2 * TILE + r + 1)
                        last = pe.transpose(turn_ps[:, m % 3, r * W:(r + 1) * W], samp[:, ((TAPS * k + m) * TILE + r) % SR, :],
                                            ident[:])
                    last.then_inc(turned, 1)
                    if m >= 1:
                        product(m - 1)
                    if following and m < OFF_TAPS:
                        offsets(*following, m)
                    if following and m == OFF_TURN:
                        turn_offsets(*following)
                product(TAPS - 1)

            sweep(pe, front, taps)

        @block.scalar
        def _(act):
            act.sem_inc(off_taken, 1)
            act.sem_inc(turn_taken, 3)
            act.wait_ge(w_in, 64)

            def front(t, k):
                act.wait_ge(off_made, t + 3)
                act.wait_ge(pos_made, t + 1)
                act.activation(off[:], off_ps[0:2 * TAPS, :], ACT.Identity, bias=off_b[:]).then_inc(off_taken, 1)

            def taps(t, k, following):
                def first(m):
                    for r in range(TILE):
                        q = (TAPS * k + m) * TILE + r
                        n = m * TILE + r
                        g = n % GR
                        act.wait_ge(gathered[g], 16 * (t * (NP // GR) + n // GR + 1))
                        if r == 0:
                            act.wait_ge(turned, t * TAPS + m + 1)
                        act.activation(samp[:, q % SR, :], patch[:, g, 0:C], ACT.Copy, scale=wgt[:, k, r * TAPS + m, 0, 0:1]
                                       ).then_inc(mixed0, 1)

                def take(m):
                    act.wait_ge(turned, t * TAPS + m + 3)
                    act.wait_ge(tap_done, t * TAPS + m + 1)
                    act.copy(samp_t[:, (TAPS * k + m) % 2, :], turn_ps[:, m % 3, :]).then_inc(turn_taken, 1)

                for m in range(TAPS):
                    first(m)
                    if m >= 1:
                        take(m - 1)
                    if following and m == OFF_COPY:
                        front(*following)
                take(TAPS - 1)

            sweep(act, front, taps)

        @block.vector
        def _(dve):
            dve.memset(xr[:], 0.0).then_inc(border, 1)
            dve.sem_inc(pos_made, 1)
            dve.sem_inc(link, 2)
            dve.sem_inc(out_taken, 2)
            dve.sem_inc(turned, 2)
            dve.sem_inc(tap_done, 2)
            dve.sem_inc(mixed, PRIME)
            dve.wait_ge(tables, 2 + B)
            dve.wait_ge(w_in, 64)

            def front(t, k):
                b, j = t // IMG_TILES, t % IMG_TILES
                n = [t * LINKS + 2]

                def then(ins):
                    n[0] += 1
                    ins.then_inc(link, 1)
                    dve.wait_ge(link, n[0])

                o = pos_ps[:, 0:2 * NP].rearrange("p (m d) -> p d m", d=2)
                dve.wait_ge(pos_made, t + 2)
                dve.tensor_tensor(pos[:, 0, :], o[:, 0, :], base_y[:, DS(j, 1), :].rearrange("p o m -> p (o m)"),
                                  ALU.add).then_inc(link, 1)
                n[0] += 1
                then(dve.tensor_tensor(pos[:, 1, :], o[:, 1, :], base_x[:], ALU.add))
                then(dve.tensor_scalar(pos[:], pos[:], -1.0, float(H), ALU.max, ALU.min))
                then(dve.tensor_copy(low_i[:], pos[:]))
                then(dve.tensor_copy(low[:], low_i[:]))
                then(dve.tensor_tensor(over[:], low[:], pos[:], ALU.is_gt))
                then(dve.tensor_tensor(low[:], low[:], over[:], ALU.subtract))
                then(dve.tensor_scalar(low[:], low[:], float(H - 1), None, ALU.min))
                then(dve.tensor_tensor(frac[:, 1], pos[:], low[:], ALU.subtract))
                then(dve.tensor_scalar(frac[:, 0], frac[:, 1], -1.0, 1.0, ALU.mult, ALU.add))
                for cx in range(2):
                    for cy in range(2):
                        last = dve.tensor_tensor(wgt[:, k, :, cx, cy], frac[:, cx, 1, :], frac[:, cy, 0, :], ALU.mult)
                last.then_inc(link, 1)
                n[0] += 1
                then(dve.tensor_scalar(at[:], low[:, 1, :], float(COL_STEP), base_i[:, DS(b, 1)], ALU.mult, ALU.add))
                then(dve.scalar_tensor_tensor(out=at[:], in0=low[:, 0, :], scalar=float(ROW_STEP), in1=at[:],
                                              op0=ALU.mult, op1=ALU.add))
                then(dve.tensor_copy(idx[:, k, :], at[:]))
                dve.sem_inc(idx_made, 1)

            def taps(t, k, following):
                for m in range(TAPS):
                    for c in range(1, 4):
                        for r in range(TILE):
                            q = (TAPS * k + m) * TILE + r
                            n = m * TILE + r
                            base = PRIME + 3 * TILE * (TAPS * t + m)
                            if c == 1:
                                dve.wait_ge(mixed0, (TAPS * t + m) * TILE + r + 1)
                            else:
                                dve.wait_ge(mixed, base + (c - 2) * TILE + r + 1)
                            dve.scalar_tensor_tensor(out=samp[:, q % SR, :], in0=patch[:, n % GR, c * C:(c + 1) * C],
                                                     scalar=wgt[:, k, r * TAPS + m, c // 2, c % 2:c % 2 + 1], in1=samp[:, q % SR, :],
                                                     op0=ALU.mult, op1=ALU.add).then_inc(mixed, 1)
                    if following and m == INDEX:
                        front(*following)
                dve.wait_ge(tap_done, t * TAPS + TAPS + 2)
                dve.wait_ge(x2_loaded[k], 16 * (t // 2 + 1))
                dve.scalar_tensor_tensor(out=x2[:, k, :], in0=out_ps[:, k, :], scalar=tap_b[:, 0:1], in1=x2[:, k, :],
                                         op0=ALU.add, op1=ALU.add).then_inc(out_taken, 1)

            sweep(dve, front, taps)

        @block.gpsimd
        def _(pool):
            pool.iota(base_y[:].rearrange("p j m -> p (j m)"), [[TILE, IMG_TILES], [1, TILE], [1, 3], [0, 3]], base=-1,
                      channel_multiplier=0, allow_small_or_imprecise_dtypes=True).then_inc(tables, 1)
            pool.iota(base_x[:], [[0, TILE], [0, 3], [1, 3]], base=-1, channel_multiplier=1,
                      allow_small_or_imprecise_dtypes=True).then_inc(tables, 1)
            for b in range(B):
                pool.memset(base_i[:, b:b + 1], float(b * PH * ROW_STEP + ROW_STEP + COL_STEP)).then_inc(tables, 1)

            def front(t, k):
                pass

            def taps(t, k, following):
                pool.wait_ge(idx_made, t + 1)
                for n in range(NP):
                    m, r = n // TILE, n % TILE
                    pool.wait_ge(mixed, 3 * TILE * (TAPS * t + m) + 2 * TILE + r + 1)
                    pool.sem_inc(pool_passed, 1)
                    pool.indirect_dma_start(out=patch[:, n % GR, :], out_offset=None, in_=io["patch_rows"],
                                            in_offset=bass.IndirectOffsetOnAxis(ap=idx[:, k, r * TAPS + m:r * TAPS + m + 1], axis=1)
                                            ).then_inc(gathered[n % GR], 16)

            sweep(pool, front, taps)


EX = 64
TOP = 8
PAIRS = B // 2
HID = 512
HC = HID // 128


def pick_phase(nc, sems, consts, io, pooled_t):
    ident = consts["ident"]
    with Scope(nc, sems) as s:
        logit = s.sb("pk_logit", [128, T])
        rest = s.sb("pk_rest", [128, T])
        top = s.sb("pk_top", [128, TOP])
        place = s.sb("pk_place", [128, TOP], U32)
        place_f = s.sb("pk_place_f", [128, TOP])
        place_i = s.sb("pk_place_i", [128, PAIRS, TOP], U32)
        row0 = s.sb("pk_row0", [128, PAIRS])
        nmax, total, inv = s.sb("pk_nmax", [128, 1]), s.sb("pk_total", [128, 1]), s.sb("pk_inv", [128, 1])
        prob = s.sb("pk_prob", [128, PAIRS, TOP])
        token = s.sb("pk_token", [128, TOP, C])
        pooled = s.sb("pk_pooled", [128, C])
        turn = s.ps("pk_turn", [128, BANK])
        loaded, rows_set, link = s.sem("pk_loaded"), s.sem("pk_rows_set"), s.sem("pk_link")
        exp_ready, exp_made, stored = s.sem("pk_exp_ready"), s.sem("pk_exp_made"), s.sem("pk_stored")
        idx_made, gathered, pooled_made, turned = (s.sem(f"pk_{n}") for n in ("idx_made", "gathered", "pooled_made", "turned"))
        picked_made, turn_taken = s.sem("pk_picked_made"), s.sem("pk_turn_taken")
        block = s.ctx.enter_context(nc.Block())

        @block.sync
        def _(sp):
            for p in range(PAIRS):
                if p:
                    sp.wait_ge(stored, 16 * p)
                sp.dma_start(logit[:], io["logits_p"][p]).then_inc(loaded, 16)
                sp.wait_ge(picked_made, p + 1)
                sp.dma_start(io["picked"][p], logit[:]).then_inc(stored, 16)
            sp.wait_ge(stored, 16 * PAIRS)

        @block.gpsimd
        def _(pool):
            for p in range(PAIRS):
                for h in range(2):
                    pool.memset(row0[64 * h:64 * h + 64, p:p + 1], float((2 * p + h) * T)).then_inc(rows_set, 1)
            for p in range(PAIRS):
                pool.wait_ge(idx_made, p + 1)
                if p:
                    pool.wait_ge(pooled_made, p)
                for k in range(TOP):
                    pool.indirect_dma_start(out=token[:, k, :], out_offset=None, in_=io["token_rows"],
                                            in_offset=bass.IndirectOffsetOnAxis(ap=place_i[:, p, k:k + 1], axis=0)
                                            ).then_inc(gathered, 16)

        @block.scalar
        def _(act):
            for p in range(PAIRS):
                act.wait_ge(exp_ready, p + 1)
                act.activation(logit[:], logit[:], ACT.Exp, bias=nmax[:], accum_out=total[:]).then_inc(exp_made, 1)
                act.activation(prob[:, p, :], top[:], ACT.Exp, bias=nmax[:]).then_inc(exp_made, 1)

        @block.tensor
        def _(pe):
            for p in range(PAIRS):
                pe.wait_ge(pooled_made, p + 1)
                if p:
                    pe.wait_ge(turn_taken, p)
                pe.transpose(turn[:, 0:C], pooled[:], ident[:]).then_inc(turned, 1)

        @block.vector
        def _(dve):
            n = [0]

            def then(ins):
                n[0] += 1
                ins.then_inc(link, 1)
                dve.wait_ge(link, n[0])

            dve.wait_ge(rows_set, 2 * PAIRS)
            for p in range(PAIRS):
                dve.wait_ge(loaded, 16 * (p + 1))
                then(dve.max(out=top[:], in_=logit[:]))
                then(dve.max_index(out=place[:], in_max=top[:], in_values=logit[:]))
                then(dve.match_replace(out=rest[:], in_to_replace=top[:], in_values=logit[:], imm_value=-3.0e38))
                then(dve.tensor_tensor(rest[:], rest[:], logit[:], ALU.not_equal))
                then(dve.tensor_scalar(nmax[:], top[:, 0:1], -1.0, None, ALU.mult))
                then(dve.tensor_copy(place_f[:], place[:]))
                then(dve.tensor_scalar(place_f[:], place_f[:], row0[:, p:p + 1], None, ALU.add))
                then(dve.tensor_copy(place_i[:, p, :], place_f[:]))
                dve.sem_inc(exp_ready, 1)
                dve.sem_inc(idx_made, 1)
                dve.wait_ge(exp_made, 2 * p + 2)
                then(dve.reciprocal(inv[:], total[:]))
                then(dve.tensor_scalar(prob[:, p, :], prob[:, p, :], inv[:, 0:1], None, ALU.mult))
                then(dve.scalar_tensor_tensor(out=logit[:], in0=logit[:], scalar=inv[:, 0:1], in1=rest[:],
                                              op0=ALU.mult, op1=ALU.mult))
                dve.sem_inc(picked_made, 1)
                dve.wait_ge(gathered, 16 * TOP * (p + 1))
                if p:
                    dve.wait_ge(turned, p)
                then(dve.tensor_scalar(pooled[:], token[:, 0, :], prob[:, p, 0:1], None, ALU.mult))
                for k in range(1, TOP):
                    then(dve.scalar_tensor_tensor(out=pooled[:], in0=token[:, k, :], scalar=prob[:, p, k:k + 1],
                                                  in1=pooled[:], op0=ALU.mult, op1=ALU.add))
                dve.sem_inc(pooled_made, 1)
                dve.wait_ge(turned, p + 1)
                dve.tensor_copy(pooled_t[:, p, :], turn[:, 0:C]).then_inc(turn_taken, 1)


SUM_SLOTS = 4


def expert_phase(nc, sems, consts, io, pooled_t):
    ident = consts["ident"]
    NW = 4
    with Scope(nc, sems) as s:
        w1, w2 = s.sb("ex_w1", [128, NW, HID]), s.sb("ex_w2", [128, NW, HC, C])
        b1, b2 = s.sb("ex_b1", [128, EX * HC]), s.sb("ex_b2", [128, EX])
        hid = s.sb("ex_hid", [128, 2, HC, B])
        act_h = s.sb("ex_act_h", [128, 2, HC, B])
        out_c = s.sb("ex_out_c", [128, B, EX])
        out_t = s.sb("ex_out_t", [128, PAIRS, C])
        pick = s.sb("ex_pick", [128, SUM_SLOTS, COLS])
        x3 = s.sb("ex_x3", [128, SUM_SLOTS, 2, COLS])
        hid_ps, o_ps = s.ps("ex_hid_ps", [128, 2, BANK]), s.ps("ex_o_ps", [128, 2, BANK])
        sum_ps = s.ps("ex_sum_ps", [128, 4, BANK])
        b_in = s.sem("ex_b_in")
        w_loaded = [s.sem(f"ex_w_loaded{k}") for k in range(NW)]
        hid_made, hid_taken, gelu_made = s.sem("ex_hid_made"), s.sem("ex_hid_taken"), s.sem("ex_gelu_made")
        o_made, o_taken = s.sem("ex_o_made"), s.sem("ex_o_taken")
        turned, turn_taken = s.sem("ex_turned"), s.sem("ex_turn_taken")
        t_loaded = [s.sem(f"ex_t_loaded{k}") for k in range(SUM_SLOTS)]
        sum_made, sum_taken = s.sem("ex_sum_made"), s.sem("ex_sum_taken")
        stored = [s.sem(f"ex_stored{k}") for k in range(SUM_SLOTS)]
        pooled = pooled_t[:].rearrange("d p (h e) -> d (p h) e", e=EX)
        block = s.ctx.enter_context(nc.Block())

        @block.sync
        def _(sp):
            sp.dma_start(b1[:], io["b1"]).then_inc(b_in, 16)
            sp.dma_start(b2[:], io["b2"]).then_inc(b_in, 16)
            with sp.Fori(0, EX // NW) as i:
                for k in range(NW):
                    e = i * NW + k
                    sp.wait_ge(o_taken, e + 1)
                    sp.dma_start(w1[:, k, :], io["w1"][DS(e, 1), 0:C, :].rearrange("o d h -> (o d) h")).then_inc(w_loaded[k], 16)
                    sp.dma_start(w2[:, k, :, :], io["w2"][DS(e, 1), 0:HID, :].rearrange("o (p c) f -> (o p) c f", c=HC)
                                 ).then_inc(w_loaded[k], 16)
            for p in range(PAIRS):
                with sp.Fori(0, IMG_TILES // SUM_SLOTS) as j:
                    for k in range(SUM_SLOTS):
                        t = p * IMG_TILES + j * SUM_SLOTS + k
                        n = p * (IMG_TILES // SUM_SLOTS) + j
                        sp.wait_ge(sum_taken, t + 1)
                        sp.wait_ge(stored[k], 32 * (n + 1))
                        sp.dma_start(pick[:, k, :], io["picked"][p, :, DS((j * SUM_SLOTS + k) * COLS, COLS)]).then_inc(t_loaded[k], 16)
                        for h in range(2):
                            sp.dma_start(x3[:, k, h, :], io["x3"][2 * p + h, :, DS((j * SUM_SLOTS + k) * COLS, COLS)]
                                         ).then_inc(t_loaded[k], 16)
            for k in range(SUM_SLOTS):
                sp.wait_ge(stored[k], 32 * (PAIRS * IMG_TILES // SUM_SLOTS + 1))

        @block.tensor
        def _(pe):
            with pe.Fori(0, EX // NW) as i:
                for k in range(NW):
                    e = i * NW + k
                    pe.wait_ge(w_loaded[k], 32 * (i + 1))
                    pe.wait_ge(hid_taken, e + 1)
                    for c in range(HC):
                        last = pe.matmul(hid_ps[:, k % 2, c * B:(c + 1) * B], w1[:, k, c:HID:HC],
                                         pooled[:, :, DS(e, 1)].rearrange("d b o -> d (b o)"), start=True, stop=True)
                    last.then_inc(hid_made, 1)
                    pe.wait_ge(gelu_made, e + 1)
                    pe.wait_ge(o_taken, e + NW - 1)
                    for c in range(HC):
                        last = pe.matmul(o_ps[:, k % 2, 0:B], w2[:, k, c, :], act_h[:, k % 2, c, :],
                                         start=(c == 0), stop=(c == HC - 1))
                    last.then_inc(o_made, 1)
            pe.wait_ge(o_taken, EX + NW)
            for p in range(PAIRS):
                pe.transpose(o_ps[:, p, 0:C], out_c[:, 2 * p:2 * p + 2, :].rearrange("o b e -> o (b e)"), ident[:]).then_inc(turned, 1)
            pe.wait_ge(turn_taken, PAIRS)
            for p in range(PAIRS):
                with pe.Fori(0, IMG_TILES // SUM_SLOTS) as j:
                    for k in range(SUM_SLOTS):
                        t = p * IMG_TILES + j * SUM_SLOTS + k
                        pe.wait_ge(t_loaded[k], 48 * (p * (IMG_TILES // SUM_SLOTS) + j + 1))
                        pe.wait_ge(sum_taken, t + SUM_SLOTS - 1)
                        for h in range(2):
                            last = pe.matmul(sum_ps[:, 2 * (k % 2) + h, :], out_t[64 * h:64 * h + 64, p, :],
                                             pick[64 * h:64 * h + 64, k, :], start=True, stop=True)
                        last.then_inc(sum_made, 1)

        @block.scalar
        def _(act):
            for k in range(SUM_SLOTS):
                act.sem_inc(stored[k], 32)
            with act.Fori(0, EX // 2) as i:
                for k in range(2):
                    e = i * 2 + k
                    act.wait_ge(hid_taken, e + 3)
                    act.activation(act_h[:, k, :, :], hid[:, k, :, :], ACT.Gelu).then_inc(gelu_made, 1)
            for p in range(PAIRS):
                with act.Fori(0, IMG_TILES // SUM_SLOTS) as j:
                    for k in range(SUM_SLOTS):
                        t = p * IMG_TILES + j * SUM_SLOTS + k
                        act.wait_ge(sum_taken, t + SUM_SLOTS + 1)
                        for h in range(2):
                            act.dma_start(io["out"][2 * p + h, :, DS((j * SUM_SLOTS + k) * COLS, COLS)], x3[:, k, h, :]
                                          ).then_inc(stored[k], 16)

        @block.vector
        def _(dve):
            dve.sem_inc(o_taken, NW)
            dve.sem_inc(hid_taken, 2)
            dve.sem_inc(sum_taken, SUM_SLOTS)
            dve.wait_ge(b_in, 32)
            with dve.Fori(0, EX // 2) as i:
                for k in range(2):
                    e = i * 2 + k
                    dve.wait_ge(hid_made, e + 1)
                    dve.tensor_tensor(hid[:, k, :, :], hid_ps[:, k, 0:HC * B].rearrange("p (c b) -> p c b", b=B),
                                      b1[:, DS(e * HC, HC)].unsqueeze(2).to_broadcast([128, HC, B]), ALU.add
                                      ).then_inc(hid_taken, 1)
                    dve.wait_ge(o_made, e + 1)
                    dve.tensor_scalar(out_c[:, :, DS(e, 1)].rearrange("o b x -> o (b x)"), o_ps[:, k, 0:B],
                                      b2[:, DS(e, 1)], None, ALU.add).then_inc(o_taken, 1)
            for p in range(PAIRS):
                dve.wait_ge(turned, p + 1)
                dve.tensor_copy(out_t[:, p, :], o_ps[:, p, 0:C]).then_inc(turn_taken, 1)
            for p in range(PAIRS):
                with dve.Fori(0, IMG_TILES // SUM_SLOTS) as j:
                    for k in range(SUM_SLOTS):
                        t = p * IMG_TILES + j * SUM_SLOTS + k
                        dve.wait_ge(sum_made, t + 1)
                        dve.tensor_tensor(x3[:, k], x3[:, k], sum_ps[:, 2 * (k % 2):2 * (k % 2) + 2, :], ALU.add).then_inc(sum_taken, 1)


def network(nc, sems, io):
    with ExitStack() as ctx:
        def sb(name, shape):
            return ctx.enter_context(nc.sbuf_tensor(name, shape, F32))

        def dram(name, shape, dt=F32):
            return nc.dram_tensor(name, shape, dt, kind="Internal").ap()

        consts = {"ident": sb("ident", [128, 128]), "mean_mat": sb("mean_mat", [128, 128]),
                  "center_mat": sb("center_mat", [128, 128]), "coef_qk": sb("coef_qk", [128, 2]),
                  "coef_v": sb("coef_v", [128, 2])}
        coef_sim, coef_att, coef_emb, coef_f = (sb("coef_sim", [128, 4 * G]), sb("coef_att", [128, 2]),
                                                sb("coef_emb", [128, 2]), sb("coef_f", [128, 2]))
        pooled_t = sb("pooled_t", [128, PAIRS, 2 * EX])
        qk_parts = dram("d_qk_parts", (PARTS, 2 * QC * G, N * W), BF16)
        rel_parts = dram("d_rel_parts", (2, PARTS, QC, REL), BF16)
        v = dram("d_v", (W, N * C))
        attn, emb = dram("d_attn", (C, N * W)), dram("d_emb", (BLOCKS, VC, HB, W))
        x1, xn1, x2, x3 = (dram(f"d_{n}", (B, C, T)) for n in ("x1", "xn1", "x2", "x3"))
        rows = dram("d_rows", (B, C, H + 2, W))
        patches = dram("d_patches", (B, PH, PW, 2, C))
        logits, tokens = dram("d_logits", (B, EX, T)), dram("d_tokens", (B, H, W, C))
        picked = dram("d_picked", (PAIRS, 2 * EX, T))
        x = io["x"].rearrange("b c h w -> b c (h w)")

        setup_phase(nc, sems, consts["ident"], consts["mean_mat"], consts["center_mat"])
        norm_phase(nc, sems, consts, "qkv_stats", {"src": x, "w_qk": io["w_qk"], "w_v": io["w_v"], "gb": io["gb_qkv"],
                                                   "coef": [consts["coef_qk"], consts["coef_v"]]}, LNC_EPS)
        norm_phase(nc, sems, consts, "qkv", {"src": x, "w_qk": io["w_qk"], "w_v": io["w_v"], "qk_parts": qk_parts, "v": v}, LNC_EPS)
        embedding_parts_phase(nc, sems, io["rel_rev"], rel_parts)
        att_io = {"qk_parts": qk_parts.rearrange("a (s c g) f -> a s c g f", s=2, c=QC), "v": v, "rel_parts": rel_parts,
                  "rel_v": io["rel_v"], "parity": io["parity"], "sim_gamma": io["sim_gamma"],
                  "sim_beta": io["sim_beta"], "attn": attn, "emb": emb}
        attention_phase(nc, sems, consts["ident"], consts["mean_mat"], att_io, True, coef_sim)
        attention_phase(nc, sems, consts["ident"], consts["mean_mat"], att_io, False, coef_sim)
        mix_io = {"attn": attn, "emb": emb, "x": x, "x1": x1, "gb_out": io["gb_out"]}
        mix_phase(nc, sems, mix_io, coef_att, coef_emb, True)
        mix_phase(nc, sems, mix_io, coef_att, coef_emb, False)
        norm_phase(nc, sems, consts, "ffn", {"src": x1, "xn": xn1, "w_f": io["w_f"], "gb": io["gb_f"], "coef": [coef_f]}, EPS)
        recurrence_phase(nc, sems, consts, {"xn": xn1, "x1": x1, "x2": x2, "w_f_nat": io["w_f_nat"], "v_t": io["v_t"]}, coef_f)
        norm_phase(nc, sems, consts, "image", {"src": x2, "rows": rows, "patches": patches}, LNC_EPS)
        deform_phase(nc, sems, consts, {"rows": rows, "x2": x2, "x3": x3, "off_w": io["off_w"], "off_b": io["off_b"],
                                        "tap_w": io["tap_w"], "tap_b": io["tap_b"],
                                        "patch_rows": patches.rearrange("b y x h c -> (b y x h c)").rearrange("(n f) -> n f", f=PATCH)})
        norm_phase(nc, sems, consts, "gate", {"src": x3, "w_g": io["w_g"], "b_g": io["b_g"], "logits": logits, "tokens": tokens}, EPS)
        pick_phase(nc, sems, consts, {"logits_p": logits.rearrange("(p h) e t -> p (h e) t", h=2), "picked": picked,
                                      "token_rows": tokens.rearrange("b h w c -> (b h w) c")}, pooled_t)
        expert_phase(nc, sems, consts, {"w1": io["w1"], "w2": io["w2"], "b1": io["b1"], "b2": io["b2"], "picked": picked,
                                        "x3": x3, "out": io["out"].rearrange("b c h w -> b c (h w)")}, pooled_t)


def kernel(**inputs):
    import numpy as np
    import concourse.bacc as bacc
    from concourse.bass_utils import run_bass_kernel_spmd

    a = {n: np.asarray(v) for n, v in inputs.items()}

    def qk_rows(m):
        m = m.reshape((G, 4, QC) + m.shape[1:])[:, :2]
        return np.moveaxis(m, 0, 2).reshape((2 * QC * G,) + m.shape[3:])

    def v_rows(m):
        return m.reshape((G, 2, VC) + m.shape[1:])[:, 1].reshape((C,) + m.shape[1:])

    qg, qb = a["L0_conv_bn_qkv_gamma"], a["L0_conv_bn_qkv_beta"]
    og, ob = (a[f"L0_conv_bn_out_{n}"].reshape(C, 2) for n in ("gamma", "beta"))
    wq = a["L0_conv_conv_w"]
    rel = a["L0_conv_rel_emb"]
    w1, w2 = a["L1_ffn_weight1"], a["L1_ffn_weight2"]
    arrays = {
        "x": a["x"],
        "w_qk": qk_rows(wq).T, "w_v": v_rows(wq).T,
        "gb_qkv": np.stack([np.stack([qk_rows(m), v_rows(m)], -1) for m in (qg, qb)], -1),
        "rel_rev": rel[:2 * QC, ::-1], "rel_v": rel[2 * QC:, ::-1].T,
        "parity": np.stack([np.arange(C) // VC % 2 == e for e in range(2)], -1).astype(np.float32),
        "sim_gamma": a["L0_conv_bn_sim_gamma"], "sim_beta": a["L0_conv_bn_sim_beta"],
        "gb_out": np.stack([og, ob], -1),
        "w_f": a["L0_ffn_W"].T, "w_f_nat": a["L0_ffn_W"], "v_t": a["L0_ffn_V"].T,
        "gb_f": np.stack([a["L0_ffn_gamma"], a["L0_ffn_beta"]], -1)[:, None],
        "off_w": a["L1_conv_offset_w"].reshape(2 * TAPS, C, TAPS).transpose(1, 2, 0), "off_b": a["L1_conv_offset_b"][:, None],
        "tap_w": a["L1_conv_conv_w"].reshape(C, C, TAPS).transpose(1, 2, 0), "tap_b": a["L1_conv_conv_b"][:, None],
        "w_g": a["L1_ffn_gate_w"].T, "b_g": a["L1_ffn_gate_b"][:, None],
        "w1": w1, "w2": w2,
        "b1": w1[:, C, :].reshape(EX, 128, HC).transpose(1, 0, 2).reshape(128, EX * HC), "b2": w2[:, HID, :].T,
    }
    arrays = {n: np.ascontiguousarray(v) for n, v in arrays.items()}
    nc = bacc.Bacc("TRN2", target_bir_lowering=False, num_devices=1)
    io = {n: nc.dram_tensor(f"in_{n}", v.shape, mybir.dt.from_np(v.dtype), kind="ExternalInput").ap() for n, v in arrays.items()}
    io["out"] = nc.dram_tensor("out_x", (B, C, H, W), F32, kind="ExternalOutput").ap()
    with ExitStack() as sems:
        network(nc, sems, io)
    r = run_bass_kernel_spmd(nc, [{f"in_{n}": v for n, v in arrays.items()}], core_ids=[0])
    return r.results[0]["out_x"]
```
